# Optimizing a Trainium2 kernel written in Bass

```python
import numpy as np
import jax
import jax.numpy as jnp

def _softmax(x, axis=-1):
    return jax.nn.softmax(x, axis=axis)

def _gelu(x):
    return jax.nn.gelu(x, approximate=True)

def _silu(x):
    return jax.nn.silu(x)

def _sigmoid(x):
    return jax.nn.sigmoid(x)

def _layernorm(x, axis=-1, eps=1e-05):
    m = jnp.mean(x, axis=axis, keepdims=True)
    v = jnp.var(x, axis=axis, keepdims=True)
    return (x - m) / jnp.sqrt(v + eps)

def _scatter_add(tgt, idx, src, axis=0):
    return tgt.at[idx].add(src)

def _segment_sum(src, seg, n):
    return jax.ops.segment_sum(src, seg, n)
kernel_name = 'mk_gps_d1_gnn_r8_a03f8e'

def setup_inputs(seed: int=0):
    np.random.seed(seed)
    _w = jnp.asarray

    def _rec_inputs():
        import jax
        import jax.numpy as jnp
        _gk = jax.random.key(seed)
        x = -0.0003713 + 1 * jax.random.normal(jax.random.fold_in(_gk, 1), (6250, 256), jnp.float32)
        _s = jax.random.randint(jax.random.fold_in(_gk, 2), (50000,), 0, 6250, jnp.int32)
        _d = jax.random.randint(jax.random.fold_in(_gk, 3), (50000,), 0, 6250, jnp.int32)
        _loop = jnp.arange(6250, dtype=jnp.int32)
        src = jnp.concatenate([_s, _d, _loop])
        dst = jnp.concatenate([_d, _s, _loop])
        _o = jnp.argsort(dst, stable=True)
        src = src[_o]
        dst = dst[_o]
        return (x, src, dst)
    x, src, dst = _rec_inputs()

    def _L0_gnn_setup():
        import jax, jax.numpy as jnp
        import numpy as np
        N = 6250
        E = 100000
        IN_C = 256
        HEADS = 8
        OUT_C = 32
        key = jax.random.key(seed)
        k1, k2, k3, k4, k5 = jax.random.split(key, 5)
        x = jax.random.normal(k1, (N, IN_C), dtype=jnp.float32)
        edge_index = jax.random.randint(k2, (2, E), 0, N, dtype=jnp.int64)
        lim_W = float(np.sqrt(6.0 / (IN_C + HEADS * OUT_C)))
        lim_a = float(np.sqrt(6.0 / (HEADS + OUT_C)))
        W = jax.random.uniform(k3, (IN_C, HEADS * OUT_C), minval=-lim_W, maxval=lim_W, dtype=jnp.float32)
        a_src = jax.random.uniform(k4, (HEADS, OUT_C), minval=-lim_a, maxval=lim_a, dtype=jnp.float32)
        a_dst = jax.random.uniform(k5, (HEADS, OUT_C), minval=-lim_a, maxval=lim_a, dtype=jnp.float32)
        return {'x': x, 'edge_index': edge_index, 'W': W, 'a_src': a_src, 'a_dst': a_dst}
    _L0_gnn_all = _L0_gnn_setup()
    _L0_gnn_in = {k: v for k, v in _L0_gnn_all.items() if k in ('W', 'a_src', 'a_dst')}
    del _L0_gnn_all

    def _L0_mix_setup():
        import jax, jax.numpy as jnp
        import numpy as np
        HEADS = 8
        DIM_HEAD = 64
        EPS = 1e-05

        def _inst_norm_lastdim(t):
            mu = jnp.mean(t, axis=-1, keepdims=True)
            var = jnp.mean(jnp.square(t - mu), axis=-1, keepdims=True)
            return (t - mu) * jax.lax.rsqrt(var + EPS)
        key = jax.random.key(seed)
        k1, k2, k3, k4 = jax.random.split(key, 4)
        b, n, dim = (4, 1024, 256)
        inner = HEADS * DIM_HEAD
        x = jax.random.normal(k1, (b, n, dim), dtype=jnp.float32)
        Wqkv = jax.random.normal(k2, (3 * inner, dim), dtype=jnp.float32) * (1.0 / np.sqrt(dim))
        Wout = jax.random.normal(k3, (dim, inner), dtype=jnp.float32) * (1.0 / np.sqrt(inner))
        bout = jax.random.normal(k4, (dim,), dtype=jnp.float32) * 0.01
        return {'x': x, 'Wqkv': Wqkv, 'Wout': Wout, 'bout': bout}
    _L0_mix_all = _L0_mix_setup()
    _L0_mix_in = {k: v for k, v in _L0_mix_all.items() if k in ('Wqkv', 'Wout', 'bout')}
    del _L0_mix_all

    def _L0_ffn_setup():
        import jax, jax.numpy as jnp
        import numpy as np
        B, S, H, F, E, K = (8, 512, 256, 512, 16, 2)
        EPS = 1e-05
        key = jax.random.key(seed)
        ks = jax.random.split(key, 9)
        sc = 0.02
        return {'x': jax.random.normal(ks[0], (B, S, H), dtype=jnp.float32), 'gate_w': jax.random.normal(ks[1], (H, E), dtype=jnp.float32) * sc, 'gate_b': jnp.zeros((E,), dtype=jnp.float32), 'w1': jax.random.normal(ks[2], (E, H, F), dtype=jnp.float32) * sc, 'b1': jnp.zeros((E, F), dtype=jnp.float32), 'w2': jax.random.normal(ks[3], (E, F, H), dtype=jnp.float32) * sc, 'b2': jnp.zeros((E, H), dtype=jnp.float32), 'gamma': jnp.ones((H,), dtype=jnp.float32), 'beta': jnp.zeros((H,), dtype=jnp.float32)}
    _L0_ffn_all = _L0_ffn_setup()
    _L0_ffn_in = {k: v for k, v in _L0_ffn_all.items() if k in ('gate_w', 'gate_b', 'w1', 'b1', 'w2', 'b2', 'gamma', 'beta')}
    del _L0_ffn_all
    return {'x': x, 'src': src, 'dst': dst, 'L0_gnn_W': _L0_gnn_in['W'], 'L0_gnn_a_src': _L0_gnn_in['a_src'], 'L0_gnn_a_dst': _L0_gnn_in['a_dst'], 'L0_mix_Wqkv': _L0_mix_in['Wqkv'], 'L0_mix_Wout': _L0_mix_in['Wout'], 'L0_mix_bout': _L0_mix_in['bout'], 'L0_ffn_gate_w': _L0_ffn_in['gate_w'], 'L0_ffn_gate_b': _L0_ffn_in['gate_b'], 'L0_ffn_w1': _L0_ffn_in['w1'], 'L0_ffn_b1': _L0_ffn_in['b1'], 'L0_ffn_w2': _L0_ffn_in['w2'], 'L0_ffn_b2': _L0_ffn_in['b2'], 'L0_ffn_gamma': _L0_ffn_in['gamma'], 'L0_ffn_beta': _L0_ffn_in['beta']}

def reference(x, src, dst, L0_gnn_W, L0_gnn_a_src, L0_gnn_a_dst, L0_mix_Wqkv, L0_mix_Wout, L0_mix_bout, L0_ffn_gate_w, L0_ffn_gate_b, L0_ffn_w1, L0_ffn_b1, L0_ffn_w2, L0_ffn_b2, L0_ffn_gamma, L0_ffn_beta):
    import jax
    import jax.numpy as jnp

    def _L0_gnn_ref(x, edge_index, W, a_src, a_dst):
        import jax, jax.numpy as jnp
        import numpy as np
        N = 6250
        E = 100000
        IN_C = 256
        HEADS = 8
        OUT_C = 32
        n = x.shape[0]
        H, D = a_src.shape
        x_proj = (x @ W).reshape(n, H, D)
        alpha_src = jnp.einsum('nhd,hd->nh', x_proj, a_src)
        alpha_dst = jnp.einsum('nhd,hd->nh', x_proj, a_dst)
        row, col = (edge_index[0], edge_index[1])
        e = alpha_src[row] + alpha_dst[col]
        m = jax.ops.segment_max(e, col, num_segments=n)
        m = jnp.where(jnp.isfinite(m), m, 0.0)
        e_exp = jnp.exp(e - m[col])
        s = jax.ops.segment_sum(e_exp, col, num_segments=n)
        att = e_exp / (s[col] + 1e-16)
        out = jax.ops.segment_sum(att[:, :, None] * x_proj[row], col, num_segments=n)
        return out.reshape(n, H * D)

    def _L0_mix_ref(x, Wqkv, Wout, bout):
        import jax, jax.numpy as jnp
        import numpy as np
        HEADS = 8
        DIM_HEAD = 64
        EPS = 1e-05

        def _inst_norm_lastdim(t):
            mu = jnp.mean(t, axis=-1, keepdims=True)
            var = jnp.mean(jnp.square(t - mu), axis=-1, keepdims=True)
            return (t - mu) * jax.lax.rsqrt(var + EPS)
        b, n, dim = x.shape
        qkv = jnp.einsum('bnc,fc->bnf', x, Wqkv)
        q, k, v = jnp.split(qkv, 3, axis=-1)

        def to_heads(t):
            return t.reshape(b, n, HEADS, DIM_HEAD).transpose(0, 2, 1, 3)
        q, k, v = (to_heads(q), to_heads(k), to_heads(v))
        k = _inst_norm_lastdim(k)
        v = _inst_norm_lastdim(v)
        dots = jnp.einsum('bhnd,bhne->bhde', k, v)
        out = jnp.einsum('bhnd,bhde->bhne', q, dots) / n
        out = out.transpose(0, 2, 1, 3).reshape(b, n, HEADS * DIM_HEAD)
        return jnp.einsum('bnf,cf->bnc', out, Wout) + bout

    def _L0_ffn_ref(x, gate_w, gate_b, w1, b1, w2, b2, gamma, beta):
        import jax, jax.numpy as jnp
        import numpy as np
        B, S, H, F, E, K = (8, 512, 256, 512, 16, 2)
        EPS = 1e-05
        gate_logits = x @ gate_w + gate_b
        topk_vals, topk_idx = jax.lax.top_k(gate_logits, K)
        topk_w = jax.nn.softmax(topk_vals, axis=-1)
        h = jax.nn.relu(jnp.einsum('bsh,ehf->bsef', x, w1) + b1)
        expert_out = jnp.einsum('bsef,efh->bseh', h, w2) + b2
        sel = jnp.take_along_axis(expert_out, topk_idx[:, :, :, None], axis=2)
        moe = jnp.sum(topk_w[..., None] * sel, axis=2)
        y = x + moe
        mu = jnp.mean(y, axis=-1, keepdims=True)
        var = jnp.var(y, axis=-1, keepdims=True)
        return (y - mu) / jnp.sqrt(var + EPS) * gamma + beta
    edge_index = jnp.stack([src, dst])
    xn = _layernorm(x, axis=-1)
    x = x + _L0_gnn_ref(xn, edge_index, L0_gnn_W, L0_gnn_a_src, L0_gnn_a_dst) + _L0_mix_ref(xn[None], L0_mix_Wqkv, L0_mix_Wout, L0_mix_bout)[0]
    x = x + _L0_ffn_ref(_layernorm(x, axis=-1)[None], L0_ffn_gate_w, L0_ffn_gate_b, L0_ffn_w1, L0_ffn_b1, L0_ffn_w2, L0_ffn_b2, L0_ffn_gamma, L0_ffn_beta)[0]
    return x

_drawn_inputs = setup_inputs


def setup_inputs(seed=0):
    import zlib

    import numpy as np

    out = dict(_drawn_inputs(seed))
    spreads = {'L0_ffn_gate_b': (0.0, 0.1),
     'L0_ffn_b1': (0.0, 0.776),
     'L0_ffn_b2': (0.0, 0.1),
     'L0_ffn_gamma': (1.0, 0.2),
     'L0_ffn_beta': (0.0, 0.1)}
    factors = {'L0_gnn_a_dst': 8.0, 'L0_mix_bout': 6.418}
    for name, (base, spread) in spreads.items():
        noise = np.random.default_rng([zlib.crc32(name.encode()), seed]).standard_normal(out[name].shape)
        drawn = base * np.exp(spread * noise) if base else spread * noise
        out[name] = jnp.asarray(drawn.astype(out[name].dtype))
    for name, factor in factors.items():
        out[name] = (out[name] * factor).astype(out[name].dtype)
    return out
```

```python
from contextlib import ExitStack, contextmanager

import numpy as np

import concourse.bass as bass
from concourse import mybir

P = 128
N, C = 6250, 256
HEADS, HD = 8, 32
MH, MD = 8, 64
INNER = MH * MD
NE = 106250
EXPERTS, FF, TOPK = 16, 512, 2
EPS = 1e-5

TILES = -(-N // P)
LAST = N - (TILES - 1) * P
ETILES = -(-NE // P)
ELAST = NE - (ETILES - 1) * P
UNROLL = 16
ROUNDS = -(-(ETILES + TILES - 1) // UNROLL)
PAIRS = ROUNDS * UNROLL
PCH = -(-PAIRS // P)
ECH = -(-ETILES // P)
NO_NODE = 1 << 20
EXT = C + 2 * HEADS
ROW = C + HEADS
STILES = (N * TOPK + EXPERTS * (P - 1)) // P
STILES += STILES % 2
F32, I32, U32 = mybir.dt.float32, mybir.dt.int32, mybir.dt.uint32
ALU = mybir.AluOpType
ACT = mybir.ActivationFunctionType
X = mybir.AxisListType.X


class Steps:

    def __init__(self, engine, sem):
        self.engine, self.sem, self.n, self.base = engine, sem, 0, 0

    def done(self, instruction):
        self.go(instruction)
        self.engine.wait_ge(self.sem, self.base + self.n)

    def at(self, base):
        self.base, self.n = base, 0

    def go(self, instruction):
        self.n += 1
        instruction.then_inc(self.sem, 1)


@contextmanager
def by_two(engine, start, end):
    with engine.Fori(start // 2, end // 2) as half:
        yield half * 2


def each_pair(engine, body):
    body(0, (0, 1))
    with by_two(engine, 2, TILES - 1) as t0:
        body(t0, (0, 1))
    body(TILES - 1, (0,))


def each_tile(engine, body):
    def both(t0, buffers):
        for b in buffers:
            body(t0, b)

    each_pair(engine, both)


def is_last(t0):
    return isinstance(t0, int) and t0 == TILES - 1


def starts(t0):
    return isinstance(t0, int) and t0 == 0


def spread(ap, n):
    return ap.unsqueeze(2).to_broadcast([ap.shape[0], ap.shape[1], n])


def over(ap, n):
    return ap.unsqueeze(1).to_broadcast([ap.shape[0], n, ap.shape[1]])


def build(nc, x, src, dst, gnn_W, a_src, a_dst, Wqkv, Wout, bout, gate_w, gate_b, w1, b1, w2, b2,
          gamma, beta, out):
    ctx = ExitStack()
    with ctx:
        def sb(name, shape, dt=F32):
            return ctx.enter_context(nc.sbuf_tensor(name, shape, dt))

        def sem(name):
            return ctx.enter_context(nc.semaphore(name))

        def dram(name, shape, dt=F32):
            return nc.dram_tensor(name, shape, dt).ap()

        src_rows = dram("src_rows", (ETILES, P), I32)
        dst_rows = dram("dst_rows", (ETILES, P), I32)
        pair_acc_d = dram("pair_acc_d", (PCH * P,), I32)
        xnT_d = dram("xnT_d", (TILES, P, C))
        table = dram("table", (TILES * P, ROW))
        slots_x = dram("slots_x", ((STILES + 1) * P, C))
        slots_y = dram("slots_y", (STILES * P, C))

        bank = [ctx.enter_context(nc.psum_tensor(f"bank{i}", [P, 512], F32)) for i in range(8)]

        pool_on = sem("pool_on")

        ident = sb("ident", [P, P])
        iota = sb("iota", [P, P])
        ones = sb("ones", [P, P])
        below = sb("below", [P, P])
        work = sb("work", [P, TILES, EXT])
        acc = sb("acc", [P, TILES, EXT])
        stats = sb("stats", [P, TILES, 6])
        mean = sb("mean", [P, TILES])
        rstd = sb("rstd", [P, TILES])
        small = sb("small", [P, TILES])
        wext = sb("wext", [P, 2, EXT])
        wkvT = sb("wkvT", [P, 2, 2 * INNER])
        wq = sb("wq", [P, 4, C])
        woutT = sb("woutT", [P, 4, C])
        mixG = sb("mixG", [P, 2, C])
        bout_row = sb("bout_row", [1, C])
        src_cols = sb("src_cols", [P, PCH * P], I32)
        dst_cols = sb("dst_cols", [P, PCH * P + 2])
        pair_acc = sb("pair_acc", [1, PCH * P], I32)
        big = sb("big", [P, 8192])

        def flat(t):
            return t[:, :, :].rearrange("p t c -> p (t c)")

        work_f, acc_f = flat(work), flat(acc)

        def layer_stats(dve, steps):
            me, mo = stats[:, :, 1], stats[:, :, 4]
            steps.done(dve.tensor_tensor(mean[:, :], me, mo, ALU.subtract))
            steps.done(dve.tensor_tensor(small[:, :], mean[:, :], mean[:, :], ALU.mult))
            steps.done(dve.tensor_tensor(rstd[:, :], stats[:, :, 2], stats[:, :, 5], ALU.add))
            steps.done(dve.tensor_scalar(rstd[:, :], rstd[:, :], 1.0 / C, EPS, ALU.mult, ALU.add))
            steps.done(dve.scalar_tensor_tensor(rstd[:, :], small[:, :], 0.25, rstd[:, :],
                                                ALU.mult, ALU.add))
            steps.done(dve.tensor_tensor(mean[:, :], me, mo, ALU.add))
            steps.done(dve.tensor_scalar(mean[:, :], mean[:, :], 0.5, None, ALU.mult))

        kv_raw = big[:, 0:2048].rearrange("p (r c) -> p r c", c=C)
        wout_raw = big[:, 2048:3072].rearrange("p (r c) -> p r c", c=INNER)
        a_bc = big[:, 3072:3584].rearrange("p (a c) -> p a c", a=2)
        prod = big[:, 3584:3840]
        hmean = big[:, 3840:3872].rearrange("p (c g) -> p c g", c=2)
        with ExitStack() as stage:
            def tmp(name, shape, dt=F32):
                return stage.enter_context(nc.sbuf_tensor(name, shape, dt))

            last_rows = tmp("last_rows", [1, 2, P], I32)
            ends = tmp("ends", [P, ECH, P], I32)
            endsf = tmp("endsf", [P, ECH, 2])
            node0 = tmp("node0", [P, TILES])
            jrow = tmp("jrow", [P, TILES])
            kcol = tmp("kcol", [P, PCH])
            cmp = tmp("cmp", [P, TILES * ECH])
            cnt = tmp("cnt", [P, 2 * TILES])
            bounds = tmp("bounds", [P, 2 * TILES])
            npair = tmp("npair", [P, TILES])
            kend = tmp("kend", [P, TILES])
            toff = tmp("toff", [P, TILES])
            jk = tmp("jk", [P, PCH])
            tk = tmp("tk", [P, PCH])
            tki = tmp("tki", [P, PCH], I32)
            jbase = tmp("jbase", [P, PCH])
            joff = tmp("joff", [P, PCH], I32)
            dst_g = tmp("dst_g", [P, PCH, P], I32)
            src_g = tmp("src_g", [P, PCH, P], I32)
            dst_f = tmp("dst_f", [P, PCH, P])
            src_f = tmp("src_f", [P, PCH, P])
            zero_row = tmp("zero_row", [P, C])
            w_in = sem("w_in")
            bc_in = sem("bc_in")
            copied = sem("copied")
            tail_in = sem("tail_in")
            tail_out = sem("tail_out")
            ends_in = sem("ends_in")
            padded = sem("padded")
            consts = sem("consts")
            su_pe = sem("su_pe")
            su_act = sem("su_act")
            su_dve = sem("su_dve")
            counted = sem("counted")
            counts_sum = sem("counts_sum")
            tk_ready = sem("tk_ready")
            dst_got, src_got = sem("dst_got"), sem("src_got")
            joff_out, joff_in = sem("joff_out"), sem("joff_in")
            cols_f = sem("cols_f")
            cols_t = sem("cols_t")
            zeroed = sem("zeroed")
            zero_set = sem("zero_set")
            su_pool = sem("su_pool")
            with nc.Block() as block:
                @block.sync
                def _(sp):
                    full = (ETILES - 1) * P
                    sp.wait_ge(padded, 2)
                    for q, (s, rows) in enumerate(((src, src_rows), (dst, dst_rows))):
                        sp.dma_start(last_rows[0:1, q, 0:ELAST],
                                     s[full:NE].rearrange("(a b) -> a b", a=1)).then_inc(tail_in, 16)
                        sp.dma_start(rows[0:ETILES - 1, :],
                                     s[0:full].rearrange("(a b) -> a b", b=P)).then_inc(copied, 16)
                    sp.wait_ge(tail_in, 32)
                    for q, rows in enumerate((src_rows, dst_rows)):
                        sp.dma_start(rows[ETILES - 1:ETILES, :], last_rows[0:1, q, :]).then_inc(tail_out, 16)
                    sp.wait_ge(copied, 32)
                    sp.wait_ge(tail_out, 32)
                    whole = ETILES // P
                    sp.dma_start(ends[:, 0:whole, :],
                                 dst_rows[0:whole * P, :].rearrange("(c p) e -> p c e", p=P)).then_inc(ends_in, 16)
                    sp.dma_start(ends[0:ETILES - whole * P, whole, :],
                                 dst_rows[whole * P:ETILES, :]).then_inc(ends_in, 16)
                    sp.wait_ge(tk_ready, 2)
                    with nc.allow_non_contiguous_dma(reason="896 numbers"):
                        sp.dma_start(pair_acc_d.rearrange("(c p) -> p c", p=P), joff[:, :]).then_inc(joff_out, 16)
                    sp.wait_ge(joff_out, 16)
                    sp.dma_start(pair_acc[0:1, :], pair_acc_d.rearrange("(a b) -> a b", a=1)).then_inc(joff_in, 16)
                    sp.wait_ge(joff_in, 16)

                @block.scalar
                def _(act):
                    act.dma_start(wext[:, :, 0:C], gnn_W.rearrange("(c p) n -> p c n", p=P)).then_inc(w_in, 16)
                    act.dma_start(kv_raw, Wqkv[INNER:3 * INNER, :].rearrange("(r p) c -> p r c", p=P)).then_inc(w_in, 16)
                    act.dma_start(wout_raw, Wout.rearrange("(r p) c -> p r c", p=P)).then_inc(w_in, 16)
                    act.dma_start(wq[:, :, :], Wqkv[0:INNER, :].rearrange("(r p) c -> p r c", p=P)).then_inc(w_in, 16)
                    act.dma_start(bout_row[:, :], bout.rearrange("(a c) -> a c", a=1)).then_inc(w_in, 16)
                    for q, a in enumerate((a_src, a_dst)):
                        act.dma_start(a_bc[:, q, :], a.rearrange("h d -> (h d)").partition_broadcast(P)).then_inc(bc_in, 16)
                    for f in range(6):
                        act.wait_ge(su_pe, f + 1)
                        to = wkvT[:, f // 2, (f % 2) * 512:(f % 2 + 1) * 512] if f < 4 else \
                            woutT[:, 2 * (f - 4):2 * (f - 3), :].rearrange("p a c -> p (a c)")
                        act.copy(to, bank[f][:, :]).then_inc(su_act, 1)

                @block.gpsimd
                def _(pool):
                    steps = Steps(pool, su_pool)
                    steps.done(pool.memset(last_rows[:, 0, :], 0))
                    steps.done(pool.memset(last_rows[:, 1, :], NO_NODE))
                    pool.sem_inc(padded, 1)
                    steps.done(pool.memset(ones[:, :], 1.0))
                    steps.done(pool.memset(ident[:, :], 0.0))
                    steps.done(pool.affine_select(out=ident[:, :], in_=ident[:, :], compare_op=ALU.not_equal,
                                                  fill=1.0, base=0, pattern=[[-1, P]], channel_multiplier=1))
                    steps.done(pool.affine_select(out=below[:, :], in_=ones[:, :], compare_op=ALU.is_gt,
                                                  fill=0.0, base=0, pattern=[[1, P]], channel_multiplier=-1))
                    kw = dict(allow_small_or_imprecise_dtypes=True)
                    steps.done(pool.iota(iota[:, :], pattern=[[1, P]], base=0, channel_multiplier=0, **kw))
                    steps.done(pool.iota(node0[:, :], pattern=[[P, TILES]], base=0, channel_multiplier=0, **kw))
                    steps.done(pool.iota(jrow[:, :], pattern=[[1, TILES]], base=0, channel_multiplier=0, **kw))
                    steps.done(pool.iota(kcol[:, :], pattern=[[P, PCH]], base=0, channel_multiplier=1, **kw))
                    steps.done(pool.memset(zero_row[:, :], 0.0))
                    pool.sem_inc(consts, 1)
                    zt = zero_row[:, :].unsqueeze(1)
                    sx = slots_x.rearrange("(a p) c -> p a c", p=P)
                    for a in range(0, STILES + 1, 23):
                        n = min(23, STILES + 1 - a)
                        pool.dma_start(sx[:, a:a + n, :], zt.to_broadcast([P, n, C])).then_inc(zeroed, 16)
                    pool.memset(acc_f, 0.0).then_inc(su_pool, 1)
                    pool.wait_ge(tk_ready, 1)
                    for c in range(PCH):
                        at = bass.IndirectOffsetOnAxis(ap=tki[:, c:c + 1], axis=0)
                        pool.indirect_dma_start(dst_g[:, c, :], None, dst_rows, at).then_inc(dst_got, 16)
                        pool.indirect_dma_start(src_g[:, c, :], None, src_rows, at).then_inc(src_got, 16)
                    pool.wait_ge(dst_got, 16 * PCH)
                    pool.wait_ge(src_got, 16 * PCH)
                    pool.wait_ge(zeroed, 16 * -(-(STILES + 1) // 23))

                @block.tensor
                def _(pe):
                    pe.wait_ge(w_in, 80)
                    pe.wait_ge(consts, 1)
                    for f in range(4):
                        for q in range(4):
                            t = pe.transpose(bank[f][:, q * P:(q + 1) * P],
                                             kv_raw[:, (f % 2) * 4 + q, (f // 2) * P:(f // 2 + 1) * P], ident[:, :])
                        t.then_inc(su_pe, 1)
                    for f in range(2):
                        for q in range(2):
                            for c in range(2):
                                t = pe.transpose(bank[4 + f][:, q * C + c * P:q * C + (c + 1) * P],
                                                 wout_raw[:, c, (2 * f + q) * P:(2 * f + q + 1) * P], ident[:, :])
                        t.then_inc(su_pe, 1)
                    pe.wait_ge(counted, 1)
                    pe.matmul(bank[6][:, 0:2 * TILES], ones[:, :], cnt[:, :], start=True, stop=True).then_inc(counts_sum, 1)
                    pe.wait_ge(su_act, 4)
                    pe.wait_ge(cols_f, 1)
                    for q, t_f in enumerate((dst_f, src_f)):
                        for c in range(PCH):
                            t = pe.transpose(bank[2 * q + c // 4][:, (c % 4) * P:(c % 4 + 1) * P], t_f[:, c, :], ident[:, :])
                        t.then_inc(cols_t, 1)

                @block.vector
                def _(dve):
                    steps = Steps(dve, su_dve)
                    steps.done(dve.memset(ends[:, ECH - 1, :], NO_NODE))
                    dve.sem_inc(padded, 1)
                    dve.wait_ge(consts, 1)
                    dve.wait_ge(ends_in, 32)
                    for q in range(2):
                        steps.done(dve.tensor_copy(endsf[:, :, q], ends[:, :, q * (P - 1)]))
                    cmp_t = cmp[:, 0:TILES * ECH].rearrange("p (j c) -> p j c", c=ECH)
                    steps.done(dve.tensor_tensor(cmp_t, over(endsf[:, :, 1], TILES), spread(node0[:, :], ECH), ALU.is_lt))
                    steps.done(dve.tensor_reduce(cnt[:, 0:TILES], cmp_t, X, ALU.add))
                    steps.done(dve.tensor_scalar(node0[:, :], node0[:, :], float(P), None, ALU.add))
                    steps.done(dve.tensor_tensor(cmp_t, over(endsf[:, :, 0], TILES), spread(node0[:, :], ECH), ALU.is_lt))
                    dve.tensor_reduce(cnt[:, TILES:2 * TILES], cmp_t, X, ALU.add).then_inc(counted, 1)
                    dve.wait_ge(counts_sum, 1)
                    steps.done(dve.tensor_copy(bounds[:, :], bank[6][:, 0:2 * TILES]))
                    ts, te = bounds[:, 0:TILES], bounds[:, TILES:2 * TILES]
                    steps.done(dve.scalar_tensor_tensor(te, ts, 1.0, te, ALU.add, ALU.max))
                    steps.done(dve.tensor_tensor(npair[:, :], te, ts, ALU.subtract))
                    steps.done(dve.tensor_tensor_scan(kend[:, :], ones[:, 0:TILES], npair[:, :], 0.0, ALU.mult, ALU.add))
                    steps.done(dve.tensor_tensor(toff[:, :], te, kend[:, :], ALU.subtract))
                    cmp_k = cmp[:, 0:PCH * TILES].rearrange("p (c j) -> p c j", j=TILES)
                    steps.done(dve.tensor_tensor(cmp_k, over(kend[:, :], PCH), spread(kcol[:, :], TILES), ALU.is_le))
                    steps.done(dve.tensor_reduce(jk[:, :], cmp_k, X, ALU.add))
                    steps.done(dve.tensor_tensor(cmp_k, over(jrow[:, :], PCH), spread(jk[:, :], TILES), ALU.is_equal))
                    steps.done(dve.tensor_tensor(cmp_k, cmp_k, over(toff[:, :], PCH), ALU.mult))
                    steps.done(dve.tensor_reduce(tk[:, :], cmp_k, X, ALU.add))
                    steps.done(dve.tensor_tensor(tk[:, :], tk[:, :], kcol[:, :], ALU.add))
                    steps.done(dve.tensor_scalar(tki[:, :], tk[:, :], float(ETILES - 1), None, ALU.min))
                    dve.sem_inc(tk_ready, 1)
                    steps.done(dve.tensor_scalar(joff[:, :], jk[:, :], float(TILES - 1), float(EXT), ALU.min, ALU.mult))
                    dve.sem_inc(tk_ready, 1)
                    steps.done(dve.tensor_scalar(jbase[:, :], jk[:, :], -float(P), None, ALU.mult))
                    dve.wait_ge(w_in, 80)
                    dve.wait_ge(bc_in, 32)
                    for c in range(2):
                        for q in range(2):
                            steps.done(dve.tensor_tensor(prod, wext[:, c, 0:C], a_bc[:, q, :], ALU.mult))
                            steps.done(dve.tensor_reduce(wext[:, c, C + HEADS * q:C + HEADS * (q + 1)],
                                                         prod.rearrange("p (h d) -> p h d", d=HD), X, ALU.add))
                    dve.wait_ge(su_act, 4)
                    for c in range(2):
                        grouped = wkvT[:, c, :].rearrange("p (g d) -> p g d", d=MD)
                        steps.done(dve.tensor_reduce(hmean[:, c, :], grouped, X, ALU.add))
                        steps.done(dve.tensor_scalar(hmean[:, c, :], hmean[:, c, :], 1.0 / MD, None, ALU.mult))
                        steps.done(dve.tensor_tensor(grouped, grouped, spread(hmean[:, c, :], MD), ALU.subtract))
                    dve.wait_ge(dst_got, 16 * PCH)
                    dve.wait_ge(src_got, 16 * PCH)
                    for c in range(PCH):
                        steps.done(dve.tensor_scalar(dst_f[:, c, :], dst_g[:, c, :], jbase[:, c:c + 1], None, ALU.add))
                    steps.done(dve.tensor_copy(src_f[:, :, :], src_g[:, :, :]))
                    dve.sem_inc(cols_f, 1)
                    dve.wait_ge(cols_t, 2)
                    half = PCH * P - 512
                    steps.done(dve.tensor_copy(dst_cols[:, 0:512], bank[0][:, :]))
                    steps.done(dve.tensor_copy(dst_cols[:, 512:PCH * P], bank[1][:, 0:half]))
                    steps.done(dve.memset(dst_cols[:, PCH * P:PCH * P + 2], -1.0))
                    steps.done(dve.tensor_copy(src_cols[:, 0:512], bank[2][:, :]))
                    steps.done(dve.tensor_copy(src_cols[:, 512:PCH * P], bank[3][:, 0:half]))

        with ExitStack() as stage:
            def tmp(name, shape, dt=F32):
                return stage.enter_context(nc.sbuf_tensor(name, shape, dt))

            xn = tmp("xn", [P, 2, C])
            xnT = tmp("xnT", [P, 2, C])
            x_in = sem("x_in")
            last_zero = sem("last_zero")
            sqrted = sem("sqrted")
            var_ready = sem("var_ready")
            pj_dve = sem("pj_dve")
            xn_ready = sem("xn_ready")
            xn_turned = sem("xn_turned")
            xnT_ready = sem("xnT_ready")
            xnT_kept = [sem(f"xnT_kept{b}") for b in range(2)]
            proj_done = sem("proj_done")
            proj_kept = sem("proj_kept")
            XCH = (TILES - 1) // 4
            with nc.Block() as block:
                @block.sync
                def _(sp):
                    for q in range(4):
                        a, z = q * XCH, (q + 1) * XCH
                        sp.dma_start(work[:, a:z, 0:C], x[a * P:z * P, :].rearrange("(t p) c -> p t c", p=P)).then_inc(x_in, 16)
                    sp.wait_ge(last_zero, 1)
                    sp.dma_start(work[0:LAST, TILES - 1, 0:C], x[(TILES - 1) * P:N, :]).then_inc(x_in, 16)

                    def keep(t0, b):
                        sp.wait_ge(xnT_ready, t0 + b + 1)
                        sp.dma_start(xnT_d[bass.ds(t0 + b, 1), :, :].rearrange("a p c -> p (a c)"),
                                     xnT[:, b, :]).then_inc(xnT_kept[b], 16)

                    each_tile(sp, keep)
                    sp.wait_ge(xnT_kept[0], 16 * (TILES // 2 + 1))
                    sp.wait_ge(xnT_kept[1], 16 * (TILES // 2))

                @block.gpsimd
                def _(pool):
                    pool.memset(work[:, TILES - 1, :], 0.0).then_inc(last_zero, 1)

                @block.vector
                def _(dve):
                    steps = Steps(dve, pj_dve)
                    dve.wait_ge(x_in, 80)
                    with dve.Fori(0, TILES) as t:
                        dve.bn_stats(stats[:, bass.ds(t, 1), :].rearrange("p a c -> p (a c)"),
                                     work[:, bass.ds(t, 1), 0:C].rearrange("p a c -> p (a c)")).then_inc(pj_dve, 1)
                    steps.n = TILES
                    dve.wait_ge(pj_dve, TILES)
                    layer_stats(dve, steps)
                    dve.sem_inc(var_ready, 1)
                    dve.wait_ge(sqrted, 1)
                    steps.done(dve.reciprocal(rstd[:, :], rstd[:, :]))
                    dve.sem_inc(xn_turned, 2)

                    def norm(t0, b):
                        t = t0 + b
                        dve.wait_ge(xn_turned, t + 1)
                        dve.tensor_scalar(xn[:, b, :], work_f[:, bass.ds(t * EXT, C)], mean[:, bass.ds(t, 1)],
                                          rstd[:, bass.ds(t, 1)], ALU.subtract, ALU.mult).then_inc(xn_ready, 1)

                    each_tile(dve, norm)

                @block.tensor
                def _(pe):
                    pe.sem_inc(proj_kept, 2)

                    def turn_and_project(t0, b):
                        t = t0 + b
                        pe.wait_ge(xn_ready, t + 1)
                        pe.wait_ge(proj_kept, t + 1)
                        for c in range(2):
                            r = pe.transpose(bank[b][:, c * P:(c + 1) * P], xn[:, b, c * P:(c + 1) * P], ident[:, :])
                        r.then_inc(xn_turned, 1)
                        pe.wait_ge(xnT_ready, t + 1)
                        for c in range(2):
                            r = pe.matmul(bank[2 + b][:, 0:EXT], xnT[:, b, c * P:(c + 1) * P], wext[:, c, :],
                                          start=c == 0, stop=c == 1)
                        r.then_inc(proj_done, 1)

                    each_tile(pe, turn_and_project)

                @block.scalar
                def _(act):
                    act.wait_ge(var_ready, 1)
                    act.activation(rstd[:, :], rstd[:, :], ACT.Sqrt).then_inc(sqrted, 1)

                    def move(t0, b):
                        t = t0 + b
                        act.wait_ge(xn_turned, t + 3)
                        if not starts(t0):
                            act.wait_ge(xnT_kept[b], 8 * t0)
                        act.copy(xnT[:, b, :], bank[b][:, 0:C]).then_inc(xnT_ready, 1)
                        act.wait_ge(proj_done, t + 1)
                        act.copy(work_f[:, bass.ds(t * EXT, EXT)], bank[2 + b][:, 0:EXT]).then_inc(proj_kept, 1)

                    each_tile(act, move)

        with ExitStack() as stage:
            def tmp(name, shape, dt=F32):
                return stage.enter_context(nc.sbuf_tensor(name, shape, dt))

            ext2 = tmp("ext2", [P, 2 * HEADS])
            ext1 = tmp("ext1", [2 * HEADS, 1])
            diag = tmp("diag", [2 * HEADS, 2 * HEADS])
            amax = tmp("amax", [P, 2 * HEADS])
            wexp = tmp("wexp", [P, TILES, HEADS])
            wg_dve = sem("wg_dve")
            ext_ready, ext_turned = sem("ext_ready"), sem("ext_turned")
            diag_ready, amax_ready = sem("diag_ready"), sem("amax_ready")
            wexp_in, wexp_out = sem("wexp_in"), sem("wexp_out")
            rows_ready = sem("rows_ready")
            table_out = sem("table_out")
            GROUP = 7
            with nc.Block() as block:
                @block.vector
                def _(dve):
                    steps = Steps(dve, wg_dve)
                    alpha = work[:, :, C:C + HEADS]
                    steps.done(dve.tensor_reduce(ext2[:, 0:HEADS], alpha.rearrange("p t h -> p h t"), X, ALU.max))
                    steps.done(dve.tensor_scalar(wexp[:, :, :], alpha, -1.0, None, ALU.mult))
                    dve.tensor_reduce(ext2[:, HEADS:2 * HEADS], wexp[:, :, :].rearrange("p t h -> p h t"), X,
                                      ALU.max).then_inc(ext_ready, 1)
                    dve.wait_ge(ext_turned, 1)
                    steps.done(dve.tensor_reduce(ext1[:, :], bank[0][0:2 * HEADS, 0:P], X, ALU.max))
                    dve.tensor_scalar(diag[:, :], ident[0:2 * HEADS, 0:2 * HEADS], ext1[:, 0:1], None,
                                      ALU.mult).then_inc(diag_ready, 1)
                    dve.wait_ge(amax_ready, 1)
                    steps.done(dve.tensor_copy(amax[:, :], bank[1][:, 0:2 * HEADS]))
                    dve.tensor_tensor(wexp[:, :, :], alpha, over(amax[:, 0:HEADS], TILES), ALU.subtract).then_inc(wexp_in, 1)
                    dve.wait_ge(wexp_out, 1)
                    steps.done(dve.tensor_copy(alpha, wexp[:, :, :]))
                    wexp_f = wexp[:, :, :].rearrange("p t h -> p (t h)")
                    with dve.Fori(0, TILES) as t:
                        rows = work_f[:, bass.ds(t * EXT, C)].rearrange("p (h d) -> p h d", d=HD)
                        dve.tensor_tensor(rows, rows, spread(wexp_f[:, bass.ds(t * HEADS, HEADS)], HD),
                                          ALU.mult).then_inc(rows_ready, 1)

                @block.tensor
                def _(pe):
                    pe.wait_ge(ext_ready, 1)
                    pe.transpose(bank[0][0:2 * HEADS, 0:P], ext2[:, :], ident[:, :]).then_inc(ext_turned, 1)
                    pe.wait_ge(diag_ready, 1)
                    pe.matmul(bank[1][:, 0:2 * HEADS], ones[0:2 * HEADS, :], diag[:, :], start=True,
                              stop=True).then_inc(amax_ready, 1)

                @block.scalar
                def _(act):
                    act.wait_ge(wexp_in, 1)
                    act.activation(wexp[:, :, :], wexp[:, :, :], ACT.Exp).then_inc(wexp_out, 1)

                @block.sync
                def _(sp):
                    tab = table.rearrange("(t p) c -> p t c", p=P)
                    with sp.Fori(0, TILES // GROUP) as g:
                        t0 = g * GROUP
                        sp.wait_ge(rows_ready, t0 + GROUP)
                        sp.dma_start(tab[:, bass.ds(t0, GROUP), :], work[:, bass.ds(t0, GROUP), 0:ROW]).then_inc(table_out, 16)
                    sp.wait_ge(table_out, 16 * (TILES // GROUP))

        got = big[:, 0:UNROLL * ROW].rearrange("p (s c) -> p s c", c=ROW)
        with ExitStack() as stage:
            def tmp(name, shape, dt=F32):
                return stage.enter_context(nc.sbuf_tensor(name, shape, dt))

            HALF = UNROLL // 2
            idx = tmp("idx", [P, UNROLL], I32)
            onehot = tmp("onehot", [P, 4, P])
            kv_x = tmp("kv_x", [P, C])
            squares = tmp("squares", [P, 2 * INNER])
            kv_var = tmp("kv_var", [P, 2 * MH])
            kv_r = tmp("kv_r", [P, 2 * MH])
            k_scale = tmp("k_scale", [P, MH])
            k_n = tmp("k_n", [P, INNER])
            v_n = tmp("v_n", [P, INNER])
            zeros = tmp("zeros", [P, 512])
            dotsS = tmp("dotsS", [P, 4, P])
            g1T = tmp("g1T", [P, 4, C])
            idx_ready = sem("idx_ready")
            row_got = [sem(f"row_got{s}") for s in range(UNROLL)]
            rows_used = sem("rows_used")
            onehot_ready = sem("onehot_ready")
            summed = sem("summed")
            kvx_in = sem("kvx_in")
            kv_done = sem("kv_done")
            squared, v_moved = sem("squared"), sem("v_moved")
            var_in, var_out = sem("var_in"), sem("var_out")
            k_ready = sem("k_ready")
            dots_done = sem("dots_done")
            eg_dve = sem("eg_dve")
            zeros_set = sem("zeros_set")
            dS_ready, g1_done, g1_moved, g_done, g_moved = (sem(n) for n in (
                "dS_ready", "g1_done", "g1_moved", "g_done", "g_moved"))
            KB, VB, DB = bank[4], bank[5], bank[6]
            with nc.Block() as block:
                @block.gpsimd
                def _(pool):
                    def gathers(r):
                        for s in range(UNROLL):
                            if s % HALF == 0:
                                pool.wait_ge(idx_ready, 2 * r + 1 + s // HALF)
                            pool.wait_ge(rows_used, r * UNROLL + s + 1)
                            pool.sem_inc(pool_on, 1)
                            pool.indirect_dma_start(got[:, s, :], None, table,
                                                    bass.IndirectOffsetOnAxis(ap=idx[:, s:s + 1], axis=0)
                                                    ).then_inc(row_got[s], 16)

                    with pool.Fori(0, ROUNDS) as r:
                        gathers(r)

                @block.scalar
                def _(act):
                    def indices(r):
                        for h in range(2):
                            act.wait_ge(rows_used, r * UNROLL + (h + 1) * HALF)
                            act.copy(idx[:, h * HALF:(h + 1) * HALF],
                                     src_cols[:, bass.ds(r * UNROLL + h * HALF, HALF)]).then_inc(idx_ready, 1)

                    def keys_values(r):
                        act.wait_ge(kv_done, r + 1)
                        act.activation(squares[:, 0:INNER], KB[:, :], ACT.Square)
                        act.activation(squares[:, INNER:2 * INNER], VB[:, :], ACT.Square).then_inc(squared, 1)
                        act.wait_ge(dots_done, r + 1)
                        act.copy(v_n[:, :], VB[:, :]).then_inc(v_moved, 1)
                        act.wait_ge(var_in, r + 1)
                        act.activation(kv_r[:, :], kv_var[:, :], ACT.Sqrt).then_inc(var_out, 1)

                    with act.Fori(0, TILES) as r:
                        indices(r)
                        keys_values(r)
                    with act.Fori(TILES, ROUNDS) as r:
                        indices(r)

                @block.sync
                def _(sp):
                    def load(r):
                        sp.dma_start(kv_x[:, :], xnT_d[bass.ds(r, 1), :, :].rearrange("a p c -> p (a c)")).then_inc(kvx_in, 16)

                    load(0)
                    with sp.Fori(1, TILES) as r:
                        sp.wait_ge(kv_done, r)
                        load(r)

                @block.tensor
                def _(pe):
                    pe.sem_inc(rows_used, UNROLL)
                    pe.sem_inc(summed, 4)
                    pe.sem_inc(k_ready, 1)
                    pe.wait_ge(zeros_set, 1)
                    pe.matmul(DB[:, :], zeros[:, 0:P], zeros[:, :], start=True, stop=False, skip_group_check=True).then_inc(dots_done, 1)

                    def sum_rows(r, s):
                        k = r * UNROLL + s
                        pe.wait_ge(onehot_ready, k + 1)
                        pe.wait_ge(row_got[s], r * 16 + 16)
                        pe.wait_ge(summed, k + 1)
                        pe.matmul(bank[s % 4][:, 0:ROW], onehot[:, s % 4, :], got[:, s, :], start=True,
                                  stop=True).then_inc(rows_used, 1)

                    def project_kv(r):
                        pe.wait_ge(kvx_in, r * 16 + 16)
                        pe.wait_ge(k_ready, r + 1)
                        for o, b in ((0, KB), (INNER, VB)):
                            for c in range(2):
                                m = pe.matmul(b[:, :], kv_x[:, c * P:(c + 1) * P], wkvT[:, c, o:o + INNER],
                                              start=c == 0, stop=c == 1)
                        m.then_inc(kv_done, 1)

                    def dots(r):
                        pe.wait_ge(k_ready, r + 2)
                        pe.wait_ge(v_moved, r + 1)
                        for q in range(4):
                            m = pe.matmul(DB[:, q * P:(q + 1) * P], k_n[:, q * P:(q + 1) * P], v_n[:, q * P:(q + 1) * P],
                                          start=False, stop=False, skip_group_check=True)
                        m.then_inc(dots_done, 1)

                    with pe.Fori(0, TILES) as r:
                        project_kv(r)
                        for s in range(UNROLL):
                            sum_rows(r, s)
                        dots(r)
                    pe.matmul(DB[:, :], zeros[:, 0:P], zeros[:, :], start=False, stop=True, skip_group_check=True).then_inc(dots_done, 1)
                    pe.wait_ge(dS_ready, 1)
                    for q in range(4):
                        m = pe.matmul([KB, VB][q // 2][:, (q % 2) * C:(q % 2 + 1) * C], dotsS[:, q, :], wq[:, q, :],
                                      start=True, stop=True)
                    m.then_inc(g1_done, 1)
                    pe.wait_ge(g1_moved, 1)
                    for c in range(2):
                        for q in range(4):
                            m = pe.matmul(bank[7][:, c * C:(c + 1) * C], g1T[:, q, c * P:(c + 1) * P], woutT[:, q, :],
                                          start=q == 0, stop=q == 3)
                    m.then_inc(g_done, 1)
                    with pe.Fori(TILES, ROUNDS) as r:
                        for s in range(UNROLL):
                            sum_rows(r, s)

                @block.vector
                def _(dve):
                    dve.memset(zeros[:, :], 0.0).then_inc(zeros_set, 1)
                    dve.memset(dotsS[:, :, :], 0.0).then_inc(zeros_set, 1)
                    regs = [dve.alloc_register(f"at{s}") for s in range(UNROLL)]

                    def targets(k, s):
                        dve.wait_ge(rows_used, k + UNROLL - 3)
                        dve.tensor_scalar(onehot[:, s % 4, :], iota[:, :], dst_cols[:, bass.ds(k, 1)], None,
                                          ALU.is_equal).then_inc(onehot_ready, 1)

                    def add(k, s):
                        at = dve.snap(regs[s], min_val=0, max_val=(TILES - 1) * EXT)
                        to = acc_f[:, bass.ds(at, ROW)]
                        dve.wait_ge(rows_used, k + UNROLL + 1)
                        dve.wait_ge(summed, k + 4)
                        dve.tensor_tensor(to, to, bank[s % 4][:, 0:ROW], ALU.add).then_inc(summed, 1)

                    steps = Steps(dve, eg_dve)

                    def kv_var_of(r):
                        dve.wait_ge(squared, r + 1)
                        steps.done(dve.tensor_reduce(kv_var[:, :], squares[:, :].rearrange("p (g d) -> p g d", d=MD), X, ALU.add))
                        dve.tensor_scalar(kv_var[:, :], kv_var[:, :], 1.0 / MD, EPS, ALU.mult, ALU.add).then_inc(var_in, 1)

                    def scale_k(r):
                        dve.wait_ge(var_out, r + 1)
                        steps.done(dve.reciprocal(kv_r[:, :], kv_r[:, :]))
                        steps.done(dve.tensor_tensor(k_scale[:, :], kv_r[:, 0:MH], kv_r[:, MH:2 * MH], ALU.mult))
                        dve.wait_ge(v_moved, r + 1)
                        dve.tensor_tensor(k_n[:, :].rearrange("p (g d) -> p g d", d=MD),
                                          KB[:, :].rearrange("p (g d) -> p g d", d=MD), spread(k_scale[:, :], MD),
                                          ALU.mult).then_inc(k_ready, 1)

                    targets(0, 0)
                    targets(1, 1)

                    def round_(r, with_kv):
                        dve.load(regs, pair_acc[0:1, bass.ds(r * UNROLL, UNROLL)])
                        for s in range(UNROLL):
                            targets(r * UNROLL + s + 2, s + 2)
                            add(r * UNROLL + s, s)
                            if with_kv and s == UNROLL // 2:
                                kv_var_of(r)
                            if with_kv and s == UNROLL // 2 + 4:
                                scale_k(r)

                    with dve.Fori(0, TILES) as r:
                        steps.at(r * 3)
                        round_(r, True)
                    dve.wait_ge(dots_done, TILES + 2)
                    dve.wait_ge(zeros_set, 2)
                    for q in range(4):
                        for h in range(2):
                            d = dve.tensor_scalar(dotsS[h * MD:(h + 1) * MD, q, h * MD:(h + 1) * MD],
                                                  DB[h * MD:(h + 1) * MD, q * P + h * MD:q * P + (h + 1) * MD],
                                                  1.0 / N, None, ALU.mult)
                    d.then_inc(dS_ready, 1)
                    dve.wait_ge(g1_done, 1)
                    for q, b in enumerate((KB, VB)):
                        d = dve.tensor_copy(g1T[:, 2 * q:2 * q + 2, :].rearrange("p a c -> p (a c)"), b[:, :])
                    d.then_inc(g1_moved, 1)
                    dve.wait_ge(g_done, 1)
                    dve.tensor_copy(mixG[:, :, :].rearrange("p a c -> p (a c)"), bank[7][:, :]).then_inc(g_moved, 1)
                    with dve.Fori(TILES, ROUNDS) as r:
                        round_(r, False)
                    dve.wait_ge(summed, PAIRS + 4)


        xn2 = work
        with ExitStack() as stage2:
            def keep_(name, shape, dt=F32):
                return stage2.enter_context(nc.sbuf_tensor(name, shape, dt))

            pick = keep_("pick", [P, 2, TILES, EXPERTS])
            share = keep_("share", [P, 2, TILES])
            slot = keep_("slot", [P, TILES, 2], I32)
            top = keep_("top", [P, 2, TILES])
            topi = keep_("topi", [P, 2, TILES])
            expert_row = keep_("expert_row", [1, STILES], I32)
            b1T = keep_("b1T", [P, EXPERTS * 4])
            b2_all = keep_("b2_all", [EXPERTS, C])
            gamma_bc = keep_("gamma_bc", [P, C])
            beta_bc = keep_("beta_bc", [P, C])
            rowid = keep_("rowid", [P, 2])
            with ExitStack() as stage:
                def tmp(name, shape, dt=F32):
                    return stage.enter_context(nc.sbuf_tensor(name, shape, dt))

                gate = tmp("gate", [P, 2, EXPERTS])
                gate_b_row = tmp("gate_b_row", [1, EXPERTS])
                b1_raw = tmp("b1_raw", [EXPERTS * 4, P])
                x_t = tmp("x_t", [P, 2, C])
                xnT_t = tmp("xnT_t", [P, 2, C])
                rsum = tmp("rsum", [P, TILES, HEADS])
                gat = tmp("gat", [P, 2, C])
                row2 = tmp("row2", [P, 2, C])
                row2T = tmp("row2T", [P, 2, C])
                logits = tmp("logits", [P, 2, EXPERTS])
                top8 = tmp("top8", [P, 2, 8])
                top8i = tmp("top8i", [P, 2, 8], U32)
                js_in = sem("js_in")
                x_got = [sem(f"x_got{b}") for b in range(2)]
                jn_dve = sem("jn_dve")
                b1_turned, b1_kept = sem("b1_turned"), sem("b1_kept")
                mixed = sem("mixed")
                x1_ready = sem("x1_ready")
                var2_ready, sqrt2 = sem("var2_ready"), sem("sqrt2")
                row2_ready, row2_turned, row2T_ready = sem("row2_ready"), sem("row2_turned"), sem("row2T_ready")
                gated, logits_read = sem("gated"), sem("logits_read")
                e_in, e_out = sem("e_in"), sem("e_out")
                with nc.Block() as block:
                    @block.sync
                    def _(sp):
                        sp.dma_start(gate[:, :, :], gate_w.rearrange("(c p) e -> p c e", p=P)).then_inc(js_in, 16)
                        sp.dma_start(gate_b_row[:, :], gate_b.rearrange("(a c) -> a c", a=1)).then_inc(js_in, 16)
                        sp.dma_start(b1_raw[:, :], b1.rearrange("e (f p) -> (e f) p", p=P)).then_inc(js_in, 16)
                        sp.dma_start(b2_all[:, :], b2).then_inc(js_in, 16)
                        sp.dma_start(gamma_bc[:, :], gamma.partition_broadcast(P)).then_inc(js_in, 16)
                        sp.dma_start(beta_bc[:, :], beta.partition_broadcast(P)).then_inc(js_in, 16)

                        def load(t0, b):
                            t = t0 + b
                            sp.wait_ge(x1_ready, t + 1)
                            if is_last(t0):
                                sp.dma_start(x_t[0:LAST, b, :], x[t * P:N, :]).then_inc(x_got[b], 16)
                            else:
                                sp.dma_start(x_t[:, b, :], x[bass.ds(t * P, P), :]).then_inc(x_got[b], 16)
                            sp.dma_start(xnT_t[:, b, :], xnT_d[bass.ds(t, 1), :, :].rearrange("a p c -> p (a c)")).then_inc(x_got[b], 16)

                        each_tile(sp, load)
                        sp.wait_ge(js_in, 96)

                    @block.tensor
                    def _(pe):
                        pe.sem_inc(x1_ready, 2)
                        pe.wait_ge(js_in, 96)
                        pe.transpose(bank[6][:, 0:EXPERTS * 4], b1_raw[:, :], ident[0:EXPERTS * 4, 0:EXPERTS * 4]).then_inc(b1_turned, 1)

                        def mix(t0, b):
                            pe.wait_ge(x_got[b], 16 * t0 + 32)
                            pe.wait_ge(x1_ready, t0 + b + 1)
                            for c in range(2):
                                pe.matmul(bank[b][:, 0:C], xnT_t[:, b, c * P:(c + 1) * P], mixG[:, c, :], start=c == 0, stop=False)
                            pe.matmul(bank[b][:, 0:C], ones[0:1, :], bout_row[:, :], start=False, stop=True).then_inc(mixed, 1)

                        each_tile(pe, mix)

                        def gates(t0, b):
                            t = t0 + b
                            pe.wait_ge(row2_ready, t + 1)
                            pe.wait_ge(logits_read, t + 1)
                            for c in range(2):
                                m = pe.transpose(bank[2 + b][:, c * P:(c + 1) * P], row2[:, b, c * P:(c + 1) * P], ident[:, :])
                            m.then_inc(row2_turned, 1)
                            pe.wait_ge(row2T_ready, t + 3)
                            for c in range(2):
                                pe.matmul(bank[4 + b][:, 0:EXPERTS], row2T[:, b, c * P:(c + 1) * P], gate[:, c, :], start=c == 0, stop=False)
                            pe.matmul(bank[4 + b][:, 0:EXPERTS], ones[0:1, :], gate_b_row[:, :], start=False, stop=True).then_inc(gated, 1)

                        pe.sem_inc(logits_read, 2)
                        pe.sem_inc(row2T_ready, 2)
                        each_tile(pe, gates)

                    @block.scalar
                    def _(act):
                        act.wait_ge(b1_turned, 1)
                        act.copy(b1T[:, :], bank[6][:, 0:EXPERTS * 4]).then_inc(b1_kept, 1)
                        act.wait_ge(var2_ready, 1)
                        act.activation(rstd[:, :], rstd[:, :], ACT.Sqrt).then_inc(sqrt2, 1)

                        def move(t0, b):
                            t = t0 + b
                            act.wait_ge(row2_ready, t + 1)
                            act.copy(work_f[:, bass.ds(t * EXT, C)], row2[:, b, :])
                            act.wait_ge(row2_turned, t + 1)
                            act.copy(row2T[:, b, :], bank[2 + b][:, 0:C]).then_inc(row2T_ready, 1)

                        each_tile(act, move)
                        act.wait_ge(e_in, 1)
                        act.activation(share[:, 1, :], share[:, 0, :], ACT.Exp).then_inc(e_out, 1)

                    @block.vector
                    def _(dve):
                        steps = Steps(dve, jn_dve)
                        steps.done(dve.tensor_scalar(rsum[:, :, :], acc[:, :, C:C + HEADS], 1e-16, None, ALU.add))
                        steps.done(dve.reciprocal(rsum[:, :, :], rsum[:, :, :]))
                        rsum_f = rsum[:, :, :].rearrange("p t h -> p (t h)")
                        first = steps.n

                        def joined(t0, b):
                            t = t0 + b
                            steps.at(first + t * 4)
                            rows = acc_f[:, bass.ds(t * EXT, C)]
                            steps.done(dve.tensor_tensor(gat[:, b, :].rearrange("p (h d) -> p h d", d=HD),
                                                         rows.rearrange("p (h d) -> p h d", d=HD),
                                                         spread(rsum_f[:, bass.ds(t * HEADS, HEADS)], HD), ALU.mult))
                            dve.wait_ge(x_got[b], 16 * t0 + 32)
                            steps.done(dve.tensor_tensor(gat[:, b, :], gat[:, b, :], x_t[:, b, :], ALU.add))
                            dve.wait_ge(mixed, t + 1)
                            steps.done(dve.tensor_tensor(rows, gat[:, b, :], bank[b][:, 0:C], ALU.add))
                            dve.sem_inc(x1_ready, 1)
                            steps.done(dve.bn_stats(stats[:, bass.ds(t, 1), :].rearrange("p a c -> p (a c)"), rows))

                        each_tile(dve, joined)
                        steps.at(first + TILES * 4)
                        layer_stats(dve, steps)
                        dve.sem_inc(var2_ready, 1)
                        dve.wait_ge(sqrt2, 1)
                        steps.done(dve.reciprocal(rstd[:, :], rstd[:, :]))
                        after = steps.base + steps.n

                        def normed(t0, b):
                            t = t0 + b
                            dve.wait_ge(row2T_ready, t + 1)
                            dve.tensor_scalar(row2[:, b, :], acc_f[:, bass.ds(t * EXT, C)], mean[:, bass.ds(t, 1)],
                                              rstd[:, bass.ds(t, 1)], ALU.subtract, ALU.mult).then_inc(row2_ready, 1)

                        def best(t0, b):
                            t = t0 + b
                            steps.at(after + t * 5)
                            dve.wait_ge(gated, t + 1)
                            steps.done(dve.tensor_copy(logits[:, b, :], bank[4 + b][:, 0:EXPERTS]))
                            dve.sem_inc(logits_read, 1)
                            steps.done(dve.max(top8[:, b, :], logits[:, b, :]))
                            steps.go(dve.tensor_copy(top[:, :, bass.ds(t, 1)].rearrange("p q a -> p (q a)"), top8[:, b, 0:2]))
                            steps.done(dve.max_index(top8i[:, b, :], top8[:, b, :], logits[:, b, :]))
                            steps.done(dve.tensor_copy(topi[:, :, bass.ds(t, 1)].rearrange("p q a -> p (q a)"), top8i[:, b, 0:2]))

                        def choose(t0, buffers):
                            for b in buffers:
                                normed(t0, b)
                            for b in buffers:
                                best(t0, b)

                        each_pair(dve, choose)
                        steps.at(after + TILES * 5)
                        steps.done(dve.tensor_tensor(share[:, 0, :], top[:, 1, :], top[:, 0, :], ALU.subtract))
                        dve.sem_inc(e_in, 1)
                        dve.wait_ge(e_out, 1)
                        steps.done(dve.tensor_scalar(share[:, 0, :], share[:, 1, :], 1.0, None, ALU.add))
                        steps.done(dve.reciprocal(share[:, 0, :], share[:, 0, :]))
                        steps.done(dve.tensor_tensor(share[:, 1, :], share[:, 1, :], share[:, 0, :], ALU.mult))
                        for q in range(2):
                            steps.done(dve.tensor_tensor(pick[:, q, :, :], over(iota[:, 0:EXPERTS], TILES),
                                                         spread(topi[:, q, :], EXPERTS), ALU.is_equal))
                        dve.wait_ge(b1_kept, 1)

            with ExitStack() as stage:
                def tmp(name, shape, dt=F32):
                    return stage.enter_context(nc.sbuf_tensor(name, shape, dt))

                both = tmp("both", [P, TILES, EXPERTS])
                total = tmp("total", [P, TILES, EXPERTS])
                ahead = tmp("ahead", [P, TILES, EXPERTS])
                place = tmp("place", [P, TILES, EXPERTS])
                etiles = tmp("etiles", [P, EXPERTS])
                etiles_i = tmp("etiles_i", [P, EXPERTS], I32)
                eend = tmp("eend", [P, EXPERTS])
                ebase = tmp("ebase", [P, EXPERTS])
                trash = tmp("trash", [P, 2])
                slot_f = tmp("slot_f", [P, 2, TILES])
                scol = tmp("scol", [1, STILES])
                ecmp = tmp("ecmp", [1, STILES, EXPERTS])
                eidx = tmp("eidx", [1, STILES])
                stage_x = tmp("stage_x", [P, 2, C])
                stage_s = tmp("stage_s", [P, 2, 2], I32)
                rt_pool, iota_set = sem("rt_pool"), sem("iota_set")
                rt_dve = sem("rt_dve")
                both_ready, ranked = sem("both_ready"), sem("ranked")
                slots_ready = sem("slots_ready")
                staged = sem("staged")
                sent = [sem(f"sent{b}") for b in range(2)]
                HT = TILES // 2 + 1
                spans = ((0, HT), (HT, TILES))
                with nc.Block() as block:
                    @block.gpsimd
                    def _(pool):
                        kw = dict(allow_small_or_imprecise_dtypes=True)
                        pool.iota(scol[:, :], pattern=[[1, STILES]], base=0, channel_multiplier=0, **kw)
                        pool.iota(trash[:, :], pattern=[[-P // 2, 2]], base=STILES * P, channel_multiplier=1, **kw)
                        pool.iota(rowid[:, 1:2], pattern=[[1, 1]], base=0, channel_multiplier=1, **kw).then_inc(iota_set, 1)

                        def send(t0, b):
                            pool.wait_ge(staged, t0 + b + 1)
                            pool.sem_inc(pool_on, 1)
                            for q in range(2):
                                pool.indirect_dma_start(slots_x, bass.IndirectOffsetOnAxis(ap=stage_s[:, b, q:q + 1], axis=0),
                                                        stage_x[:, b, :], None).then_inc(sent[b], 16)

                        each_tile(pool, send)
                        pool.wait_ge(sent[0], 32 * (TILES // 2 + 1))
                        pool.wait_ge(sent[1], 32 * (TILES // 2))

                    @block.scalar
                    def _(act):
                        act.wait_ge(slots_ready, 1)
                        slot_i = slot[:, :, :].rearrange("p t q -> p (t q)")

                        def put(t0, b):
                            t = t0 + b
                            if not starts(t0):
                                act.wait_ge(sent[b], 16 * t0)
                            act.copy(stage_x[:, b, :], work_f[:, bass.ds(t * EXT, C)])
                            act.copy(stage_s[:, b, :], slot_i[:, bass.ds(t * 2, 2)]).then_inc(staged, 1)

                        each_tile(act, put)

                    @block.tensor
                    def _(pe):
                        pe.wait_ge(both_ready, 1)
                        for h, (a, z) in enumerate(spans):
                            rows = both[:, a:z, :].rearrange("p t e -> p (t e)")
                            pe.matmul(bank[h][:, 0:(z - a) * EXPERTS], ones[:, :], rows, start=True, stop=True)
                            m = pe.matmul(bank[2 + h][:, 0:(z - a) * EXPERTS], below[:, :], rows, start=True, stop=True)
                        m.then_inc(ranked, 1)

                    @block.vector
                    def _(dve):
                        steps = Steps(dve, rt_dve)
                        dve.wait_ge(iota_set, 1)
                        steps.done(dve.tensor_scalar(rowid[:, 0:1], rowid[:, 1:2], float(LAST), None, ALU.is_lt))
                        for q in range(2):
                            steps.done(dve.tensor_scalar(pick[:, q, TILES - 1, :], pick[:, q, TILES - 1, :], rowid[:, 0:1], None, ALU.mult))
                        dve.tensor_tensor(both[:, :, :], pick[:, 0, :, :], pick[:, 1, :, :], ALU.add).then_inc(both_ready, 1)
                        dve.wait_ge(ranked, 1)
                        for h, (a, z) in enumerate(spans):
                            n = (z - a) * EXPERTS
                            steps.done(dve.tensor_copy(total[:, a:z, :].rearrange("p t e -> p (t e)"), bank[h][:, 0:n]))
                            steps.done(dve.tensor_copy(place[:, a:z, :].rearrange("p t e -> p (t e)"), bank[2 + h][:, 0:n]))
                        for e in range(EXPERTS):
                            steps.done(dve.tensor_tensor_scan(ahead[:, :, e], ones[:, 0:TILES], total[:, :, e], 0.0, ALU.mult, ALU.add))
                        steps.done(dve.tensor_scalar(etiles_i[:, :], ahead[:, TILES - 1, :], float(P - 1), None, ALU.add))
                        steps.done(dve.tensor_scalar(etiles_i[:, :], etiles_i[:, :], 7, None, ALU.arith_shift_right))
                        steps.done(dve.tensor_copy(etiles[:, :], etiles_i[:, :]))
                        steps.done(dve.tensor_tensor_scan(eend[:, :], ones[:, 0:EXPERTS], etiles[:, :], 0.0, ALU.mult, ALU.add))
                        steps.done(dve.tensor_tensor(ebase[:, :], eend[:, :], etiles[:, :], ALU.subtract))
                        steps.done(dve.tensor_scalar(ebase[:, :], ebase[:, :], float(P), None, ALU.mult))
                        steps.done(dve.tensor_tensor(ahead[:, :, :], ahead[:, :, :], total[:, :, :], ALU.subtract))
                        steps.done(dve.tensor_tensor(place[:, :, :], place[:, :, :], ahead[:, :, :], ALU.add))
                        steps.done(dve.tensor_tensor(place[:, :, :], place[:, :, :], over(ebase[:, :], TILES), ALU.add))
                        for q in range(2):
                            steps.done(dve.tensor_tensor(total[:, :, :], place[:, :, :], pick[:, q, :, :], ALU.mult))
                            steps.done(dve.tensor_reduce(slot_f[:, q, :], total[:, :, :], X, ALU.add))
                        steps.done(dve.tensor_scalar(rowid[:, 1:2], rowid[:, 0:1], -1.0, 1.0, ALU.mult, ALU.add))
                        steps.done(dve.tensor_scalar(trash[:, :], trash[:, :], rowid[:, 1:2], None, ALU.mult))
                        for q in range(2):
                            steps.done(dve.tensor_tensor(slot_f[:, q, TILES - 1:TILES], slot_f[:, q, TILES - 1:TILES], trash[:, q:q + 1], ALU.add))
                            steps.done(dve.tensor_copy(slot[:, :, q], slot_f[:, q, :]))
                        dve.sem_inc(slots_ready, 1)
                        steps.done(dve.tensor_tensor(ecmp[:, :, :], over(eend[0:1, :], STILES), spread(scol[:, :], EXPERTS), ALU.is_le))
                        steps.done(dve.tensor_reduce(eidx[:, :], ecmp[:, :, :], X, ALU.add))
                        steps.done(dve.tensor_scalar(expert_row[:, :], eidx[:, :], float(EXPERTS - 1), None, ALU.min))
                        dve.wait_ge(sent[0], 32 * (TILES // 2 + 1))
                        for q in range(2):
                            steps.done(dve.tensor_tensor(slot_f[:, q, TILES - 1:TILES], slot_f[:, q, TILES - 1:TILES], rowid[:, 0:1], ALU.mult))
                            steps.done(dve.tensor_copy(slot[:, :, q], slot_f[:, q, :]))

            with ExitStack() as stage:
                def tmp(name, shape, dt=F32):
                    return stage.enter_context(nc.sbuf_tensor(name, shape, dt))

                w1_s = big[:, 0:2048].rearrange("p (b c f) -> p b c f", b=2, c=2)
                w2_s = big[:, 2048:4096].rearrange("p (b c f) -> p b c f", b=2, c=4)
                in_s = big[:, 4096:4608].rearrange("p (b c) -> p b c", b=2)
                inT = big[:, 4608:5120].rearrange("p (b c) -> p b c", b=2)
                hid = big[:, 5120:6144].rearrange("p (b f s) -> p b f s", b=2, f=4)
                res = big[:, 6144:6656].rearrange("p (b c) -> p b c", b=2)
                w1_got = [sem(f"w1_got{b}") for b in range(2)]
                w2_got = [sem(f"w2_got{b}") for b in range(2)]
                in_got = [sem(f"in_got{b}") for b in range(2)]
                in_turned, inT_ready = sem("in_turned"), sem("inT_ready")
                h_done, h_ready = sem("h_done"), sem("h_ready")
                y_done, y_ready = sem("y_done"), sem("y_ready")
                y_out = [sem(f"y_out{b}") for b in range(2)]
                FC = FF // P
                with nc.Block() as block:
                    @block.sync
                    def _(sp):
                        e_reg = sp.alloc_register("expert_sp")

                        def load(s0, b):
                            s = s0 + b
                            sp.load(e_reg, expert_row[0:1, bass.ds(s, 1)])
                            e = sp.snap(e_reg, min_val=0, max_val=EXPERTS - 1)
                            sp.wait_ge(in_turned, s + 1)
                            sp.dma_start(in_s[:, b, :], slots_x[bass.ds(s * P, P), :]).then_inc(in_got[b], 16)
                            sp.wait_ge(h_done, s + 1)
                            sp.dma_start(w1_s[:, b, :, :], w1[bass.ds(e, 1), :, :].rearrange("a (c p) f -> p (a c) f", p=P)).then_inc(w1_got[b], 16)
                            sp.wait_ge(y_done, s + 1)
                            sp.dma_start(w2_s[:, b, :, :], w2[bass.ds(e, 1), :, :].rearrange("a (c p) f -> p (a c) f", p=P)).then_inc(w2_got[b], 16)

                        with by_two(sp, 0, STILES) as s0:
                            load(s0, 0)
                            load(s0, 1)

                    @block.tensor
                    def _(pe):
                        pe.sem_inc(in_turned, 2)
                        pe.sem_inc(h_done, 2)
                        pe.sem_inc(y_done, 2)
                        pe.sem_inc(y_ready, 2)

                        def turn(s, b, got):
                            pe.wait_ge(in_got[b], got)
                            for c in range(2):
                                m = pe.transpose(bank[b][:, c * P:(c + 1) * P], in_s[:, b, c * P:(c + 1) * P], ident[:, :])
                            m.then_inc(in_turned, 1)

                        def hidden(s, b, got):
                            pe.wait_ge(inT_ready, s + 1)
                            pe.wait_ge(w1_got[b], got)
                            for f in range(FC):
                                for c in range(2):
                                    m = pe.matmul(bank[2 + b][:, f * P:(f + 1) * P], w1_s[:, b, c, f * P:(f + 1) * P],
                                                  inT[:, b, c * P:(c + 1) * P], start=c == 0, stop=c == 1)
                            m.then_inc(h_done, 1)

                        def down(s, b, got):
                            pe.wait_ge(h_ready, s + 1)
                            pe.wait_ge(w2_got[b], got)
                            pe.wait_ge(y_ready, s + 1)
                            for f in range(FC):
                                m = pe.matmul(bank[4 + b][:, 0:C], hid[:, b, f, :], w2_s[:, b, f, :], start=f == 0, stop=f == FC - 1)
                            m.then_inc(y_done, 1)

                        turn(0, 0, 16)
                        hidden(0, 0, 16)
                        turn(1, 1, 16)
                        hidden(1, 1, 16)
                        pe.wait_ge(h_ready, 1)
                        pe.wait_ge(w2_got[0], 16)
                        for f in range(FC):
                            m = pe.matmul(bank[4][:, 0:C], hid[:, 0, f, :], w2_s[:, 0, f, :], start=f == 0, stop=f == FC - 1)
                        m.then_inc(y_done, 1)
                        turn(2, 0, 32)

                        def two(s, more):
                            hidden(s, 0, 8 * s + 16)
                            down(s - 1, 1, 8 * s)
                            turn(s + 1, 1, 8 * s + 16)
                            hidden(s + 1, 1, 8 * s + 16)
                            down(s, 0, 8 * s + 16)
                            if more:
                                turn(s + 2, 0, 8 * s + 32)

                        with by_two(pe, 2, STILES - 2) as s:
                            two(s, True)
                        two(STILES - 2, False)
                        down(STILES - 1, 1, 8 * STILES)

                    @block.scalar
                    def _(act):
                        e_reg = act.alloc_register("expert_act")

                        def relu(s0, b):
                            s = s0 + b
                            act.load(e_reg, expert_row[0:1, bass.ds(s, 1)])
                            e = act.snap(e_reg, min_val=0, max_val=EXPERTS - 1)
                            act.wait_ge(h_done, s + 3)
                            act.wait_ge(y_done, s + 1)
                            for f in range(FC):
                                a = act.activation(hid[:, b, f, :], bank[2 + b][:, f * P:(f + 1) * P], ACT.Relu,
                                                   bias=b1T[:, bass.ds(e * FC + f, 1)])
                            a.then_inc(h_ready, 1)

                        with by_two(act, 0, STILES) as s0:
                            relu(s0, 0)
                            relu(s0, 1)

                    @block.vector
                    def _(dve):
                        def move_in(s, b):
                            dve.wait_ge(in_turned, s + 3)
                            dve.wait_ge(h_done, s + 1)
                            dve.tensor_copy(inT[:, b, :], bank[b][:, 0:C]).then_inc(inT_ready, 1)

                        def move_out(s, b):
                            dve.wait_ge(y_done, s + 3)
                            if not (isinstance(s, int) and s < 2):
                                dve.wait_ge(y_out[b], 8 * (s - b))
                            dve.tensor_copy(res[:, b, :], bank[4 + b][:, 0:C]).then_inc(y_ready, 1)

                        move_in(0, 0)
                        move_in(1, 1)

                        def two(s):
                            move_out(s, 0)
                            move_in(s + 2, 0)
                            move_out(s + 1, 1)
                            move_in(s + 3, 1)

                        two(0)
                        with by_two(dve, 2, STILES - 2) as s:
                            two(s)
                        move_out(STILES - 2, 0)
                        move_out(STILES - 1, 1)

                    @block.gpsimd
                    def _(pool):
                        def store(s0, b):
                            pool.wait_ge(y_ready, s0 + b + 3)
                            pool.dma_start(slots_y[bass.ds((s0 + b) * P, P), :], res[:, b, :]).then_inc(y_out[b], 16)

                        with by_two(pool, 0, STILES) as s0:
                            store(s0, 0)
                            store(s0, 1)
                        for b in range(2):
                            pool.wait_ge(y_out[b], 8 * STILES)

            with ExitStack() as stage:
                def tmp(name, shape, dt=F32):
                    return stage.enter_context(nc.sbuf_tensor(name, shape, dt))

                y_idx = tmp("y_idx", [P, 2, 2], I32)
                y_got = big[:, 0:1024].rearrange("p (b q c) -> p b q c", b=2, q=2)
                wd = tmp("wd", [P, 2, EXPERTS])
                wdT = tmp("wdT", [EXPERTS, 2, P])
                ysum = big[:, 1024:1536].rearrange("p (b c) -> p b c", b=2)
                yrow = big[:, 1536:2048].rearrange("p (b c) -> p b c", b=2)
                idx_put = sem("idx_put")
                y_in = [[sem(f"y_in{b}{q}") for q in range(2)] for b in range(2)]
                cb_dve = sem("cb_dve")
                wd_ready, wd_turned, wdT_ready = sem("wd_ready"), sem("wd_turned"), sem("wdT_ready")
                b2_done = sem("b2_done")
                y_summed = sem("y_summed")
                var3_ready, sqrt3 = sem("var3_ready"), sem("sqrt3")
                o_ready = sem("o_ready")
                o_out = [sem(f"o_out{b}") for b in range(2)]
                with nc.Block() as block:
                    @block.scalar
                    def _(act):
                        slot_i = slot[:, :, :].rearrange("p t q -> p (t q)")

                        def step(t0, b):
                            t = t0 + b
                            if not starts(t0):
                                for q in range(2):
                                    act.wait_ge(y_in[b][q], 8 * t0)
                            act.copy(y_idx[:, b, :], slot_i[:, bass.ds(t * 2, 2)]).then_inc(idx_put, 1)
                            act.wait_ge(wd_turned, t + 1)
                            act.copy(wdT[:, b, :], bank[b][0:EXPERTS, 0:P]).then_inc(wdT_ready, 1)

                        each_tile(act, step)
                        act.wait_ge(var3_ready, 1)
                        act.activation(rstd[:, :], rstd[:, :], ACT.Sqrt).then_inc(sqrt3, 1)

                    @block.gpsimd
                    def _(pool):
                        def fetch(t0, b):
                            t = t0 + b
                            pool.wait_ge(idx_put, t + 1)
                            pool.wait_ge(y_summed, t + 1)
                            pool.sem_inc(pool_on, 1)
                            for q in range(2):
                                pool.indirect_dma_start(y_got[:, b, q, :], None, slots_y,
                                                        bass.IndirectOffsetOnAxis(ap=y_idx[:, b, q:q + 1], axis=0)).then_inc(y_in[b][q], 16)

                        each_tile(pool, fetch)

                    @block.tensor
                    def _(pe):
                        pe.sem_inc(y_summed, 2)
                        pe.sem_inc(b2_done, 2)

                        def bias(t0, b):
                            t = t0 + b
                            pe.wait_ge(wd_ready, t + 1)
                            pe.transpose(bank[b][0:EXPERTS, 0:P], wd[:, b, :], ident[:, :]).then_inc(wd_turned, 1)
                            pe.wait_ge(wdT_ready, t + 1)
                            pe.matmul(bank[2 + b][:, 0:C], wdT[:, b, :], b2_all[:, :], start=True, stop=True).then_inc(b2_done, 1)

                        each_tile(pe, bias)

                    @block.vector
                    def _(dve):
                        steps = Steps(dve, cb_dve)
                        share_f = share[:, :, :].rearrange("p q t -> p (q t)")
                        pick_f = pick[:, :, :, :].rearrange("p q t e -> p (q t e)")

                        def part(t0, b):
                            t = t0 + b
                            steps.at(6 * t0 + 2 * b)
                            dve.wait_ge(b2_done, t0 + 2)
                            s = [share_f[:, bass.ds(t + q * TILES, 1)] for q in range(2)]
                            o = [pick_f[:, bass.ds((t + q * TILES) * EXPERTS, EXPERTS)] for q in range(2)]
                            steps.done(dve.tensor_scalar(wd[:, b, :], o[0], s[0], None, ALU.mult))
                            steps.done(dve.scalar_tensor_tensor(wd[:, b, :], o[1], s[1], wd[:, b, :], ALU.mult, ALU.add))
                            dve.sem_inc(wd_ready, 1)

                        def whole(t0, b):
                            t = t0 + b
                            s = [share_f[:, bass.ds(t + q * TILES, 1)] for q in range(2)]
                            rows = work_f[:, bass.ds(t * EXT, C)]
                            steps.at(6 * t0 + (2 if is_last(t0) else 4 + 4 * b))
                            dve.wait_ge(b2_done, t + 3)
                            steps.done(dve.tensor_tensor(ysum[:, b, :], rows, bank[2 + b][:, 0:C], ALU.add))
                            for q in range(2):
                                dve.wait_ge(y_in[b][q], 8 * t0 + 16)
                                steps.done(dve.scalar_tensor_tensor(rows if q else ysum[:, b, :], y_got[:, b, q, :], s[q],
                                                                    ysum[:, b, :], ALU.mult, ALU.add))
                            dve.sem_inc(y_summed, 1)
                            steps.done(dve.bn_stats(stats[:, bass.ds(t, 1), :].rearrange("p a c -> p (a c)"), rows))

                        def sums(t0, buffers):
                            for b in buffers:
                                part(t0, b)
                            for b in buffers:
                                whole(t0, b)

                        each_pair(dve, sums)
                        steps.at(6 * TILES)
                        layer_stats(dve, steps)
                        dve.sem_inc(var3_ready, 1)
                        dve.wait_ge(sqrt3, 1)
                        steps.done(dve.reciprocal(rstd[:, :], rstd[:, :]))
                        after = steps.base + steps.n

                        def final(t0, b):
                            t = t0 + b
                            steps.at(after + 3 * t)
                            if not starts(t0):
                                dve.wait_ge(o_out[b], 8 * t0)
                            steps.done(dve.tensor_scalar(yrow[:, b, :], work_f[:, bass.ds(t * EXT, C)], mean[:, bass.ds(t, 1)],
                                                         rstd[:, bass.ds(t, 1)], ALU.subtract, ALU.mult))
                            steps.done(dve.tensor_tensor(yrow[:, b, :], yrow[:, b, :], gamma_bc[:, :], ALU.mult))
                            steps.done(dve.tensor_tensor(yrow[:, b, :], yrow[:, b, :], beta_bc[:, :], ALU.add))
                            dve.tensor_tensor(yrow[:, b, :], yrow[:, b, :], acc_f[:, bass.ds(t * EXT, C)], ALU.add).then_inc(o_ready, 1)

                        each_tile(dve, final)

                    @block.sync
                    def _(sp):
                        def store(t0, b):
                            t = t0 + b
                            sp.wait_ge(o_ready, t + 1)
                            if is_last(t0):
                                sp.dma_start(out[t * P:N, :], yrow[0:LAST, b, :]).then_inc(o_out[b], 16)
                            else:
                                sp.dma_start(out[bass.ds(t * P, P), :], yrow[:, b, :]).then_inc(o_out[b], 16)

                        each_tile(sp, store)
                        sp.wait_ge(o_out[0], 16 * (TILES // 2 + 1))
                        sp.wait_ge(o_out[1], 16 * (TILES // 2))


_INS = ['x', 'src', 'dst', 'L0_gnn_W', 'L0_gnn_a_src', 'L0_gnn_a_dst', 'L0_mix_Wqkv', 'L0_mix_Wout', 'L0_mix_bout',
        'L0_ffn_gate_w', 'L0_ffn_gate_b', 'L0_ffn_w1', 'L0_ffn_b1', 'L0_ffn_w2', 'L0_ffn_b2', 'L0_ffn_gamma',
        'L0_ffn_beta']


def kernel(**inputs):
    import concourse.bacc as _bacc
    from concourse.bass_utils import run_bass_kernel_spmd as _run

    nc = _bacc.Bacc("TRN2", target_bir_lowering=False, num_devices=1)
    arrays, args = {}, []
    for name in _INS:
        a = np.ascontiguousarray(inputs[name])
        arrays[f"in_{name}"] = a
        args.append(nc.dram_tensor(f"in_{name}", a.shape, mybir.dt.from_np(a.dtype), kind="ExternalInput").ap())
    args.append(nc.dram_tensor("out_0", (N, C), F32, kind="ExternalOutput").ap())
    build(nc, *args)
    r = _run(nc, [arrays], core_ids=[0])
    return r.results[0]["out_0"]
```

```python
from contextlib import ExitStack, contextmanager

import numpy as np

import concourse.bass as bass
from concourse import mybir

P = 128
N, C = 6250, 256
HEADS, HD = 8, 32
MH, MD = 8, 64
INNER = MH * MD
NE = 106250
EXPERTS, FF, TOPK = 16, 512, 2
EPS = 1e-5

TILES = -(-N // P)
LAST = N - (TILES - 1) * P
ETILES = -(-NE // P)
ELAST = NE - (ETILES - 1) * P
UNROLL = 16
ROUNDS = -(-(ETILES + TILES - 1) // UNROLL)
PAIRS = ROUNDS * UNROLL
PCH = -(-PAIRS // P)
ECH = -(-ETILES // P)
NO_NODE = 1 << 20
EXT = C + 2 * HEADS
ROW = C + HEADS
STILES = (N * TOPK + EXPERTS * (P - 1)) // P
STILES += -(STILES - 2) % 8
FC = FF // P
G = 7
GROUPS = TILES // G
assert GROUPS * G == TILES and (TILES - 1) % 4 == 0 and STILES % 4 == 2
REGION = (TILES + 1) * P
NULL_ROW = EXPERTS * REGION
SLOTS = NULL_ROW + P
XROW = C + 1
F32, I32, U32 = mybir.dt.float32, mybir.dt.int32, mybir.dt.uint32
ALU = mybir.AluOpType
ACT = mybir.ActivationFunctionType
X = mybir.AxisListType.X


class Steps:

    def __init__(self, engine, sem):
        self.engine, self.sem, self.n, self.base = engine, sem, 0, 0

    def done(self, instruction):
        self.go(instruction)
        self.engine.wait_ge(self.sem, self.base + self.n)

    def at(self, base):
        self.base, self.n = base, 0

    def go(self, instruction):
        self.n += 1
        instruction.then_inc(self.sem, 1)


@contextmanager
def by_two(engine, start, end):
    with engine.Fori(start // 2, end // 2) as half:
        yield half * 2


def each_pair(engine, body):
    body(0, (0, 1))
    with by_two(engine, 2, TILES - 1) as t0:
        body(t0, (0, 1))
    body(TILES - 1, (0,))


def each_tile(engine, body):
    def both(t0, buffers):
        for b in buffers:
            body(t0, b)

    each_pair(engine, both)


def by_four(engine, body):
    for m in range(4):
        body(0, m)
    with engine.Fori(1, TILES // 4) as h:
        for m in range(4):
            body(h * 4, m)
    body(TILES - 1, 0)


def is_last(t0):
    return isinstance(t0, int) and t0 == TILES - 1


def is_group_last(g):
    return isinstance(g, int) and g == GROUPS - 1


def starts(t0):
    return isinstance(t0, int) and t0 == 0


def spread(ap, n):
    return ap.unsqueeze(2).to_broadcast([ap.shape[0], ap.shape[1], n])


def over(ap, n):
    return ap.unsqueeze(1).to_broadcast([ap.shape[0], n, ap.shape[1]])


def build(nc, x, src, dst, gnn_W, a_src, a_dst, Wqkv, Wout, bout, gate_w, gate_b, w1, b1, w2, b2,
          gamma, beta, out):
    ctx = ExitStack()
    with ctx:
        def sb(name, shape, dt=F32):
            return ctx.enter_context(nc.sbuf_tensor(name, shape, dt))

        def sem(name):
            return ctx.enter_context(nc.semaphore(name))

        def dram(name, shape, dt=F32):
            return nc.dram_tensor(name, shape, dt).ap()

        src_rows = dram("src_rows", (ETILES, P), I32)
        dst_rows = dram("dst_rows", (ETILES, P), I32)
        pair_acc_d = dram("pair_acc_d", (PCH * P,), I32)
        xnT_d = dram("xnT_d", (TILES, P, C))
        xb_d = dram("xb_d", (TILES * P, C))
        table = dram("table", (TILES * P, ROW))
        slots_x = dram("slots_x", (SLOTS, XROW))
        moe_d = dram("moe_d", (2 * TILES * P, C))

        bank = [ctx.enter_context(nc.psum_tensor(f"bank{i}", [P, 512], F32)) for i in range(8)]

        dve_on = sem("dve_on")
        pool_on = sem("pool_on")

        ident = sb("ident", [P, P])
        iota = sb("iota", [P, P])
        ones = sb("ones", [P, P])
        below = sb("below", [P, P])
        work = sb("work", [P, TILES, EXT])
        acc = sb("acc", [P, TILES, EXT])
        stats = sb("stats", [P, TILES, 6])
        mean = sb("mean", [P, TILES])
        rstd = sb("rstd", [P, TILES])
        small = sb("small", [P, TILES])
        wext = sb("wext", [P, 2, EXT])
        wkvT = sb("wkvT", [P, 2, 2 * INNER])
        wq = sb("wq", [P, 4, C])
        woutT = sb("woutT", [P, 4, C])
        mixG = sb("mixG", [P, 2, C])
        bout_bc = sb("bout_bc", [P, C])
        src_cols = sb("src_cols", [P, PCH * P], I32)
        dst_cols = sb("dst_cols", [P, PCH * P + 2])
        pair_acc = sb("pair_acc", [1, PCH * P], I32)
        big = sb("big", [P, 8192])

        def flat(t):
            return t[:, :, :].rearrange("p t c -> p (t c)")

        work_f, acc_f = flat(work), flat(acc)

        def layer_stats(dve, steps, tiles=slice(0, TILES)):
            me, mo = stats[:, tiles, 1], stats[:, tiles, 4]
            mean_, rstd_, small_ = mean[:, tiles], rstd[:, tiles], small[:, tiles]
            steps.done(dve.tensor_tensor(mean_, me, mo, ALU.subtract))
            steps.done(dve.tensor_tensor(small_, mean_, mean_, ALU.mult))
            steps.done(dve.tensor_tensor(rstd_, stats[:, tiles, 2], stats[:, tiles, 5], ALU.add))
            steps.done(dve.tensor_scalar(rstd_, rstd_, 1.0 / C, EPS, ALU.mult, ALU.add))
            steps.done(dve.scalar_tensor_tensor(rstd_, small_, 0.25, rstd_, ALU.mult, ALU.add))
            steps.done(dve.tensor_tensor(mean_, me, mo, ALU.add))
            steps.done(dve.tensor_scalar(mean_, mean_, 0.5, None, ALU.mult))

        kv_raw = big[:, 0:2048].rearrange("p (r c) -> p r c", c=C)
        wout_raw = big[:, 2048:3072].rearrange("p (r c) -> p r c", c=INNER)
        a_bc = big[:, 3072:3584].rearrange("p (a c) -> p a c", a=2)
        prod = big[:, 3584:3840]
        hmean = big[:, 3840:3872].rearrange("p (c g) -> p c g", c=2)
        dst_g = sb("dst_g", [P, PCH, P], I32)
        src_g = sb("src_g", [P, PCH, P], I32)
        dst_f = big[:, 4096:4096 + PCH * P].rearrange("p (c e) -> p c e", e=P)
        src_f = big[:, 6144:6144 + PCH * P].rearrange("p (c e) -> p c e", e=P)
        jbase = sb("jbase", [P, PCH])
        tki = sb("tki", [P, PCH], I32)
        edges_got = sem("edges_got")
        x_in, last_zero, stated = sem("x_in"), sem("last_zero"), sem("stated")
        XCH = (TILES - 1) // 4
        with ExitStack() as stage:
            def tmp(name, shape, dt=F32):
                return stage.enter_context(nc.sbuf_tensor(name, shape, dt))

            last_rows = tmp("last_rows", [1, 2, P], I32)
            ends = tmp("ends", [P, ECH, P], I32)
            endsf = tmp("endsf", [P, ECH, 2])
            node0 = tmp("node0", [P, TILES])
            jrow = tmp("jrow", [P, TILES])
            kcol = tmp("kcol", [P, PCH])
            cmp = tmp("cmp", [P, TILES * ECH])
            cnt = tmp("cnt", [P, 2 * TILES])
            bounds = tmp("bounds", [P, 2 * TILES])
            npair = tmp("npair", [P, TILES])
            kend = tmp("kend", [P, TILES])
            toff = tmp("toff", [P, TILES])
            jk = tmp("jk", [P, PCH])
            tk = tmp("tk", [P, PCH])
            joff = tmp("joff", [P, PCH], I32)
            w_in = sem("w_in")
            bc_in = sem("bc_in")
            copied = sem("copied")
            tail_in = sem("tail_in")
            tail_out = sem("tail_out")
            ends_in = sem("ends_in")
            padded = sem("padded")
            consts = sem("consts")
            su_pe = sem("su_pe")
            su_act = sem("su_act")
            su_dve = sem("su_dve")
            counted = sem("counted")
            counts_sum = sem("counts_sum")
            tk_ready = sem("tk_ready")
            joff_out, joff_in = sem("joff_out"), sem("joff_in")
            su_pool = sem("su_pool")
            with nc.Block() as block:
                @block.sync
                def _(sp):
                    full = (ETILES - 1) * P
                    sp.wait_ge(padded, 2)
                    for q, (s, rows) in enumerate(((src, src_rows), (dst, dst_rows))):
                        sp.dma_start(last_rows[0:1, q, 0:ELAST],
                                     s[full:NE].rearrange("(a b) -> a b", a=1)).then_inc(tail_in, 16)
                        sp.dma_start(rows[0:ETILES - 1, :],
                                     s[0:full].rearrange("(a b) -> a b", b=P)).then_inc(copied, 16)
                    sp.wait_ge(tail_in, 32)
                    for q, rows in enumerate((src_rows, dst_rows)):
                        sp.dma_start(rows[ETILES - 1:ETILES, :], last_rows[0:1, q, :]).then_inc(tail_out, 16)
                    sp.wait_ge(copied, 32)
                    sp.wait_ge(tail_out, 32)
                    whole = ETILES // P
                    sp.dma_start(ends[:, 0:whole, :],
                                 dst_rows[0:whole * P, :].rearrange("(c p) e -> p c e", p=P)).then_inc(ends_in, 16)
                    sp.dma_start(ends[0:ETILES - whole * P, whole, :],
                                 dst_rows[whole * P:ETILES, :]).then_inc(ends_in, 16)
                    for q in range(4):
                        a, z = q * XCH, (q + 1) * XCH
                        sp.dma_start(work[:, a:z, 0:C], x[a * P:z * P, :].rearrange("(t p) c -> p t c", p=P)).then_inc(x_in, 16)
                    sp.wait_ge(last_zero, 1)
                    sp.dma_start(work[0:LAST, TILES - 1, 0:C], x[(TILES - 1) * P:N, :]).then_inc(x_in, 16)
                    sp.wait_ge(tk_ready, 2)
                    with nc.allow_non_contiguous_dma(reason="896 numbers"):
                        sp.dma_start(pair_acc_d.rearrange("(c p) -> p c", p=P), joff[:, :]).then_inc(joff_out, 16)
                    sp.wait_ge(joff_out, 16)
                    sp.dma_start(pair_acc[0:1, :], pair_acc_d.rearrange("(a b) -> a b", a=1)).then_inc(joff_in, 16)
                    sp.wait_ge(joff_in, 16)

                @block.scalar
                def _(act):
                    act.dma_start(wext[:, :, 0:C], gnn_W.rearrange("(c p) n -> p c n", p=P)).then_inc(w_in, 16)
                    act.dma_start(kv_raw, Wqkv[INNER:3 * INNER, :].rearrange("(r p) c -> p r c", p=P)).then_inc(w_in, 16)
                    act.dma_start(wout_raw, Wout.rearrange("(r p) c -> p r c", p=P)).then_inc(w_in, 16)
                    act.dma_start(wq[:, :, :], Wqkv[0:INNER, :].rearrange("(r p) c -> p r c", p=P)).then_inc(w_in, 16)
                    act.dma_start(bout_bc[:, :], bout.partition_broadcast(P)).then_inc(w_in, 16)
                    for q, a in enumerate((a_src, a_dst)):
                        act.dma_start(a_bc[:, q, :], a.rearrange("h d -> (h d)").partition_broadcast(P)).then_inc(bc_in, 16)
                    for f in range(6):
                        act.wait_ge(su_pe, f + 1)
                        to = wkvT[:, f // 2, (f % 2) * 512:(f % 2 + 1) * 512] if f < 4 else \
                            woutT[:, 2 * (f - 4):2 * (f - 3), :].rearrange("p a c -> p (a c)")
                        act.copy(to, bank[f][:, :]).then_inc(su_act, 1)

                @block.gpsimd
                def _(pool):
                    steps = Steps(pool, su_pool)
                    steps.done(pool.memset(last_rows[:, 0, :], 0))
                    steps.done(pool.memset(last_rows[:, 1, :], NO_NODE))
                    pool.sem_inc(padded, 1)
                    pool.memset(work[:, TILES - 1, :], 0.0).then_inc(last_zero, 1)
                    steps.done(pool.memset(ones[:, :], 1.0))
                    steps.done(pool.memset(ident[:, :], 0.0))
                    steps.done(pool.affine_select(out=ident[:, :], in_=ident[:, :], compare_op=ALU.not_equal,
                                                  fill=1.0, base=0, pattern=[[-1, P]], channel_multiplier=1))
                    steps.done(pool.affine_select(out=below[:, :], in_=ones[:, :], compare_op=ALU.is_gt,
                                                  fill=0.0, base=0, pattern=[[1, P]], channel_multiplier=-1))
                    kw = dict(allow_small_or_imprecise_dtypes=True)
                    steps.done(pool.iota(iota[:, :], pattern=[[1, P]], base=0, channel_multiplier=0, **kw))
                    steps.done(pool.iota(node0[:, :], pattern=[[P, TILES]], base=0, channel_multiplier=0, **kw))
                    steps.done(pool.iota(jrow[:, :], pattern=[[1, TILES]], base=0, channel_multiplier=0, **kw))
                    steps.done(pool.iota(kcol[:, :], pattern=[[P, PCH]], base=0, channel_multiplier=1, **kw))
                    pool.sem_inc(consts, 1)
                    pool.memset(acc_f, 0.0).then_inc(su_pool, 1)
                    pool.wait_ge(tk_ready, 1)
                    for c in range(PCH):
                        at = bass.IndirectOffsetOnAxis(ap=tki[:, c:c + 1], axis=0)
                        pool.indirect_dma_start(dst_g[:, c, :], None, dst_rows, at).then_inc(edges_got, 16)
                        pool.indirect_dma_start(src_g[:, c, :], None, src_rows, at).then_inc(edges_got, 16)

                @block.tensor
                def _(pe):
                    pe.wait_ge(w_in, 80)
                    pe.wait_ge(consts, 1)
                    for f in range(4):
                        for q in range(4):
                            t = pe.transpose(bank[f][:, q * P:(q + 1) * P],
                                             kv_raw[:, (f % 2) * 4 + q, (f // 2) * P:(f // 2 + 1) * P], ident[:, :])
                        t.then_inc(su_pe, 1)
                    for f in range(2):
                        for q in range(2):
                            for c in range(2):
                                t = pe.transpose(bank[4 + f][:, q * C + c * P:q * C + (c + 1) * P],
                                                 wout_raw[:, c, (2 * f + q) * P:(2 * f + q + 1) * P], ident[:, :])
                        t.then_inc(su_pe, 1)
                    pe.wait_ge(counted, 1)
                    pe.matmul(bank[6][:, 0:2 * TILES], ones[:, :], cnt[:, :], start=True, stop=True).then_inc(counts_sum, 1)

                @block.vector
                def _(dve):
                    steps = Steps(dve, su_dve)
                    steps.done(dve.memset(ends[:, ECH - 1, :], NO_NODE))
                    dve.sem_inc(padded, 1)
                    dve.wait_ge(consts, 1)
                    dve.wait_ge(ends_in, 32)
                    for q in range(2):
                        steps.done(dve.tensor_copy(endsf[:, :, q], ends[:, :, q * (P - 1)]))
                    cmp_t = cmp[:, 0:TILES * ECH].rearrange("p (j c) -> p j c", c=ECH)
                    steps.done(dve.tensor_tensor(cmp_t, over(endsf[:, :, 1], TILES), spread(node0[:, :], ECH), ALU.is_lt))
                    steps.done(dve.tensor_reduce(cnt[:, 0:TILES], cmp_t, X, ALU.add))
                    steps.done(dve.tensor_scalar(node0[:, :], node0[:, :], float(P), None, ALU.add))
                    steps.done(dve.tensor_tensor(cmp_t, over(endsf[:, :, 0], TILES), spread(node0[:, :], ECH), ALU.is_lt))
                    dve.tensor_reduce(cnt[:, TILES:2 * TILES], cmp_t, X, ALU.add).then_inc(counted, 1)
                    dve.wait_ge(counts_sum, 1)
                    steps.done(dve.tensor_copy(bounds[:, :], bank[6][:, 0:2 * TILES]))
                    ts, te = bounds[:, 0:TILES], bounds[:, TILES:2 * TILES]
                    steps.done(dve.scalar_tensor_tensor(te, ts, 1.0, te, ALU.add, ALU.max))
                    steps.done(dve.tensor_tensor(npair[:, :], te, ts, ALU.subtract))
                    steps.done(dve.tensor_tensor_scan(kend[:, :], ones[:, 0:TILES], npair[:, :], 0.0, ALU.mult, ALU.add))
                    steps.done(dve.tensor_tensor(toff[:, :], te, kend[:, :], ALU.subtract))
                    cmp_k = cmp[:, 0:PCH * TILES].rearrange("p (c j) -> p c j", j=TILES)
                    steps.done(dve.tensor_tensor(cmp_k, over(kend[:, :], PCH), spread(kcol[:, :], TILES), ALU.is_le))
                    steps.done(dve.tensor_reduce(jk[:, :], cmp_k, X, ALU.add))
                    steps.done(dve.tensor_tensor(cmp_k, over(jrow[:, :], PCH), spread(jk[:, :], TILES), ALU.is_equal))
                    steps.done(dve.tensor_tensor(cmp_k, cmp_k, over(toff[:, :], PCH), ALU.mult))
                    steps.done(dve.tensor_reduce(tk[:, :], cmp_k, X, ALU.add))
                    steps.done(dve.tensor_tensor(tk[:, :], tk[:, :], kcol[:, :], ALU.add))
                    steps.done(dve.tensor_scalar(tki[:, :], tk[:, :], float(ETILES - 1), None, ALU.min))
                    dve.sem_inc(tk_ready, 1)
                    steps.done(dve.tensor_scalar(joff[:, :], jk[:, :], float(TILES - 1), float(EXT), ALU.min, ALU.mult))
                    dve.sem_inc(tk_ready, 1)
                    steps.done(dve.tensor_scalar(jbase[:, :], jk[:, :], -float(P), None, ALU.mult))
                    dve.wait_ge(w_in, 80)
                    dve.wait_ge(bc_in, 32)
                    for c in range(2):
                        for q in range(2):
                            steps.done(dve.tensor_tensor(prod, wext[:, c, 0:C], a_bc[:, q, :], ALU.mult))
                            steps.done(dve.tensor_reduce(wext[:, c, C + HEADS * q:C + HEADS * (q + 1)],
                                                         prod.rearrange("p (h d) -> p h d", d=HD), X, ALU.add))
                    dve.wait_ge(su_act, 4)
                    for c in range(2):
                        grouped = wkvT[:, c, :].rearrange("p (g d) -> p g d", d=MD)
                        steps.done(dve.tensor_reduce(hmean[:, c, :], grouped, X, ALU.add))
                        steps.done(dve.tensor_scalar(hmean[:, c, :], hmean[:, c, :], 1.0 / MD, None, ALU.mult))
                        steps.done(dve.tensor_tensor(grouped, grouped, spread(hmean[:, c, :], MD), ALU.subtract))
                    dve.wait_ge(x_in, 80)
                    with dve.Fori(0, GROUPS) as g:
                        for i in range(G):
                            t = g * G + i
                            dve.bn_stats(stats[:, bass.ds(t, 1), :].rearrange("p a c -> p (a c)"),
                                         work_f[:, bass.ds(t * EXT, C)]).then_inc(stated, 1)
                    dve.wait_ge(stated, TILES)

        with ExitStack() as stage:
            def tmp(name, shape, dt=F32):
                return stage.enter_context(nc.sbuf_tensor(name, shape, dt))

            xn = tmp("xn", [P, 2, C])
            xnT = big[:, 0:4 * C].rearrange("p (m c) -> p m c", m=4)
            xb = big[:, 4 * C:8 * C].rearrange("p (m c) -> p m c", m=4)
            cols_f = sem("cols_f")
            cols_t = sem("cols_t")
            cl_dve = sem("cl_dve")
            xb_ready = sem("xb_ready")
            sqrted = sem("sqrted")
            var_ready = sem("var_ready")
            pj_dve = sem("pj_dve")
            xn_ready = sem("xn_ready")
            xn_turned = sem("xn_turned")
            xnT_ready = sem("xnT_ready")
            kept = [sem(f"kept{m}") for m in range(4)]
            proj_done = sem("proj_done")
            proj_kept = sem("proj_kept")
            with nc.Block() as block:
                @block.sync
                def _(sp):
                    def keep(t0, m):
                        t = t0 + m
                        sp.wait_ge(xb_ready, t + 1)
                        sp.dma_start(xb_d[bass.ds(t * P, P), :], xb[:, m, :]).then_inc(kept[m], 16)
                        sp.wait_ge(xnT_ready, t + 1)
                        sp.dma_start(xnT_d[bass.ds(t, 1), :, :].rearrange("a p c -> p (a c)"),
                                     xnT[:, m, :]).then_inc(kept[m], 16)

                    by_four(sp, keep)
                    for m in range(4):
                        sp.wait_ge(kept[m], 32 * (TILES // 4 + (m == 0)))

                @block.gpsimd
                def _(pool):
                    def add_bout(t0, m):
                        t = t0 + m
                        if not starts(t0):
                            pool.wait_ge(kept[m], 8 * t0)
                        pool.tensor_tensor(xb[:, m, :], work_f[:, bass.ds(t * EXT, C)], bout_bc[:, :], ALU.add).then_inc(xb_ready, 1)

                    by_four(pool, add_bout)

                @block.vector
                def _(dve):
                    steps = Steps(dve, pj_dve)
                    layer_stats(dve, steps)
                    dve.sem_inc(var_ready, 1)
                    dve.wait_ge(sqrted, 1)
                    steps.done(dve.reciprocal(rstd[:, :], rstd[:, :]))
                    dve.sem_inc(xn_turned, 2)

                    def norm(t0, b):
                        t = t0 + b
                        dve.wait_ge(xn_turned, t + 1)
                        dve.tensor_scalar(xn[:, b, :], work_f[:, bass.ds(t * EXT, C)], mean[:, bass.ds(t, 1)],
                                          rstd[:, bass.ds(t, 1)], ALU.subtract, ALU.mult).then_inc(xn_ready, 1)

                    each_tile(dve, norm)
                    steps = Steps(dve, cl_dve)
                    dve.wait_ge(edges_got, 32 * PCH)
                    for c in range(PCH):
                        steps.done(dve.tensor_scalar(dst_f[:, c, :], dst_g[:, c, :], jbase[:, c:c + 1], None, ALU.add))
                    steps.done(dve.tensor_copy(src_f[:, :, :], src_g[:, :, :]))
                    dve.sem_inc(cols_f, 1)
                    dve.wait_ge(cols_t, 2)
                    half = PCH * P - 512
                    steps.done(dve.tensor_copy(dst_cols[:, 0:512], bank[4][:, :]))
                    steps.done(dve.tensor_copy(dst_cols[:, 512:PCH * P], bank[5][:, 0:half]))
                    steps.done(dve.memset(dst_cols[:, PCH * P:PCH * P + 2], -1.0))
                    steps.done(dve.tensor_copy(src_cols[:, 0:512], bank[6][:, :]))
                    steps.done(dve.tensor_copy(src_cols[:, 512:PCH * P], bank[7][:, 0:half]))

                @block.tensor
                def _(pe):
                    pe.sem_inc(proj_kept, 2)

                    def turn(t, b):
                        pe.wait_ge(xn_ready, t + 1)
                        for c in range(2):
                            r = pe.transpose(bank[b][:, c * P:(c + 1) * P], xn[:, b, c * P:(c + 1) * P], ident[:, :])
                        r.then_inc(xn_turned, 1)

                    def step(t0, m):
                        t, b = t0 + m, m % 2
                        if not is_last(t0):
                            turn(t + 1, 1 - b)
                        pe.wait_ge(xnT_ready, t + 1)
                        pe.wait_ge(proj_kept, t + 1)
                        for c in range(2):
                            r = pe.matmul(bank[2 + b][:, 0:EXT], xnT[:, m, c * P:(c + 1) * P], wext[:, c, :],
                                          start=c == 0, stop=c == 1)
                        r.then_inc(proj_done, 1)

                    turn(0, 0)
                    by_four(pe, step)
                    pe.wait_ge(cols_f, 1)
                    for q, t_f in enumerate((dst_f, src_f)):
                        for c in range(PCH):
                            t = pe.transpose(bank[4 + 2 * q + c // 4][:, (c % 4) * P:(c % 4 + 1) * P], t_f[:, c, :], ident[:, :])
                        t.then_inc(cols_t, 1)

                @block.scalar
                def _(act):
                    act.wait_ge(var_ready, 1)
                    act.activation(rstd[:, :], rstd[:, :], ACT.Sqrt).then_inc(sqrted, 1)

                    def move_in(t, m):
                        act.wait_ge(xn_turned, t + 3)
                        if not (isinstance(t, int) and t < 4):
                            act.wait_ge(kept[m], 8 * (t - m))
                        act.copy(xnT[:, m, :], bank[m % 2][:, 0:C]).then_inc(xnT_ready, 1)

                    def step(t0, m):
                        t = t0 + m
                        if not is_last(t0):
                            move_in(t + 1, (m + 1) % 4)
                        act.wait_ge(proj_done, t + 1)
                        act.wait_ge(xb_ready, t + 1)
                        act.copy(work_f[:, bass.ds(t * EXT, EXT)], bank[2 + m % 2][:, 0:EXT]).then_inc(proj_kept, 1)

                    move_in(0, 0)
                    by_four(act, step)

        with ExitStack() as stage:
            def tmp(name, shape, dt=F32):
                return stage.enter_context(nc.sbuf_tensor(name, shape, dt))

            ext2 = tmp("ext2", [P, 2 * HEADS])
            ext1 = tmp("ext1", [2 * HEADS, 1])
            diag = tmp("diag", [2 * HEADS, 2 * HEADS])
            amax = tmp("amax", [P, 2 * HEADS])
            wexp = tmp("wexp", [P, TILES, HEADS])
            wg_dve = sem("wg_dve")
            ext_ready, ext_turned = sem("ext_ready"), sem("ext_turned")
            diag_ready, amax_ready = sem("diag_ready"), sem("amax_ready")
            wexp_in, wexp_out = sem("wexp_in"), sem("wexp_out")
            rows_ready = sem("rows_ready")
            alpha_kept = sem("alpha_kept")
            table_out = sem("table_out")
            pool_rows = sem("pool_rows")
            FOR_POOL = 2
            wexp_f = wexp[:, :, :].rearrange("p t h -> p (t h)")

            def weigh_rows(engine, places, ready):
                with engine.Fori(0, GROUPS) as g:
                    for i in places:
                        t = g * G + i
                        rows = work_f[:, bass.ds(t * EXT, C)].rearrange("p (h d) -> p h d", d=HD)
                        engine.tensor_tensor(rows, rows, spread(wexp_f[:, bass.ds(t * HEADS, HEADS)], HD),
                                             ALU.mult).then_inc(ready, 1)

            with nc.Block() as block:
                @block.gpsimd
                def _(pool):
                    pool.wait_ge(wexp_out, 1)
                    pool.tensor_copy(work[:, :, C:C + HEADS], wexp[:, :, :]).then_inc(alpha_kept, 1)
                    weigh_rows(pool, range(FOR_POOL), pool_rows)

                @block.vector
                def _(dve):
                    steps = Steps(dve, wg_dve)
                    alpha = work[:, :, C:C + HEADS]
                    steps.done(dve.tensor_reduce(ext2[:, 0:HEADS], alpha.rearrange("p t h -> p h t"), X, ALU.max))
                    steps.done(dve.tensor_scalar(wexp[:, :, :], alpha, -1.0, None, ALU.mult))
                    dve.tensor_reduce(ext2[:, HEADS:2 * HEADS], wexp[:, :, :].rearrange("p t h -> p h t"), X,
                                      ALU.max).then_inc(ext_ready, 1)
                    dve.wait_ge(ext_turned, 1)
                    steps.done(dve.tensor_reduce(ext1[:, :], bank[0][0:2 * HEADS, 0:P], X, ALU.max))
                    dve.tensor_scalar(diag[:, :], ident[0:2 * HEADS, 0:2 * HEADS], ext1[:, 0:1], None,
                                      ALU.mult).then_inc(diag_ready, 1)
                    dve.wait_ge(amax_ready, 1)
                    steps.done(dve.tensor_copy(amax[:, :], bank[1][:, 0:2 * HEADS]))
                    dve.tensor_tensor(wexp[:, :, :], alpha, over(amax[:, 0:HEADS], TILES), ALU.subtract).then_inc(wexp_in, 1)
                    dve.wait_ge(wexp_out, 1)
                    weigh_rows(dve, range(FOR_POOL, G), rows_ready)

                @block.tensor
                def _(pe):
                    pe.wait_ge(ext_ready, 1)
                    pe.transpose(bank[0][0:2 * HEADS, 0:P], ext2[:, :], ident[:, :]).then_inc(ext_turned, 1)
                    pe.wait_ge(diag_ready, 1)
                    pe.matmul(bank[1][:, 0:2 * HEADS], ones[0:2 * HEADS, :], diag[:, :], start=True,
                              stop=True).then_inc(amax_ready, 1)

                @block.scalar
                def _(act):
                    act.wait_ge(wexp_in, 1)
                    act.activation(wexp[:, :, :], wexp[:, :, :], ACT.Exp).then_inc(wexp_out, 1)

                @block.sync
                def _(sp):
                    tab = table.rearrange("(t p) c -> p t c", p=P)
                    sp.wait_ge(alpha_kept, 1)
                    for g in range(GROUPS):
                        sp.wait_ge(rows_ready, (g + 1) * (G - FOR_POOL))
                        sp.wait_ge(pool_rows, (g + 1) * FOR_POOL)
                        sp.dma_start(tab[:, g * G:(g + 1) * G, :], work[:, g * G:(g + 1) * G, 0:ROW]).then_inc(table_out, 16)
                    sp.wait_ge(table_out, 16 * GROUPS)

        got = big[:, 0:UNROLL * ROW].rearrange("p (s c) -> p s c", c=ROW)
        with ExitStack() as stage:
            def tmp(name, shape, dt=F32):
                return stage.enter_context(nc.sbuf_tensor(name, shape, dt))

            HALF = UNROLL // 2
            idx = tmp("idx", [P, UNROLL], I32)
            onehot = tmp("onehot", [P, 4, P])
            kv_x = tmp("kv_x", [P, C])
            squares = tmp("squares", [P, 2 * INNER])
            kv_var = tmp("kv_var", [P, 2 * MH])
            kv_r = tmp("kv_r", [P, 2 * MH])
            k_scale = tmp("k_scale", [P, MH])
            k_n = tmp("k_n", [P, INNER])
            v_n = tmp("v_n", [P, INNER])
            zeros = tmp("zeros", [P, 512])
            dotsS = tmp("dotsS", [P, 4, P])
            g1T = tmp("g1T", [P, 4, C])
            idx_ready = sem("idx_ready")
            row_got = [sem(f"row_got{s}") for s in range(UNROLL)]
            rows_used = sem("rows_used")
            onehot_ready = sem("onehot_ready")
            summed = sem("summed")
            kvx_in = sem("kvx_in")
            kv_done = sem("kv_done")
            squared, v_moved = sem("squared"), sem("v_moved")
            var_in, var_out = sem("var_in"), sem("var_out")
            k_ready = sem("k_ready")
            dots_done = sem("dots_done")
            eg_dve = sem("eg_dve")
            zeros_set = sem("zeros_set")
            dS_ready, g1_done, g1_moved, g_done, g_moved = (sem(n) for n in (
                "dS_ready", "g1_done", "g1_moved", "g_done", "g_moved"))
            KB, VB, DB = bank[4], bank[5], bank[6]
            with nc.Block() as block:
                @block.gpsimd
                def _(pool):
                    def gathers(r):
                        for s in range(UNROLL):
                            if s % HALF == 0:
                                pool.wait_ge(idx_ready, 2 * r + 1 + s // HALF)
                            pool.wait_ge(rows_used, r * UNROLL + s + 1)
                            pool.sem_inc(pool_on, 1)
                            pool.indirect_dma_start(got[:, s, :], None, table,
                                                    bass.IndirectOffsetOnAxis(ap=idx[:, s:s + 1], axis=0)
                                                    ).then_inc(row_got[s], 16)

                    with pool.Fori(0, ROUNDS) as r:
                        gathers(r)

                @block.scalar
                def _(act):
                    def indices(r):
                        for h in range(2):
                            act.wait_ge(rows_used, r * UNROLL + (h + 1) * HALF)
                            act.copy(idx[:, h * HALF:(h + 1) * HALF],
                                     src_cols[:, bass.ds(r * UNROLL + h * HALF, HALF)]).then_inc(idx_ready, 1)

                    def keys_values(r):
                        act.wait_ge(kv_done, r + 1)
                        act.activation(squares[:, 0:INNER], KB[:, :], ACT.Square)
                        act.activation(squares[:, INNER:2 * INNER], VB[:, :], ACT.Square).then_inc(squared, 1)
                        act.wait_ge(dots_done, r + 1)
                        act.copy(v_n[:, :], VB[:, :]).then_inc(v_moved, 1)
                        act.wait_ge(var_in, r + 1)
                        act.activation(kv_r[:, :], kv_var[:, :], ACT.Sqrt).then_inc(var_out, 1)

                    with act.Fori(0, TILES) as r:
                        indices(r)
                        keys_values(r)
                    with act.Fori(TILES, ROUNDS) as r:
                        indices(r)

                @block.sync
                def _(sp):
                    def load(r):
                        sp.dma_start(kv_x[:, :], xnT_d[bass.ds(r, 1), :, :].rearrange("a p c -> p (a c)")).then_inc(kvx_in, 16)

                    load(0)
                    with sp.Fori(1, TILES) as r:
                        sp.wait_ge(kv_done, r)
                        load(r)

                @block.tensor
                def _(pe):
                    pe.sem_inc(rows_used, UNROLL)
                    pe.sem_inc(summed, 4)
                    pe.sem_inc(k_ready, 1)
                    pe.wait_ge(zeros_set, 1)
                    pe.matmul(DB[:, :], zeros[:, 0:P], zeros[:, :], start=True, stop=False, skip_group_check=True).then_inc(dots_done, 1)

                    def sum_rows(r, s):
                        k = r * UNROLL + s
                        pe.wait_ge(onehot_ready, k + 1)
                        pe.wait_ge(row_got[s], r * 16 + 16)
                        pe.wait_ge(summed, k + 1)
                        pe.matmul(bank[s % 4][:, 0:ROW], onehot[:, s % 4, :], got[:, s, :], start=True,
                                  stop=True).then_inc(rows_used, 1)

                    def project_kv(r):
                        pe.wait_ge(kvx_in, r * 16 + 16)
                        pe.wait_ge(k_ready, r + 1)
                        for o, b in ((0, KB), (INNER, VB)):
                            for c in range(2):
                                m = pe.matmul(b[:, :], kv_x[:, c * P:(c + 1) * P], wkvT[:, c, o:o + INNER],
                                              start=c == 0, stop=c == 1)
                        m.then_inc(kv_done, 1)

                    def dots(r):
                        pe.wait_ge(k_ready, r + 2)
                        pe.wait_ge(v_moved, r + 1)
                        for q in range(4):
                            m = pe.matmul(DB[:, q * P:(q + 1) * P], k_n[:, q * P:(q + 1) * P], v_n[:, q * P:(q + 1) * P],
                                          start=False, stop=False, skip_group_check=True)
                        m.then_inc(dots_done, 1)

                    with pe.Fori(0, TILES) as r:
                        project_kv(r)
                        for s in range(UNROLL):
                            sum_rows(r, s)
                        dots(r)
                    pe.matmul(DB[:, :], zeros[:, 0:P], zeros[:, :], start=False, stop=True, skip_group_check=True).then_inc(dots_done, 1)
                    pe.wait_ge(dS_ready, 1)
                    for q in range(4):
                        m = pe.matmul([KB, VB][q // 2][:, (q % 2) * C:(q % 2 + 1) * C], dotsS[:, q, :], wq[:, q, :],
                                      start=True, stop=True)
                    m.then_inc(g1_done, 1)
                    pe.wait_ge(g1_moved, 1)
                    for c in range(2):
                        for q in range(4):
                            m = pe.matmul(bank[7][:, c * C:(c + 1) * C], g1T[:, q, c * P:(c + 1) * P], woutT[:, q, :],
                                          start=q == 0, stop=q == 3)
                    m.then_inc(g_done, 1)
                    with pe.Fori(TILES, ROUNDS) as r:
                        for s in range(UNROLL):
                            sum_rows(r, s)

                @block.vector
                def _(dve):
                    dve.memset(zeros[:, :], 0.0).then_inc(zeros_set, 1)
                    dve.memset(dotsS[:, :, :], 0.0).then_inc(zeros_set, 1)
                    regs = [dve.alloc_register(f"at{s}") for s in range(UNROLL)]

                    def targets(k, s):
                        dve.wait_ge(rows_used, k + UNROLL - 3)
                        dve.tensor_scalar(onehot[:, s % 4, :], iota[:, :], dst_cols[:, bass.ds(k, 1)], None,
                                          ALU.is_equal).then_inc(onehot_ready, 1)

                    def add(k, s):
                        at = dve.snap(regs[s], min_val=0, max_val=(TILES - 1) * EXT)
                        to = acc_f[:, bass.ds(at, ROW)]
                        dve.wait_ge(rows_used, k + UNROLL + 1)
                        dve.wait_ge(summed, k + 4)
                        dve.tensor_tensor(to, to, bank[s % 4][:, 0:ROW], ALU.add).then_inc(summed, 1)

                    steps = Steps(dve, eg_dve)

                    def kv_var_of(r):
                        dve.wait_ge(squared, r + 1)
                        steps.done(dve.tensor_reduce(kv_var[:, :], squares[:, :].rearrange("p (g d) -> p g d", d=MD), X, ALU.add))
                        dve.tensor_scalar(kv_var[:, :], kv_var[:, :], 1.0 / MD, EPS, ALU.mult, ALU.add).then_inc(var_in, 1)

                    def scale_k(r):
                        dve.wait_ge(var_out, r + 1)
                        steps.done(dve.reciprocal(kv_r[:, :], kv_r[:, :]))
                        steps.done(dve.tensor_tensor(k_scale[:, :], kv_r[:, 0:MH], kv_r[:, MH:2 * MH], ALU.mult))
                        dve.wait_ge(v_moved, r + 1)
                        dve.tensor_tensor(k_n[:, :].rearrange("p (g d) -> p g d", d=MD),
                                          KB[:, :].rearrange("p (g d) -> p g d", d=MD), spread(k_scale[:, :], MD),
                                          ALU.mult).then_inc(k_ready, 1)

                    targets(0, 0)
                    targets(1, 1)

                    def round_(r, with_kv):
                        dve.load(regs, pair_acc[0:1, bass.ds(r * UNROLL, UNROLL)])
                        for s in range(UNROLL):
                            targets(r * UNROLL + s + 2, s + 2)
                            add(r * UNROLL + s, s)
                            if with_kv and s == UNROLL // 2:
                                kv_var_of(r)
                            if with_kv and s == UNROLL // 2 + 4:
                                scale_k(r)

                    with dve.Fori(0, TILES) as r:
                        steps.at(r * 3)
                        round_(r, True)
                    dve.wait_ge(dots_done, TILES + 2)
                    dve.wait_ge(zeros_set, 2)
                    for q in range(4):
                        for h in range(2):
                            d = dve.tensor_scalar(dotsS[h * MD:(h + 1) * MD, q, h * MD:(h + 1) * MD],
                                                  DB[h * MD:(h + 1) * MD, q * P + h * MD:q * P + (h + 1) * MD],
                                                  1.0 / N, None, ALU.mult)
                    d.then_inc(dS_ready, 1)
                    dve.wait_ge(g1_done, 1)
                    for q, b in enumerate((KB, VB)):
                        d = dve.tensor_copy(g1T[:, 2 * q:2 * q + 2, :].rearrange("p a c -> p (a c)"), b[:, :])
                    d.then_inc(g1_moved, 1)
                    dve.wait_ge(g_done, 1)
                    dve.tensor_copy(mixG[:, :, :].rearrange("p a c -> p (a c)"), bank[7][:, :]).then_inc(g_moved, 1)
                    with dve.Fori(TILES, ROUNDS) as r:
                        round_(r, False)
                    dve.wait_ge(summed, PAIRS + 4)


        with ExitStack() as stage2:
            def keep_(name, shape, dt=F32):
                return stage2.enter_context(nc.sbuf_tensor(name, shape, dt))

            share = keep_("share", [P, 2, TILES])
            carry = keep_("carry", [P, EXPERTS])
            b1T = keep_("b1T", [P, EXPERTS * FC])
            gamma_bc = keep_("gamma_bc", [P, C])
            beta_bc = keep_("beta_bc", [P, C])
            with ExitStack() as stage:
                def tmp(name, shape, dt=F32):
                    return stage.enter_context(nc.sbuf_tensor(name, shape, dt))

                cut = [0]

                def part_of_big(n, pattern, **kw):
                    a, cut[0] = cut[0], cut[0] + n
                    return big[:, a:cut[0]].rearrange(pattern, **kw)

                x_t = part_of_big(G * C, "p (i c) -> p i c", i=G)
                xnT_t = part_of_big(G * C, "p (i c) -> p i c", i=G)
                stage_x = part_of_big(G * 2 * XROW, "p (i q c) -> p i q c", i=G, q=2)
                gate = tmp("gate", [P, 2, EXPERTS])
                gate_b_bc = tmp("gate_b_bc", [P, EXPERTS])
                b1_raw = tmp("b1_raw", [EXPERTS * FC, P])
                rsum = tmp("rsum", [P, TILES, HEADS])
                gat = tmp("gat", [P, 2, C])
                stat = tmp("stat", [P, G, 6])
                mv = tmp("mv", [P, G, 2])
                rs = tmp("rs", [P, G])
                row2 = tmp("row2", [P, G, C])
                row2T = tmp("row2T", [P, 2, C])
                logits = tmp("logits", [P, G, EXPERTS])
                top8 = tmp("top8", [P, G, 8])
                top8i = tmp("top8i", [P, G, 8], U32)
                topf = tmp("topf", [P, 2, G])
                gap = tmp("gap", [P, G])
                duo = tmp("duo", [P, 2, G])
                one = tmp("one", [P, 2, G, EXPERTS])
                both = tmp("both", [P, G + 1, EXPERTS])
                place = tmp("place", [P, G, EXPERTS])
                hit = tmp("hit", [P, G, EXPERTS])
                slot_f = tmp("slot_f", [P, 2, G])
                slot = tmp("slot", [P, 2, G], I32)
                dest = tmp("dest", [P, G, 2])
                node = tmp("node", [P, 1])
                valid = tmp("valid", [P, 1])
                beyond = tmp("beyond", [P, 1])
                js_in = sem("js_in")
                x_got = [sem(f"x_got{i}") for i in range(G)]
                jn_dve, ch_dve = sem("jn_dve"), sem("ch_dve")
                b1_turned, b1_kept = sem("b1_turned"), sem("b1_kept")
                preset = sem("preset")
                mixed = sem("mixed")
                x1_ready = sem("x1_ready")
                var2_ready, sqrt2 = sem("var2_ready"), sem("sqrt2")
                row2_ready, row2_turned, row2T_ready = sem("row2_ready"), sem("row2_turned"), sem("row2T_ready")
                gated, logits_read = sem("gated"), sem("logits_read")
                e_in, e_out = sem("e_in"), sem("e_out")
                both_ready, ranked = sem("both_ready"), sem("ranked")
                masked = sem("masked")
                meta_ready, staged = sem("meta_ready"), sem("staged")
                sent = [sem(f"sent{i}") for i in range(G)]

                def before(i):
                    return 1 if i == 0 else 2

                with nc.Block() as block:
                    @block.sync
                    def _(sp):
                        sp.dma_start(gate[:, :, :], gate_w.rearrange("(c p) e -> p c e", p=P)).then_inc(js_in, 16)
                        sp.dma_start(gate_b_bc[:, :], gate_b.partition_broadcast(P)).then_inc(js_in, 16)
                        sp.dma_start(b1_raw[:, :], b1.rearrange("e (f p) -> (e f) p", p=P)).then_inc(js_in, 16)
                        sp.dma_start(gamma_bc[:, :], gamma.partition_broadcast(P)).then_inc(js_in, 16)
                        sp.dma_start(beta_bc[:, :], beta.partition_broadcast(P)).then_inc(js_in, 16)

                        def load(g):
                            for i in range(G):
                                t = g * G + i
                                if not starts(g):
                                    sp.wait_ge(x1_ready, t - G + 3)
                                sp.dma_start(x_t[:, i, :], xb_d[bass.ds(t * P, P), :]).then_inc(x_got[i], 16)
                                sp.dma_start(xnT_t[:, i, :], xnT_d[bass.ds(t, 1), :, :].rearrange("a p c -> p (a c)")).then_inc(x_got[i], 16)

                        load(0)
                        with sp.Fori(1, GROUPS - 1) as g:
                            load(g)
                        load(GROUPS - 1)
                        sp.wait_ge(js_in, 80)

                    @block.tensor
                    def _(pe):
                        pe.sem_inc(x1_ready, 2)
                        pe.sem_inc(logits_read, 1)
                        pe.sem_inc(row2T_ready, 2)
                        pe.wait_ge(js_in, 80)
                        pe.transpose(bank[7][:, 0:EXPERTS * FC], b1_raw[:, :], ident[0:EXPERTS * FC, 0:EXPERTS * FC]).then_inc(b1_turned, 1)

                        def mix(g, i):
                            t, b = g * G + i, i % 2
                            pe.wait_ge(x_got[i], 32 * g + 32)
                            pe.wait_ge(x1_ready, t + 3 - before(i))
                            for c in range(2):
                                m = pe.matmul(bank[b][:, 0:C], xnT_t[:, i, c * P:(c + 1) * P], mixG[:, c, :], start=c == 0, stop=c == 1)
                            m.then_inc(mixed, 1)

                        def turn(g, i):
                            t, b = g * G + i, i % 2
                            pe.wait_ge(row2_ready, t + 1)
                            pe.wait_ge(row2T_ready, t + 3 - before(i))
                            for c in range(2):
                                m = pe.transpose(bank[2 + b][:, c * P:(c + 1) * P], row2[:, i, c * P:(c + 1) * P], ident[:, :])
                            m.then_inc(row2_turned, 1)

                        def gates(g, i):
                            t, b = g * G + i, i % 2
                            out_ = bank[4][:, i * EXPERTS:(i + 1) * EXPERTS]
                            if i == 0:
                                pe.wait_ge(logits_read, g + 1)
                            pe.wait_ge(row2T_ready, t + 3)
                            for c in range(2):
                                m = pe.matmul(out_, row2T[:, b, c * P:(c + 1) * P], gate[:, c, :], start=c == 0, stop=c == 1)
                            m.then_inc(gated, 1)

                        def rank(g):
                            pe.wait_ge(both_ready, g + 1)
                            pe.matmul(bank[6][:, 0:P], below[:, :], both[:, :, :].rearrange("p i e -> p (i e)"), start=True, stop=False)
                            for i in range(G):
                                m = pe.matmul(bank[6][:, (i + 1) * EXPERTS:P].rearrange("p (i e) -> p i e", e=EXPERTS), ones[:, :],
                                              over(both[:, i, :], G - i), start=False, stop=i == G - 1)
                            m.then_inc(ranked, 1)

                        def group(g, more):
                            for i in range(G):
                                turn(g, i)
                                if more:
                                    mix(g + 1, i)
                                if i > 0:
                                    gates(g, i - 1)
                            gates(g, G - 1)
                            rank(g)

                        for i in range(G):
                            mix(0, i)
                        with pe.Fori(0, GROUPS - 1) as g:
                            group(g, True)
                        group(GROUPS - 1, False)

                    @block.scalar
                    def _(act):
                        act.wait_ge(b1_turned, 1)
                        act.copy(b1T[:, :], bank[7][:, 0:EXPERTS * FC]).then_inc(b1_kept, 1)

                        def root(g):
                            act.wait_ge(var2_ready, g + 1)
                            act.activation(rs[:, :], rs[:, :], ACT.Sqrt).then_inc(sqrt2, 1)

                        def stage_(g, places):
                            for i in places:
                                if not starts(g):
                                    act.wait_ge(sent[i], 32 * g)
                                for q in range(2):
                                    act.copy(stage_x[:, i, q, 0:C], row2[:, i, :])
                                act.copy(work_f[:, bass.ds((g * G + i) * EXT, C)], row2[:, i, :]).then_inc(staged, 1)

                        def group(g, more):
                            for i in range(G):
                                act.wait_ge(row2_turned, g * G + i + 1)
                                act.copy(row2T[:, i % 2, :], bank[2 + i % 2][:, 0:C]).then_inc(row2T_ready, 1)
                            if more:
                                root(g + 1)
                            stage_(g, range(G // 2 + 1))
                            act.wait_ge(e_in, g + 1)
                            act.activation(gap[:, :], gap[:, :], ACT.Exp).then_inc(e_out, 1)
                            stage_(g, range(G // 2 + 1, G))

                        root(0)
                        group(0, True)
                        with act.Fori(1, GROUPS - 1) as g:
                            group(g, True)
                        group(GROUPS - 1, False)

                    @block.gpsimd
                    def _(pool):
                        kw = dict(allow_small_or_imprecise_dtypes=True)
                        pool.iota(node[:, :], pattern=[[1, 1]], base=0, channel_multiplier=1, **kw)
                        pool.iota(carry[:, :], pattern=[[REGION, EXPERTS]], base=0, channel_multiplier=0, **kw)
                        pool.memset(both[:, G, :], 0.0)
                        pool.iota(dest[:, :, :], pattern=[[2 * P, G], [1, 2]], base=0, channel_multiplier=2, **kw).then_inc(preset, 1)

                        def send(g):
                            pool.wait_ge(meta_ready, g + 1)
                            for i in range(G):
                                pool.wait_ge(staged, g * G + i + 1)
                                pool.sem_inc(pool_on, 1)
                                for q in range(2):
                                    pool.indirect_dma_start(slots_x, bass.IndirectOffsetOnAxis(ap=slot[:, q, i:i + 1], axis=0),
                                                            stage_x[:, i, q, :], None, bounds_check=SLOTS - 1,
                                                            oob_is_err=False).then_inc(sent[i], 16)

                        with pool.Fori(0, GROUPS) as g:
                            send(g)
                        for i in range(G):
                            pool.wait_ge(sent[i], 32 * GROUPS)

                    @block.vector
                    def _(dve):
                        steps = Steps(dve, jn_dve)
                        steps.done(dve.tensor_scalar(rsum[:, :, :], acc[:, :, C:C + HEADS], 1e-16, None, ALU.add))
                        steps.done(dve.reciprocal(rsum[:, :, :], rsum[:, :, :]))
                        dve.wait_ge(preset, 1)
                        steps.done(dve.tensor_scalar(valid[:, :], node[:, :], float(LAST), None, ALU.is_lt))
                        steps.done(dve.tensor_scalar(beyond[:, :], node[:, :], float(LAST), float(SLOTS), ALU.is_ge, ALU.mult))
                        rsum_f = rsum[:, :, :].rearrange("p t h -> p (t h)")
                        first = steps.n

                        def sweep(g, join):
                            if join is not None:
                                steps.at(first + join * 3 * G)
                            if g is not None and not starts(g):
                                dve.wait_ge(staged, g * G)
                            def normed(i):
                                if g is not None and i < G:
                                    dve.tensor_scalar(row2[:, i, :], acc_f[:, bass.ds((g * G + i) * EXT, C)], mv[:, i, 0:1],
                                                      rs[:, i:i + 1], ALU.subtract, ALU.mult).then_inc(row2_ready, 1)

                            normed(0)
                            normed(1)
                            for i in range(G):
                                if join is not None:
                                    t, b = join * G + i, i % 2
                                    rows = acc_f[:, bass.ds(t * EXT, C)]
                                    steps.go(dve.tensor_tensor(gat[:, b, :].rearrange("p (h d) -> p h d", d=HD),
                                                               rows.rearrange("p (h d) -> p h d", d=HD),
                                                               spread(rsum_f[:, bass.ds(t * HEADS, HEADS)], HD), ALU.mult))
                                normed(i + 2)
                                if join is not None:
                                    if i > 0:
                                        stats_of(join, i - 1)
                                    dve.wait_ge(jn_dve, steps.base + (3 * i + 1))
                                    dve.wait_ge(x_got[i], 32 * join + 32)
                                    steps.go(dve.tensor_tensor(gat[:, b, :], gat[:, b, :], x_t[:, i, :], ALU.add))
                                    dve.wait_ge(mixed, t + 1)
                                    dve.wait_ge(jn_dve, steps.base + (3 * i + 2))
                                    dve.tensor_tensor(rows, gat[:, b, :], bank[b][:, 0:C], ALU.add).then_inc(x1_ready, 1)
                            if join is not None:
                                stats_of(join, G - 1)

                        def stats_of(g, i):
                            t = g * G + i
                            dve.wait_ge(x1_ready, t + 3)
                            dve.sem_inc(dve_on, 1)
                            steps.go(dve.bn_stats(stat[:, i, :], acc_f[:, bass.ds(t * EXT, C)]))

                        chosen = Steps(dve, ch_dve)
                        SPREAD, CHOICE = G + 1, 2 * G + 22

                        def spread_of(g):
                            if starts(g):
                                chosen.at(0)
                            else:
                                chosen.at(g * (SPREAD + 1) + (g - 1) * CHOICE)
                            dve.wait_ge(jn_dve, first + (g + 1) * 3 * G)
                            dve.sem_inc(dve_on, 1)
                            for i in range(G):
                                chosen.go(dve.bn_aggr(mv[:, i, :], stat[:, i, :]))
                            dve.wait_ge(ch_dve, chosen.base + chosen.n)
                            chosen.done(dve.tensor_scalar(rs[:, :], mv[:, :, 1], EPS, None, ALU.add))
                            dve.sem_inc(var2_ready, 1)

                        def invert(g):
                            dve.wait_ge(sqrt2, g + 1)
                            dve.sem_inc(dve_on, 1)
                            chosen.done(dve.reciprocal(rs[:, :], rs[:, :]))

                        def choose(g):
                            last_group = is_group_last(g)
                            chosen.at((GROUPS if last_group else g + 2) * (SPREAD + 1) + g * CHOICE - (0 if last_group else 1))
                            dve.wait_ge(gated, (g + 1) * G)
                            chosen.done(dve.tensor_tensor(logits[:, :, :], bank[4][:, 0:G * EXPERTS].rearrange("p (i e) -> p i e", e=EXPERTS),
                                                          over(gate_b_bc[:, :], G), ALU.add))
                            dve.sem_inc(logits_read, 1)
                            for i in range(G):
                                chosen.go(dve.max(top8[:, i, :], logits[:, i, :]))
                            dve.wait_ge(ch_dve, chosen.base + chosen.n)
                            dve.sem_inc(dve_on, 1)
                            for i in range(G):
                                chosen.go(dve.max_index(top8i[:, i, :], top8[:, i, :], logits[:, i, :]))
                            chosen.go(dve.tensor_copy(duo[:, :, :], top8[:, :, 0:2].rearrange("p i q -> p q i")))
                            dve.wait_ge(ch_dve, chosen.base + chosen.n)
                            chosen.go(dve.tensor_copy(topf[:, :, :], top8i[:, :, 0:2].rearrange("p i q -> p q i")))
                            chosen.done(dve.tensor_tensor(gap[:, :], duo[:, 1, :], duo[:, 0, :], ALU.subtract))
                            dve.sem_inc(e_in, 1)
                            for q in range(2):
                                chosen.go(dve.tensor_tensor(one[:, q, :, :], over(iota[:, 0:EXPERTS], G), spread(topf[:, q, :], EXPERTS), ALU.is_equal))
                            dve.wait_ge(ch_dve, chosen.base + chosen.n)
                            if last_group:
                                for q in range(2):
                                    dve.tensor_scalar(one[:, q, G - 1, :], one[:, q, G - 1, :], valid[:, 0:1], None, ALU.mult).then_inc(masked, 1)
                                dve.wait_ge(masked, 2)
                            chosen.done(dve.tensor_tensor(both[:, 0:G, :], one[:, 0, :, :], one[:, 1, :, :], ALU.add))
                            dve.sem_inc(both_ready, 1)
                            dve.wait_ge(e_out, g + 1)
                            chosen.done(dve.tensor_scalar(duo[:, 0, :], gap[:, :], 1.0, None, ALU.add))
                            chosen.done(dve.reciprocal(duo[:, 0, :], duo[:, 0, :]))
                            chosen.done(dve.tensor_tensor(duo[:, 1, :], duo[:, 0, :], gap[:, :], ALU.mult))
                            for q in range(2):
                                chosen.go(dve.tensor_copy(share_f[:, bass.ds(g * G + q * TILES, G)], duo[:, q, :]))
                            if not starts(g):
                                for i in range(G):
                                    dve.wait_ge(sent[i], 32 * g)
                            for q in range(2):
                                chosen.go(dve.tensor_copy(stage_x[:, :, q, C], dest[:, :, q]))
                            dve.wait_ge(ranked, g + 1)
                            chosen.done(dve.tensor_tensor(place[:, :, :], bank[6][:, 0:G * EXPERTS].rearrange("p (i e) -> p i e", e=EXPERTS),
                                                          over(carry[:, :], G), ALU.add))
                            chosen.done(dve.tensor_tensor(carry[:, :], carry[:, :], bank[6][:, G * EXPERTS:P], ALU.add))
                            for q in range(2):
                                chosen.done(dve.tensor_tensor(hit[:, :, :], place[:, :, :], one[:, q, :, :], ALU.mult))
                                chosen.done(dve.tensor_reduce(slot_f[:, q, :], hit[:, :, :], X, ALU.add))
                            if last_group:
                                for q in range(2):
                                    dve.tensor_tensor(slot_f[:, q, G - 1:G], slot_f[:, q, G - 1:G], beyond[:, :], ALU.add).then_inc(masked, 1)
                                dve.wait_ge(masked, 4)
                            chosen.done(dve.tensor_copy(slot[:, :, :], slot_f[:, :, :]))
                            chosen.done(dve.tensor_scalar(dest[:, :, :], dest[:, :, :], float(2 * P * G), None, ALU.add))
                            dve.sem_inc(meta_ready, 1)
                            assert chosen.n == CHOICE, chosen.n
                            chosen.at(chosen.base + CHOICE)

                        share_f = share[:, :, :].rearrange("p q t -> p (q t)")
                        sweep(None, 0)
                        spread_of(0)
                        invert(0)

                        def group(g):
                            sweep(g, g + 1)
                            spread_of(g + 1)
                            choose(g)
                            invert(g + 1)

                        group(0)
                        with dve.Fori(1, GROUPS - 1) as g:
                            group(g)
                        sweep(GROUPS - 1, None)
                        choose(GROUPS - 1)
                        dve.wait_ge(b1_kept, 1)

            b2_bc = keep_("b2_bc", [P, EXPERTS * C])
            plan = keep_("plan", [1, STILES, 4], I32)
            with ExitStack() as stage:
                def tmp(name, shape, dt=F32):
                    return stage.enter_context(nc.sbuf_tensor(name, shape, dt))

                fill = tmp("fill", [P, XROW])
                fill_at = tmp("fill_at", [1, EXPERTS], I32)
                region0 = tmp("region0", [1, EXPERTS])
                count = tmp("count", [1, EXPERTS])
                etiles = tmp("etiles", [1, EXPERTS])
                etiles_i = tmp("etiles_i", [1, EXPERTS], I32)
                eend = tmp("eend", [1, EXPERTS])
                shift = tmp("shift", [1, EXPERTS])
                scol = tmp("scol", [1, STILES])
                ecmp = big[0:1, 0:STILES * EXPERTS].rearrange("a (s e) -> a s e", e=EXPERTS)
                eidx = tmp("eidx", [1, STILES])
                srow = tmp("srow", [1, STILES])
                real = tmp("real", [1, STILES])
                expert = tmp("expert", [1, STILES])
                rt_set, rt_dve = sem("rt_set"), sem("rt_dve")
                fill_set, fill_at_set, filled = sem("fill_set"), sem("fill_at_set"), sem("filled")
                b2_in = sem("b2_in")
                with nc.Block() as block:
                    @block.gpsimd
                    def _(pool):
                        kw = dict(allow_small_or_imprecise_dtypes=True)
                        pool.memset(fill[:, 0:C], 0.0)
                        pool.memset(fill[:, C:XROW], float(2 * TILES * P)).then_inc(fill_set, 1)
                        pool.iota(scol[:, :], pattern=[[1, STILES]], base=0, channel_multiplier=0, **kw)
                        pool.iota(region0[:, :], pattern=[[REGION, EXPERTS]], base=0, channel_multiplier=0, **kw).then_inc(rt_set, 1)

                    @block.sync
                    def _(sp):
                        regs = [sp.alloc_register(f"fill{e}") for e in range(EXPERTS)]
                        sp.wait_ge(fill_set, 1)
                        sp.dma_start(slots_x[NULL_ROW:SLOTS, :], fill[:, :]).then_inc(filled, 16)
                        sp.wait_ge(fill_at_set, 1)
                        sp.load(regs, fill_at[0:1, :])
                        for e in range(EXPERTS):
                            at = sp.snap(regs[e], min_val=0, max_val=NULL_ROW - P)
                            sp.dma_start(slots_x[bass.ds(at, P), :], fill[:, :]).then_inc(filled, 16)
                        sp.wait_ge(filled, 16 * (EXPERTS + 1))

                    @block.scalar
                    def _(act):
                        act.dma_start(b2_bc[:, :], b2.rearrange("e c -> (e c)").partition_broadcast(P)).then_inc(b2_in, 16)
                        act.wait_ge(b2_in, 16)

                    @block.vector
                    def _(dve):
                        steps = Steps(dve, rt_dve)
                        steps.done(dve.tensor_copy(fill_at[:, :], carry[0:1, :]))
                        dve.sem_inc(fill_at_set, 1)
                        dve.wait_ge(rt_set, 1)
                        steps.done(dve.tensor_tensor(count[:, :], carry[0:1, :], region0[:, :], ALU.subtract))
                        steps.done(dve.tensor_scalar(etiles_i[:, :], count[:, :], float(P - 1), None, ALU.add))
                        steps.done(dve.tensor_scalar(etiles_i[:, :], etiles_i[:, :], 7, None, ALU.arith_shift_right))
                        steps.done(dve.tensor_copy(etiles[:, :], etiles_i[:, :]))
                        steps.done(dve.tensor_tensor_scan(eend[:, :], ones[0:1, 0:EXPERTS], etiles[:, :], 0.0, ALU.mult, ALU.add))
                        steps.done(dve.tensor_tensor(shift[:, :], etiles[:, :], eend[:, :], ALU.subtract))
                        steps.done(dve.scalar_tensor_tensor(shift[:, :], shift[:, :], float(P), region0[:, :], ALU.mult, ALU.add))
                        steps.done(dve.tensor_tensor(ecmp[:, :, :], over(eend[:, :], STILES), spread(scol[:, :], EXPERTS), ALU.is_le))
                        steps.done(dve.tensor_reduce(eidx[:, :], ecmp[:, :, :], X, ALU.add))
                        steps.done(dve.tensor_scalar(expert[:, :], eidx[:, :], float(EXPERTS - 1), None, ALU.min))
                        steps.done(dve.tensor_copy(plan[:, :, 1], expert[:, :]))
                        steps.done(dve.memset(plan[:, 0:2, 2], 1))
                        steps.done(dve.tensor_tensor(plan[:, 2:STILES, 2], expert[:, 2:STILES], expert[:, 0:STILES - 2], ALU.not_equal))
                        steps.done(dve.tensor_scalar(real[:, :], eidx[:, :], float(EXPERTS), None, ALU.is_lt))
                        steps.done(dve.tensor_tensor(ecmp[:, :, :], over(iota[0:1, 0:EXPERTS], STILES), spread(eidx[:, :], EXPERTS), ALU.is_equal))
                        steps.done(dve.tensor_tensor(ecmp[:, :, :], ecmp[:, :, :], over(shift[:, :], STILES), ALU.mult))
                        steps.done(dve.tensor_reduce(srow[:, :], ecmp[:, :, :], X, ALU.add))
                        steps.done(dve.scalar_tensor_tensor(srow[:, :], scol[:, :], float(P), srow[:, :], ALU.mult, ALU.add))
                        steps.done(dve.tensor_scalar(srow[:, :], srow[:, :], -float(NULL_ROW), None, ALU.add))
                        steps.done(dve.tensor_tensor(srow[:, :], srow[:, :], real[:, :], ALU.mult))
                        steps.done(dve.tensor_scalar(plan[:, :, 0], srow[:, :], float(NULL_ROW), None, ALU.add))
                        steps.done(dve.memset(plan[:, :, 3], 0))

            with ExitStack() as stage:
                def tmp(name, shape, dt=F32):
                    return stage.enter_context(nc.sbuf_tensor(name, shape, dt))

                w1_s = big[:, 0:2048].rearrange("p (b c f) -> p b c f", b=2, c=2)
                w2_s = big[:, 2048:4096].rearrange("p (b c f) -> p b c f", b=2, c=4)
                hid = big[:, 4096:5120].rearrange("p (b f s) -> p b f s", b=2, f=4)
                inT = big[:, 5120:5632].rearrange("p (b c) -> p b c", b=2)
                res = big[:, 5632:6656].rearrange("p (m c) -> p m c", m=4)
                in_s = big[:, 6656:6656 + 4 * XROW].rearrange("p (m c) -> p m c", m=4)
                goal = tmp("goal", [P, 8, 1], I32)
                w1_got = [sem(f"w1_got{b}") for b in range(2)]
                w2_got = [sem(f"w2_got{b}") for b in range(2)]
                in_got = [sem(f"in_got{m}") for m in range(4)]
                in_turned, inT_ready = sem("in_turned"), sem("inT_ready")
                h_done, h_ready = sem("h_done"), sem("h_ready")
                y_done, y_ready = sem("y_done"), sem("y_ready")
                y_out = [sem(f"y_out{m}") for m in range(4)]
                x1_shifted = sem("x1_shifted")
                with nc.Block() as block:
                    @block.sync
                    def _(sp):
                        r_reg = sp.alloc_register("row_sp")
                        regs = [sp.alloc_register(f"plan_sp{q}") for q in range(2)]

                        def rows(s, m):
                            sp.load(r_reg, plan[0:1, bass.ds(s, 1), 0:1].rearrange("p a q -> p (a q)"))
                            r = sp.snap(r_reg, min_val=0, max_val=NULL_ROW)
                            if not (isinstance(s, int) and s < 4):
                                sp.wait_ge(inT_ready, s - 1)
                            sp.dma_start(in_s[:, m, :], slots_x[bass.ds(r, P), :]).then_inc(in_got[m], 16)

                        def weights(s, b):
                            sp.load(regs, plan[0:1, bass.ds(s, 1), 1:3].rearrange("p a q -> p (a q)"))
                            e = sp.snap(regs[0], min_val=0, max_val=EXPERTS - 1)
                            other = sp.snap(regs[1], min_val=0, max_val=1)
                            sp.wait_ge(h_done, s + 1)
                            sp.dma_start(w1_s[:, b, :, :], w1[bass.ds(e, 1), :, :].rearrange("a (c p) f -> p (a c) f", p=P),
                                         cond=other).then_inc(w1_got[b], 16)
                            sp.wait_ge(y_done, s + 1)
                            sp.dma_start(w2_s[:, b, :, :], w2[bass.ds(e, 1), :, :].rearrange("a (c p) f -> p (a c) f", p=P),
                                         cond=other).then_inc(w2_got[b], 16)

                        for s in range(4):
                            rows(s, s)
                        weights(0, 0)

                        def step(s, i):
                            rows(s + i + 4, i)
                            weights(s + i + 1, (i + 1) % 2)

                        with sp.Fori(0, STILES // 4 - 1) as h:
                            for i in range(4):
                                step(h * 4, i)
                        for s in range(STILES // 4 * 4 - 4, STILES - 1):
                            if s + 4 < STILES:
                                rows(s + 4, s % 4)
                            weights(s + 1, (s + 1) % 2)

                    @block.tensor
                    def _(pe):
                        pe.sem_inc(inT_ready, 2)
                        pe.sem_inc(h_done, 2)
                        pe.sem_inc(y_done, 2)
                        pe.sem_inc(y_ready, 2)

                        def turn(s, i):
                            pe.wait_ge(in_got[i % 4], 4 * (s - i) + 16 * (i // 4 + 1))
                            b = i % 2
                            for c in range(2):
                                m = pe.transpose(bank[b][:, c * P:(c + 1) * P], in_s[:, i % 4, c * P:(c + 1) * P], ident[:, :])
                            m.then_inc(in_turned, 1)

                        def hidden(s, i):
                            b = i % 2
                            pe.wait_ge(inT_ready, s + 3)
                            pe.wait_ge(w1_got[b], 8 * (s - b) + 16)
                            for f in range(FC):
                                for c in range(2):
                                    m = pe.matmul(bank[2 + b][:, f * P:(f + 1) * P], w1_s[:, b, c, f * P:(f + 1) * P],
                                                  inT[:, b, c * P:(c + 1) * P], start=c == 0, stop=c == 1)
                            m.then_inc(h_done, 1)

                        def down(s, i):
                            b = i % 2
                            pe.wait_ge(h_ready, s + 1)
                            pe.wait_ge(w2_got[b], 8 * (s - b) + 16)
                            pe.wait_ge(y_ready, s + 1)
                            for f in range(FC):
                                m = pe.matmul(bank[4 + b][:, 0:C], hid[:, b, f, :], w2_s[:, b, f, :], start=f == 0, stop=f == FC - 1)
                            m.then_inc(y_done, 1)

                        def step(s0, i):
                            s = s0 + i
                            hidden(s, i)
                            if not (isinstance(s, int) and s >= STILES - 2):
                                turn(s + 2, i + 2)
                            if not (isinstance(s, int) and s == 0):
                                down(s - 1, i + 3 if i == 0 else i - 1)

                        turn(0, 0)
                        turn(1, 1)
                        for i in range(4):
                            step(0, i)
                        with pe.Fori(1, STILES // 4) as h:
                            for i in range(4):
                                step(h * 4, i)
                        for i in range(STILES % 4):
                            step(STILES - STILES % 4, i)
                        down(STILES - 1, 1)

                    @block.scalar
                    def _(act):
                        e_reg = act.alloc_register("expert_act")

                        def relu(s0, b):
                            s = s0 + b
                            act.load(e_reg, plan[0:1, bass.ds(s, 1), 1:2].rearrange("p a q -> p (a q)"))
                            e = act.snap(e_reg, min_val=0, max_val=EXPERTS - 1)
                            act.wait_ge(h_done, s + 3)
                            act.wait_ge(y_done, s + 1)
                            for f in range(FC):
                                a = act.activation(hid[:, b, f, :], bank[2 + b][:, f * P:(f + 1) * P], ACT.Relu,
                                                   bias=b1T[:, bass.ds(e * FC + f, 1)])
                            a.then_inc(h_ready, 1)

                        with by_two(act, 0, STILES) as s0:
                            relu(s0, 0)
                            relu(s0, 1)

                    @block.vector
                    def _(dve):
                        e_reg = dve.alloc_register("expert_dve")

                        def move_in(s, b, m):
                            dve.wait_ge(in_turned, s + 1)
                            dve.wait_ge(h_done, s + 1)
                            dve.tensor_copy(goal[:, m, :], in_s[:, m % 4, C:XROW])
                            dve.tensor_copy(inT[:, b, :], bank[b][:, 0:C]).then_inc(inT_ready, 1)

                        def move_out(s, b, m):
                            dve.load(e_reg, plan[0:1, bass.ds(s, 1), 1:2].rearrange("p a q -> p (a q)"))
                            e = dve.snap(e_reg, min_val=0, max_val=EXPERTS - 1)
                            dve.wait_ge(y_done, s + 3)
                            if not (isinstance(s, int) and s < 4):
                                dve.wait_ge(y_out[m % 4], 4 * (s - m % 4))
                            dve.tensor_tensor(res[:, m % 4, :], bank[4 + b][:, 0:C], b2_bc[:, bass.ds(e * C, C)], ALU.add).then_inc(y_ready, 1)

                        def eight(s):
                            for i in range(8):
                                move_in(s + i + 2, i % 2, (i + 2) % 8)
                                move_out(s + i, i % 2, i)

                        move_in(0, 0, 0)
                        move_in(1, 1, 1)
                        eight(0)
                        with dve.Fori(1, (STILES - 2) // 8) as h:
                            eight(h * 8)
                        move_out(STILES - 2, 0, 0)
                        move_out(STILES - 1, 1, 1)

                    @block.gpsimd
                    def _(pool):
                        def send(s, b, m):
                            pool.wait_ge(y_ready, s + 3)
                            pool.sem_inc(pool_on, 1)
                            pool.indirect_dma_start(moe_d, bass.IndirectOffsetOnAxis(ap=goal[:, m, :], axis=0), res[:, m % 4, :], None,
                                                    bounds_check=2 * TILES * P - 1, oob_is_err=False).then_inc(y_out[m % 4], 16)

                        def shift_x1(t):
                            rows = acc_f[:, bass.ds(t * EXT, C)]
                            pool.tensor_tensor(rows, rows, beta_bc[:, :], ALU.add).then_inc(x1_shifted, 1)

                        shift_x1(TILES - 1)
                        with pool.Fori(0, (TILES - 1) // 4) as h:
                            for i in range(8):
                                send(h * 8 + i, i % 2, i)
                                if i % 2 == 0:
                                    shift_x1(h * 4 + i // 2)
                        with pool.Fori((TILES - 1) // 4, (STILES - 2) // 8) as h:
                            for i in range(8):
                                send(h * 8 + i, i % 2, i)
                        send(STILES - 2, 0, 0)
                        send(STILES - 1, 1, 1)
                        pool.wait_ge(x1_shifted, TILES)
                        for m in range(4):
                            pool.wait_ge(y_out[m], 16 * ((STILES - 1 - m) // 4 + 1))

            with ExitStack() as stage:
                y_got = big[:, 0:2 * G * 2 * C].rearrange("p (b i q c) -> p b i q c", b=2, i=G, q=2)
                y_in = [sem(f"y_in{b}") for b in range(2)]
                cb_dve, y_used = sem("cb_dve"), sem("y_used")
                var3_ready, sqrt3 = sem("var3_ready"), sem("sqrt3")
                scaled, stretched = sem("scaled"), sem("stretched")
                o_ready, o_out = sem("o_ready"), sem("o_out")
                moe_t = moe_d.rearrange("(t p q) c -> t p q c", p=P, q=2)

                def group_of(t, g, width):
                    return t[:, bass.ds(g * G, G), 0:width]

                with nc.Block() as block:
                    @block.sync
                    def _(sp):
                        def load(g):
                            full = G - 1 if g == GROUPS - 1 else G
                            sp.wait_ge(y_used, g + 1)
                            sp.dma_start(y_got[:, g % 2, 0:full, :, :].rearrange("p i q c -> p i (q c)"),
                                         moe_t[g * G:g * G + full, :, :, :].rearrange("t p q c -> p t (q c)")).then_inc(y_in[g % 2], 16)
                            if full < G:
                                sp.dma_start(y_got[0:LAST, g % 2, full, :, :], moe_t[TILES - 1, 0:LAST, :, :]).then_inc(y_in[g % 2], 16)

                        def store(g):
                            full = G - 1 if g == GROUPS - 1 else G
                            sp.wait_ge(o_ready, (g + 1) * G)
                            sp.dma_start(out[g * G * P:(g * G + full) * P, :].rearrange("(t p) c -> p t c", p=P),
                                         work[:, g * G:g * G + full, 0:C]).then_inc(o_out, 16)
                            if full < G:
                                sp.dma_start(out[(TILES - 1) * P:N, :], work[0:LAST, TILES - 1, 0:C]).then_inc(o_out, 16)

                        for g in range(GROUPS + 3):
                            if g < GROUPS:
                                load(g)
                            if g >= 3:
                                store(g - 3)
                        sp.wait_ge(o_out, 16 * (GROUPS + 1))

                    @block.scalar
                    def _(act):
                        with act.Fori(0, GROUPS) as g:
                            group_rstd = rstd[:, bass.ds(g * G, G)]
                            act.wait_ge(var3_ready, 2 * g + 1)
                            act.activation(group_rstd, group_rstd, ACT.Sqrt).then_inc(sqrt3, 1)
                            act.wait_ge(var3_ready, 2 * g + 2)
                            for i in range(G):
                                rows = work_f[:, bass.ds((g * G + i) * EXT, C)]
                                act.activation(rows, rows, ACT.Identity, bias=mean[:, bass.ds(g * G + i, 1)],
                                               scale=rstd[:, bass.ds(g * G + i, 1)]).then_inc(scaled, 1)

                    @block.gpsimd
                    def _(pool):
                        with pool.Fori(0, GROUPS) as g:
                            for i in range(G):
                                rows = work_f[:, bass.ds((g * G + i) * EXT, C)]
                                pool.wait_ge(scaled, g * G + i + 1)
                                pool.tensor_tensor(rows, rows, gamma_bc[:, :], ALU.mult).then_inc(stretched, 1)

                    @block.vector
                    def _(dve):
                        steps = Steps(dve, cb_dve)
                        share_f = share[:, :, :].rearrange("p q t -> p (q t)")
                        STEPS = 3 * G + 9
                        dve.sem_inc(y_used, 2)

                        def sums(g, b):
                            steps.at(g * STEPS)
                            dve.wait_ge(y_in[b], 8 * (g - b) + 16 + (16 if is_group_last(g) else 0))
                            for q in range(2):
                                for i in range(G):
                                    rows = work_f[:, bass.ds((g * G + i) * EXT, C)]
                                    steps.go(dve.scalar_tensor_tensor(rows, y_got[:, b, i, q, :], share_f[:, bass.ds(g * G + i + q * TILES, 1)],
                                                                      rows, ALU.mult, ALU.add))
                                dve.wait_ge(cb_dve, steps.base + steps.n)
                            dve.sem_inc(y_used, 1)
                            for i in range(G):
                                t = g * G + i
                                steps.go(dve.bn_stats(stats[:, bass.ds(t, 1), :].rearrange("p a c -> p (a c)"),
                                                      work_f[:, bass.ds(t * EXT, C)]))
                            dve.wait_ge(cb_dve, steps.base + steps.n)
                            layer_stats(dve, steps, bass.ds(g * G, G))
                            dve.sem_inc(var3_ready, 1)
                            group_rstd, group_mean = rstd[:, bass.ds(g * G, G)], mean[:, bass.ds(g * G, G)]
                            dve.wait_ge(sqrt3, g + 1)
                            dve.sem_inc(dve_on, 1)
                            steps.done(dve.reciprocal(group_rstd, group_rstd))
                            steps.done(dve.scalar_tensor_tensor(group_mean, group_mean, -1.0, group_rstd, ALU.mult, ALU.mult))
                            dve.sem_inc(var3_ready, 1)
                            assert steps.n == STEPS, steps.n

                        def final(g):
                            for i in range(G):
                                t = g * G + i
                                rows = work_f[:, bass.ds(t * EXT, C)]
                                dve.wait_ge(stretched, t + 1)
                                dve.tensor_tensor(rows, rows, acc_f[:, bass.ds(t * EXT, C)], ALU.add).then_inc(o_ready, 1)

                        sums(0, 0)
                        with dve.Fori(0, GROUPS // 2 - 1) as h:
                            sums(h * 2 + 1, 1)
                            final(h * 2)
                            sums(h * 2 + 2, 0)
                            final(h * 2 + 1)
                        sums(GROUPS - 2, 1)
                        final(GROUPS - 3)
                        sums(GROUPS - 1, 0)
                        final(GROUPS - 2)
                        final(GROUPS - 1)


_INS = ['x', 'src', 'dst', 'L0_gnn_W', 'L0_gnn_a_src', 'L0_gnn_a_dst', 'L0_mix_Wqkv', 'L0_mix_Wout', 'L0_mix_bout',
        'L0_ffn_gate_w', 'L0_ffn_gate_b', 'L0_ffn_w1', 'L0_ffn_b1', 'L0_ffn_w2', 'L0_ffn_b2', 'L0_ffn_gamma',
        'L0_ffn_beta']


def kernel(**inputs):
    import concourse.bacc as _bacc
    from concourse.bass_utils import run_bass_kernel_spmd as _run

    nc = _bacc.Bacc("TRN2", target_bir_lowering=False, num_devices=1)
    arrays, args = {}, []
    for name in _INS:
        a = np.ascontiguousarray(inputs[name])
        arrays[f"in_{name}"] = a
        args.append(nc.dram_tensor(f"in_{name}", a.shape, mybir.dt.from_np(a.dtype), kind="ExternalInput").ap())
    args.append(nc.dram_tensor("out_0", (N, C), F32, kind="ExternalOutput").ap())
    build(nc, *args)
    r = _run(nc, [arrays], core_ids=[0])
    return r.results[0]["out_0"]
```

```python
from contextlib import ExitStack, contextmanager

import numpy as np

import concourse.bass as bass
from concourse import mybir

P = 128
N, C = 6250, 256
HEADS, HD = 8, 32
MH, MD = 8, 64
INNER = MH * MD
NE = 106250
EXPERTS, FF, TOPK = 16, 512, 2
EPS = 1e-5

TILES = -(-N // P)
LAST = N - (TILES - 1) * P
ETILES = -(-NE // P)
ELAST = NE - (ETILES - 1) * P
UNROLL = 16
ROUNDS = -(-(ETILES + TILES - 1) // UNROLL)
PAIRS = ROUNDS * UNROLL
PCH = -(-PAIRS // P)
ECH = -(-ETILES // P)
SPREAD = 60.0
NO_NODE = 1 << 20
EXT = C + 2 * HEADS
ROW = C + HEADS
STILES = (N * TOPK + EXPERTS * (P - 1)) // P
STILES += -(STILES - 2) % 8
FC = FF // P
G = 7
GROUPS = TILES // G
assert GROUPS * G == TILES and (TILES - 1) % 4 == 0 and STILES % 4 == 2 and STILES <= P
REGION = (TILES + 1) * P
NULL_ROW = EXPERTS * REGION
SLOTS = NULL_ROW + P
XROW = C + 1
BF16, F32, I32, U32 = mybir.dt.bfloat16, mybir.dt.float32, mybir.dt.int32, mybir.dt.uint32
ALU = mybir.AluOpType
ACT = mybir.ActivationFunctionType
X = mybir.AxisListType.X


class Steps:

    def __init__(self, engine, sem):
        self.engine, self.sem, self.n, self.base = engine, sem, 0, 0

    def done(self, instruction):
        self.go(instruction)
        self.engine.wait_ge(self.sem, self.base + self.n)

    def at(self, base):
        self.base, self.n = base, 0

    def go(self, instruction):
        self.n += 1
        instruction.then_inc(self.sem, 1)


@contextmanager
def by_two(engine, start, end):
    with engine.Fori(start // 2, end // 2) as half:
        yield half * 2


def each_pair(engine, body):
    body(0, (0, 1))
    with by_two(engine, 2, TILES - 1) as t0:
        body(t0, (0, 1))
    body(TILES - 1, (0,))


def each_tile(engine, body):
    def both(t0, buffers):
        for b in buffers:
            body(t0, b)

    each_pair(engine, both)


def by_four(engine, body):
    for m in range(4):
        body(0, m)
    with engine.Fori(1, TILES // 4) as h:
        for m in range(4):
            body(h * 4, m)
    body(TILES - 1, 0)


def is_last(t0):
    return isinstance(t0, int) and t0 == TILES - 1


def is_group_last(g):
    return isinstance(g, int) and g == GROUPS - 1


def starts(t0):
    return isinstance(t0, int) and t0 == 0


def spread(ap, n):
    return ap.unsqueeze(2).to_broadcast([ap.shape[0], ap.shape[1], n])


def over(ap, n):
    return ap.unsqueeze(1).to_broadcast([ap.shape[0], n, ap.shape[1]])


def build(nc, x, src, dst, gnn_W, a_src, a_dst, Wqkv, Wout, bout, gate_w, gate_b, w1, b1, w2, b2,
          gamma, beta, out):
    ctx = ExitStack()
    with ctx:
        def sb(name, shape, dt=F32):
            return ctx.enter_context(nc.sbuf_tensor(name, shape, dt))

        def sem(name):
            return ctx.enter_context(nc.semaphore(name))

        def dram(name, shape, dt=F32):
            return nc.dram_tensor(name, shape, dt).ap()

        src_rows = dram("src_rows", (ETILES, P), I32)
        dst_rows = dram("dst_rows", (ETILES + 1, P), I32)
        pair_acc_d = dram("pair_acc_d", (PCH * P,), I32)
        xnT_d = dram("xnT_d", (TILES, P, C))
        xb_d = dram("xb_d", (TILES * P, C))
        table = dram("table", (TILES * P, ROW))
        slots_x = dram("slots_x", (SLOTS, XROW))
        moe_d = dram("moe_d", (2 * TILES * P, C))

        bank = [ctx.enter_context(nc.psum_tensor(f"bank{i}", [P, 512], F32)) for i in range(8)]

        dve_on = sem("dve_on")
        pool_on = sem("pool_on")

        ident = sb("ident", [P, P])
        iota = sb("iota", [P, P])
        ones = sb("ones", [P, P])
        below = sb("below", [P, P])
        work = sb("work", [P, TILES, EXT])
        acc = sb("acc", [P, TILES, EXT])
        stats = sb("stats", [P, TILES, 6])
        mean = sb("mean", [P, TILES])
        rstd = sb("rstd", [P, TILES])
        small = sb("small", [P, TILES])
        wext = sb("wext", [P, 2, EXT])
        wkvT = sb("wkvT", [P, 2, 2 * INNER])
        wq = sb("wq", [P, 4, C])
        woutT = sb("woutT", [P, 4, C])
        mixG = sb("mixG", [P, 2, C])
        bout_bc = sb("bout_bc", [P, C])
        src_cols = sb("src_cols", [P, PCH * P], I32)
        dst_cols = sb("dst_cols", [P, PCH * P + 2])
        pair_acc = sb("pair_acc", [1, PCH * P], I32)
        big = sb("big", [P, 8192])

        def flat(t):
            return t[:, :, :].rearrange("p t c -> p (t c)")

        work_f, acc_f = flat(work), flat(acc)

        def layer_stats(dve, steps, tiles=slice(0, TILES)):
            me, mo = stats[:, tiles, 1], stats[:, tiles, 4]
            mean_, rstd_, small_ = mean[:, tiles], rstd[:, tiles], small[:, tiles]
            steps.done(dve.tensor_tensor(mean_, me, mo, ALU.subtract))
            steps.done(dve.tensor_tensor(small_, mean_, mean_, ALU.mult))
            steps.done(dve.tensor_tensor(rstd_, stats[:, tiles, 2], stats[:, tiles, 5], ALU.add))
            steps.done(dve.tensor_scalar(rstd_, rstd_, 1.0 / C, EPS, ALU.mult, ALU.add))
            steps.done(dve.scalar_tensor_tensor(rstd_, small_, 0.25, rstd_, ALU.mult, ALU.add))
            steps.done(dve.tensor_tensor(mean_, me, mo, ALU.add))
            steps.done(dve.tensor_scalar(mean_, mean_, 0.5, None, ALU.mult))

        kv_raw = big[:, 0:2048].rearrange("p (r c) -> p r c", c=C)
        wout_raw = big[:, 2048:3072].rearrange("p (r c) -> p r c", c=INNER)
        a_bc = big[:, 3072:3584].rearrange("p (a c) -> p a c", a=2)
        prod = big[:, 3584:3840]
        hmean = big[:, 3840:3872].rearrange("p (c g) -> p c g", c=2)
        dst_g = sb("dst_g", [P, PCH, P], I32)
        src_g = sb("src_g", [P, PCH, P], I32)
        dst_f = big[:, 4096:4096 + PCH * P].rearrange("p (c e) -> p c e", e=P)
        src_f = big[:, 6144:6144 + PCH * P].rearrange("p (c e) -> p c e", e=P)
        general = sb("general", [1, 1], I32)
        unsorted = sb("unsorted", [P, 1])
        jbase = sb("jbase", [P, PCH])
        tki = sb("tki", [P, PCH], I32)
        edges_got = sem("edges_got")
        x_in = [sem("x_in0"), sem("x_in1")]
        last_zero, stated = sem("last_zero"), sem("stated")
        XCH = (TILES - 1) // 4
        with ExitStack() as stage:
            def tmp(name, shape, dt=F32):
                return stage.enter_context(nc.sbuf_tensor(name, shape, dt))

            last_rows = tmp("last_rows", [1, 2, P], I32)
            end_row = tmp("end_row", [1, P], I32)
            ends = tmp("ends", [P, ECH, P], I32)
            endsf = tmp("endsf", [P, ECH, 2])
            node0 = tmp("node0", [P, TILES])
            jrow = tmp("jrow", [P, TILES])
            kcol = tmp("kcol", [P, PCH])
            cmp = tmp("cmp", [P, TILES * ECH])
            cnt = tmp("cnt", [P, 2 * TILES])
            bounds = tmp("bounds", [P, 2 * TILES])
            npair = tmp("npair", [P, TILES])
            kend = tmp("kend", [P, TILES])
            toff = tmp("toff", [P, TILES])
            jk = tmp("jk", [P, PCH])
            tk = tmp("tk", [P, PCH])
            joff = tmp("joff", [P, PCH], I32)
            w_in = sem("w_in")
            bc_in = sem("bc_in")
            copied = sem("copied")
            tail_in = sem("tail_in")
            tail_out = sem("tail_out")
            lists_kept = sem("lists_kept")
            ends_in = sem("ends_in")
            padded = sem("padded")
            consts = sem("consts")
            su_pe = sem("su_pe")
            su_act = sem("su_act")
            su_dve = sem("su_dve")
            counted = sem("counted")
            counts_sum = sem("counts_sum")
            tk_ready = sem("tk_ready")
            joff_out, joff_in = sem("joff_out"), sem("joff_in")
            su_pool = sem("su_pool")
            with nc.Block() as block:
                @block.sync
                def _(sp):
                    full, whole = (ETILES - 1) * P, (ETILES - 1) // P
                    sp.wait_ge(padded, 2)
                    dst_full = dst[0:full].rearrange("(t e) -> t e", e=P)
                    sp.dma_start(ends[:, 0:whole, :], dst_full[0:whole * P, :].rearrange("(c p) e -> p c e", p=P)).then_inc(ends_in, 16)
                    left = ETILES - 1 - whole * P
                    sp.dma_start(ends[0:left, whole, :], dst_full[whole * P:ETILES - 1, :]).then_inc(ends_in, 16)
                    sp.dma_start(ends[left:left + 1, whole, 0:ELAST],
                                 dst[full:NE].rearrange("(a b) -> a b", a=1)).then_inc(ends_in, 16)
                    for q, (s, rows) in enumerate(((src, src_rows), (dst, dst_rows))):
                        sp.dma_start(last_rows[0:1, q, 0:ELAST],
                                     s[full:NE].rearrange("(a b) -> a b", a=1)).then_inc(tail_in, 16)
                        sp.dma_start(rows[0:ETILES - 1, :],
                                     s[0:full].rearrange("(a b) -> a b", b=P)).then_inc(copied, 16)
                    sp.wait_ge(tail_in, 32)
                    for q, rows in enumerate((src_rows, dst_rows)):
                        sp.dma_start(rows[ETILES - 1:ETILES, :], last_rows[0:1, q, :]).then_inc(tail_out, 16)
                    sp.dma_start(dst_rows[ETILES:ETILES + 1, :], end_row[0:1, :]).then_inc(tail_out, 16)
                    for q in range(4):
                        a, z = q * XCH, (q + 1) * XCH
                        sp.dma_start(work[:, a:z, 0:C], x[a * P:z * P, :].rearrange("(t p) c -> p t c", p=P)).then_inc(x_in[q // 2], 16)
                    sp.wait_ge(last_zero, 1)
                    sp.dma_start(work[0:LAST, TILES - 1, 0:C], x[(TILES - 1) * P:N, :]).then_inc(x_in[1], 16)
                    sp.wait_ge(copied, 32)
                    sp.wait_ge(tail_out, 48)
                    sp.sem_inc(lists_kept, 1)
                    sp.wait_ge(tk_ready, 2)
                    with nc.allow_non_contiguous_dma(reason="896 numbers"):
                        sp.dma_start(pair_acc_d.rearrange("(c p) -> p c", p=P), joff[:, :]).then_inc(joff_out, 16)
                    sp.wait_ge(joff_out, 16)
                    sp.dma_start(pair_acc[0:1, :], pair_acc_d.rearrange("(a b) -> a b", a=1)).then_inc(joff_in, 16)
                    sp.wait_ge(joff_in, 16)

                @block.scalar
                def _(act):
                    act.dma_start(wext[:, :, 0:C], gnn_W.rearrange("(c p) n -> p c n", p=P)).then_inc(w_in, 16)
                    act.dma_start(kv_raw, Wqkv[INNER:3 * INNER, :].rearrange("(r p) c -> p r c", p=P)).then_inc(w_in, 16)
                    act.dma_start(wout_raw, Wout.rearrange("(r p) c -> p r c", p=P)).then_inc(w_in, 16)
                    act.dma_start(wq[:, :, :], Wqkv[0:INNER, :].rearrange("(r p) c -> p r c", p=P)).then_inc(w_in, 16)
                    act.dma_start(bout_bc[:, :], bout.partition_broadcast(P)).then_inc(w_in, 16)
                    for q, a in enumerate((a_src, a_dst)):
                        act.dma_start(a_bc[:, q, :], a.rearrange("h d -> (h d)").partition_broadcast(P)).then_inc(bc_in, 16)
                    for f in range(6):
                        act.wait_ge(su_pe, f + 1)
                        to = wkvT[:, f // 2, (f % 2) * 512:(f % 2 + 1) * 512] if f < 4 else \
                            woutT[:, 2 * (f - 4):2 * (f - 3), :].rearrange("p a c -> p (a c)")
                        act.copy(to, bank[f][:, :]).then_inc(su_act, 1)

                @block.gpsimd
                def _(pool):
                    steps = Steps(pool, su_pool)
                    steps.done(pool.memset(last_rows[:, 0, :], 0))
                    steps.done(pool.memset(last_rows[:, 1, :], NO_NODE))
                    steps.done(pool.memset(end_row[:, :], NO_NODE))
                    pool.sem_inc(padded, 1)
                    pool.memset(work[:, TILES - 1, :], 0.0).then_inc(last_zero, 1)
                    steps.done(pool.memset(ones[:, :], 1.0))
                    steps.done(pool.memset(ident[:, :], 0.0))
                    steps.done(pool.affine_select(out=ident[:, :], in_=ident[:, :], compare_op=ALU.not_equal,
                                                  fill=1.0, base=0, pattern=[[-1, P]], channel_multiplier=1))
                    steps.done(pool.affine_select(out=below[:, :], in_=ones[:, :], compare_op=ALU.is_gt,
                                                  fill=0.0, base=0, pattern=[[1, P]], channel_multiplier=-1))
                    kw = dict(allow_small_or_imprecise_dtypes=True)
                    steps.done(pool.iota(iota[:, :], pattern=[[1, P]], base=0, channel_multiplier=0, **kw))
                    steps.done(pool.iota(node0[:, :], pattern=[[P, TILES]], base=0, channel_multiplier=0, **kw))
                    steps.done(pool.iota(jrow[:, :], pattern=[[1, TILES]], base=0, channel_multiplier=0, **kw))
                    steps.done(pool.iota(kcol[:, :], pattern=[[P, PCH]], base=0, channel_multiplier=1, **kw))
                    pool.sem_inc(consts, 1)
                    pool.memset(acc_f, 0.0).then_inc(su_pool, 1)
                    pool.wait_ge(lists_kept, 1)
                    pool.wait_ge(tk_ready, 1)
                    for c in range(PCH):
                        at = bass.IndirectOffsetOnAxis(ap=tki[:, c:c + 1], axis=0)
                        pool.indirect_dma_start(dst_g[:, c, :], None, dst_rows, at).then_inc(edges_got, 16)
                        pool.indirect_dma_start(src_g[:, c, :], None, src_rows, at).then_inc(edges_got, 16)

                @block.tensor
                def _(pe):
                    pe.wait_ge(w_in, 80)
                    pe.wait_ge(consts, 1)
                    for f in range(4):
                        for q in range(4):
                            t = pe.transpose(bank[f][:, q * P:(q + 1) * P],
                                             kv_raw[:, (f % 2) * 4 + q, (f // 2) * P:(f // 2 + 1) * P], ident[:, :])
                        t.then_inc(su_pe, 1)
                    pe.wait_ge(counted, 1)
                    pe.matmul(bank[6][:, 0:2 * TILES], ones[:, :], cnt[:, :], start=True, stop=True).then_inc(counts_sum, 1)
                    for f in range(2):
                        for q in range(2):
                            for c in range(2):
                                t = pe.transpose(bank[4 + f][:, q * C + c * P:q * C + (c + 1) * P],
                                                 wout_raw[:, c, (2 * f + q) * P:(2 * f + q + 1) * P], ident[:, :])
                        t.then_inc(su_pe, 1)

                @block.vector
                def _(dve):
                    steps = Steps(dve, su_dve)
                    steps.done(dve.memset(ends[:, ECH - 1, :], NO_NODE))
                    dve.sem_inc(padded, 1)
                    dve.wait_ge(consts, 1)
                    dve.wait_ge(ends_in, 48)
                    for q in range(2):
                        steps.done(dve.tensor_copy(endsf[:, :, q], ends[:, :, q * (P - 1)]))
                    cmp_t = cmp[:, 0:TILES * ECH].rearrange("p (j c) -> p j c", c=ECH)
                    steps.done(dve.tensor_tensor(cmp_t, over(endsf[:, :, 1], TILES), spread(node0[:, :], ECH), ALU.is_lt))
                    steps.done(dve.tensor_reduce(cnt[:, 0:TILES], cmp_t, X, ALU.add))
                    steps.done(dve.tensor_scalar(node0[:, :], node0[:, :], float(P), None, ALU.add))
                    steps.done(dve.tensor_tensor(cmp_t, over(endsf[:, :, 0], TILES), spread(node0[:, :], ECH), ALU.is_lt))
                    dve.tensor_reduce(cnt[:, TILES:2 * TILES], cmp_t, X, ALU.add).then_inc(counted, 1)
                    dve.wait_ge(counts_sum, 1)
                    steps.done(dve.tensor_copy(bounds[:, :], bank[6][:, 0:2 * TILES]))
                    ts, te = bounds[:, 0:TILES], bounds[:, TILES:2 * TILES]
                    steps.done(dve.scalar_tensor_tensor(te, ts, 1.0, te, ALU.add, ALU.max))
                    steps.done(dve.tensor_tensor(npair[:, :], te, ts, ALU.subtract))
                    steps.done(dve.tensor_tensor_scan(kend[:, :], ones[:, 0:TILES], npair[:, :], 0.0, ALU.mult, ALU.add))
                    steps.done(dve.tensor_tensor(toff[:, :], te, kend[:, :], ALU.subtract))
                    cmp_k = cmp[:, 0:PCH * TILES].rearrange("p (c j) -> p c j", j=TILES)
                    steps.done(dve.tensor_tensor(cmp_k, over(kend[:, :], PCH), spread(kcol[:, :], TILES), ALU.is_le))
                    steps.done(dve.tensor_reduce(jk[:, :], cmp_k, X, ALU.add))
                    steps.done(dve.tensor_tensor(cmp_k, over(jrow[:, :], PCH), spread(jk[:, :], TILES), ALU.is_equal))
                    steps.done(dve.tensor_tensor(cmp_k, cmp_k, over(toff[:, :], PCH), ALU.mult))
                    steps.done(dve.tensor_reduce(tk[:, :], cmp_k, X, ALU.add))
                    steps.done(dve.tensor_tensor(tk[:, :], tk[:, :], kcol[:, :], ALU.add))
                    steps.done(dve.tensor_scalar(tki[:, :], tk[:, :], float(ETILES - 1), None, ALU.min))
                    dve.sem_inc(tk_ready, 1)
                    steps.done(dve.tensor_scalar(joff[:, :], jk[:, :], float(TILES - 1), float(EXT), ALU.min, ALU.mult))
                    dve.sem_inc(tk_ready, 1)
                    steps.done(dve.tensor_scalar(jbase[:, :], jk[:, :], -float(P), None, ALU.mult))
                    dve.wait_ge(w_in, 80)
                    dve.wait_ge(bc_in, 32)
                    for c in range(2):
                        for q in range(2):
                            steps.done(dve.tensor_tensor(prod, wext[:, c, 0:C], a_bc[:, q, :], ALU.mult))
                            steps.done(dve.tensor_reduce(wext[:, c, C + HEADS * q:C + HEADS * (q + 1)],
                                                         prod.rearrange("p (h d) -> p h d", d=HD), X, ALU.add))
                    early = 2 * XCH // G
                    for half, (a, z) in enumerate(((0, early), (early, GROUPS))):
                        dve.wait_ge(x_in[half], 32 + 16 * half)
                        with dve.Fori(a, z) as g:
                            for i in range(G):
                                t = g * G + i
                                dve.bn_stats(stats[:, bass.ds(t, 1), :].rearrange("p a c -> p (a c)"),
                                             work_f[:, bass.ds(t * EXT, C)]).then_inc(stated, 1)
                    dve.wait_ge(stated, TILES)

        with ExitStack() as stage:
            def tmp(name, shape, dt=F32):
                return stage.enter_context(nc.sbuf_tensor(name, shape, dt))

            xn = tmp("xn", [P, 2, C])
            xnT = big[:, 0:4 * C].rearrange("p (m c) -> p m c", m=4)
            xb = big[:, 4 * C:8 * C].rearrange("p (m c) -> p m c", m=4)
            falls = big[:, 2048:2048 + ETILES]
            pairs_of = tmp("pairs_of", [P, 2, ETILES], I32)
            order_in = sem("order_in")
            cols_f = sem("cols_f")
            cols_t = sem("cols_t")
            cl_dve = sem("cl_dve")
            xb_ready = sem("xb_ready")
            sqrted = sem("sqrted")
            var_ready = sem("var_ready")
            pj_dve = sem("pj_dve")
            xn_ready = sem("xn_ready")
            xn_turned = sem("xn_turned")
            xnT_ready = sem("xnT_ready")
            kept = [sem(f"kept{m}") for m in range(4)]
            proj_done = sem("proj_done")
            proj_kept = sem("proj_kept")
            with nc.Block() as block:
                @block.sync
                def _(sp):
                    def keep(t0, m):
                        t = t0 + m
                        sp.wait_ge(xb_ready, t + 1)
                        sp.dma_start(xb_d[bass.ds(t * P, P), :], xb[:, m, :]).then_inc(kept[m], 16)
                        sp.wait_ge(xnT_ready, t + 1)
                        sp.dma_start(xnT_d[bass.ds(t, 1), :, :].rearrange("a p c -> p (a c)"),
                                     xnT[:, m, :]).then_inc(kept[m], 16)

                    flat_dst = dst_rows.rearrange("t e -> (t e)")
                    for q in range(2):
                        sp.dma_start(pairs_of[:, q, :], flat_dst[q:q + ETILES * P].rearrange("(p n) -> p n", p=P)).then_inc(order_in, 16)
                    by_four(sp, keep)
                    for m in range(4):
                        sp.wait_ge(kept[m], 32 * (TILES // 4 + (m == 0)))

                @block.gpsimd
                def _(pool):
                    def add_bout(t0, m):
                        t = t0 + m
                        if not starts(t0):
                            pool.wait_ge(kept[m], 8 * t0)
                        pool.tensor_tensor(xb[:, m, :], work_f[:, bass.ds(t * EXT, C)], bout_bc[:, :], ALU.add).then_inc(xb_ready, 1)

                    by_four(pool, add_bout)

                @block.vector
                def _(dve):
                    steps = Steps(dve, pj_dve)
                    layer_stats(dve, steps)
                    dve.sem_inc(var_ready, 1)
                    dve.wait_ge(sqrted, 1)
                    steps.done(dve.reciprocal(rstd[:, :], rstd[:, :]))
                    dve.sem_inc(xn_turned, 2)

                    def norm(t0, b):
                        t = t0 + b
                        dve.wait_ge(xn_turned, t + 1)
                        dve.tensor_scalar(xn[:, b, :], work_f[:, bass.ds(t * EXT, C)], mean[:, bass.ds(t, 1)],
                                          rstd[:, bass.ds(t, 1)], ALU.subtract, ALU.mult).then_inc(xn_ready, 1)

                    each_tile(dve, norm)
                    steps = Steps(dve, cl_dve)
                    dve.wait_ge(order_in, 32)
                    steps.done(dve.tensor_tensor(pairs_of[:, 0, :], pairs_of[:, 0, :], pairs_of[:, 1, :], ALU.is_gt))
                    steps.done(dve.tensor_copy(falls, pairs_of[:, 0, :]))
                    steps.done(dve.tensor_reduce(unsorted[:, :], falls, X, ALU.add))
                    dve.wait_ge(edges_got, 32 * PCH)
                    for c in range(PCH):
                        steps.done(dve.tensor_scalar(dst_f[:, c, :], dst_g[:, c, :], jbase[:, c:c + 1], None, ALU.add))
                    steps.done(dve.tensor_copy(src_f[:, :, :], src_g[:, :, :]))
                    dve.sem_inc(cols_f, 1)
                    dve.wait_ge(cols_t, 2)
                    half = PCH * P - 512
                    steps.done(dve.tensor_copy(dst_cols[:, 0:512], bank[4][:, :]))
                    steps.done(dve.tensor_copy(dst_cols[:, 512:PCH * P], bank[5][:, 0:half]))
                    steps.done(dve.memset(dst_cols[:, PCH * P:PCH * P + 2], -1.0))
                    steps.done(dve.tensor_copy(src_cols[:, 0:512], bank[6][:, :]))
                    steps.done(dve.tensor_copy(src_cols[:, 512:PCH * P], bank[7][:, 0:half]))

                @block.tensor
                def _(pe):
                    pe.sem_inc(proj_kept, 2)

                    def turn(t, b):
                        pe.wait_ge(xn_ready, t + 1)
                        for c in range(2):
                            r = pe.transpose(bank[b][:, c * P:(c + 1) * P], xn[:, b, c * P:(c + 1) * P], ident[:, :])
                        r.then_inc(xn_turned, 1)

                    def step(t0, m):
                        t, b = t0 + m, m % 2
                        if not is_last(t0):
                            turn(t + 1, 1 - b)
                        pe.wait_ge(xnT_ready, t + 1)
                        pe.wait_ge(proj_kept, t + 1)
                        for c in range(2):
                            r = pe.matmul(bank[2 + b][:, 0:EXT], xnT[:, m, c * P:(c + 1) * P], wext[:, c, :],
                                          start=c == 0, stop=c == 1)
                        r.then_inc(proj_done, 1)

                    turn(0, 0)
                    by_four(pe, step)
                    pe.wait_ge(cols_f, 1)
                    for q, t_f in enumerate((dst_f, src_f)):
                        for c in range(PCH):
                            t = pe.transpose(bank[4 + 2 * q + c // 4][:, (c % 4) * P:(c % 4 + 1) * P], t_f[:, c, :], ident[:, :])
                        t.then_inc(cols_t, 1)

                @block.scalar
                def _(act):
                    act.wait_ge(var_ready, 1)
                    act.activation(rstd[:, :], rstd[:, :], ACT.Sqrt).then_inc(sqrted, 1)

                    def move_in(t, m):
                        act.wait_ge(xn_turned, t + 3)
                        if not (isinstance(t, int) and t < 4):
                            act.wait_ge(kept[m], 8 * (t - m))
                        act.copy(xnT[:, m, :], bank[m % 2][:, 0:C]).then_inc(xnT_ready, 1)

                    def step(t0, m):
                        t = t0 + m
                        if not is_last(t0):
                            move_in(t + 1, (m + 1) % 4)
                        act.wait_ge(proj_done, t + 1)
                        act.wait_ge(xb_ready, t + 1)
                        act.copy(work_f[:, bass.ds(t * EXT, EXT)], bank[2 + m % 2][:, 0:EXT]).then_inc(proj_kept, 1)

                    move_in(0, 0)
                    by_four(act, step)

        with ExitStack() as stage:
            def tmp(name, shape, dt=F32):
                return stage.enter_context(nc.sbuf_tensor(name, shape, dt))

            ext2 = tmp("ext2", [P, 2 * HEADS])
            ext1 = tmp("ext1", [2 * HEADS, 1])
            diag = tmp("diag", [2 * HEADS, 2 * HEADS])
            amax = tmp("amax", [P, 2 * HEADS])
            wexp = tmp("wexp", [P, TILES, HEADS])
            wg_dve = sem("wg_dve")
            ext_ready, ext_turned = sem("ext_ready"), sem("ext_turned")
            diag_ready, amax_ready = sem("diag_ready"), sem("amax_ready")
            wexp_in, wexp_out = sem("wexp_in"), sem("wexp_out")
            rows_ready = sem("rows_ready")
            alpha_kept = sem("alpha_kept")
            table_out = sem("table_out")
            pool_rows = sem("pool_rows")
            falls_summed = sem("falls_summed")
            width, widest = tmp("width", [1, HEADS]), tmp("widest", [1, 1])
            FOR_POOL = 2
            wexp_f = wexp[:, :, :].rearrange("p t h -> p (t h)")

            def weigh_rows(engine, places, ready):
                with engine.Fori(0, GROUPS) as g:
                    for i in places:
                        t = g * G + i
                        rows = work_f[:, bass.ds(t * EXT, C)].rearrange("p (h d) -> p h d", d=HD)
                        engine.tensor_tensor(rows, rows, spread(wexp_f[:, bass.ds(t * HEADS, HEADS)], HD),
                                             ALU.mult).then_inc(ready, 1)

            with nc.Block() as block:
                @block.gpsimd
                def _(pool):
                    pool.wait_ge(wexp_out, 1)
                    pool.tensor_copy(work[:, :, C:C + HEADS], wexp[:, :, :]).then_inc(alpha_kept, 1)
                    weigh_rows(pool, range(FOR_POOL), pool_rows)

                @block.vector
                def _(dve):
                    steps = Steps(dve, wg_dve)
                    alpha = work[:, :, C:C + HEADS]
                    steps.done(dve.tensor_reduce(ext2[:, 0:HEADS], alpha.rearrange("p t h -> p h t"), X, ALU.max))
                    steps.done(dve.tensor_scalar(wexp[:, :, :], alpha, -1.0, None, ALU.mult))
                    dve.tensor_reduce(ext2[:, HEADS:2 * HEADS], wexp[:, :, :].rearrange("p t h -> p h t"), X,
                                      ALU.max).then_inc(ext_ready, 1)
                    dve.wait_ge(ext_turned, 1)
                    steps.done(dve.tensor_reduce(ext1[:, :], bank[0][0:2 * HEADS, 0:P], X, ALU.max))
                    dve.tensor_scalar(diag[:, :], ident[0:2 * HEADS, 0:2 * HEADS], ext1[:, 0:1], None,
                                      ALU.mult).then_inc(diag_ready, 1)
                    dve.wait_ge(amax_ready, 1)
                    steps.done(dve.tensor_copy(amax[:, :], bank[1][:, 0:2 * HEADS]))
                    steps.done(dve.tensor_tensor(width[:, :], amax[0:1, 0:HEADS], amax[0:1, HEADS:2 * HEADS], ALU.add))
                    steps.done(dve.tensor_reduce(widest[:, :], width[:, :], X, ALU.max))
                    steps.done(dve.tensor_scalar(widest[:, :], widest[:, :], SPREAD, None, ALU.is_gt))
                    dve.wait_ge(falls_summed, 1)
                    steps.done(dve.tensor_tensor(widest[:, :], widest[:, :], bank[2][0:1, 0:1], ALU.add))
                    steps.done(dve.tensor_scalar(general[:, :], widest[:, :], 1.0, None, ALU.min))
                    dve.tensor_tensor(wexp[:, :, :], alpha, over(amax[:, 0:HEADS], TILES), ALU.subtract).then_inc(wexp_in, 1)
                    dve.wait_ge(wexp_out, 1)
                    weigh_rows(dve, range(FOR_POOL, G), rows_ready)
                    for c in range(2):
                        grouped = wkvT[:, c, :].rearrange("p (g d) -> p g d", d=MD)
                        steps.done(dve.tensor_reduce(hmean[:, c, :], grouped, X, ALU.add))
                        steps.done(dve.tensor_scalar(hmean[:, c, :], hmean[:, c, :], 1.0 / MD, None, ALU.mult))
                        steps.done(dve.tensor_tensor(grouped, grouped, spread(hmean[:, c, :], MD), ALU.subtract))

                @block.tensor
                def _(pe):
                    pe.matmul(bank[2][0:1, 0:1], unsorted[:, :], ones[:, 0:1], start=True, stop=True).then_inc(falls_summed, 1)
                    pe.wait_ge(ext_ready, 1)
                    pe.transpose(bank[0][0:2 * HEADS, 0:P], ext2[:, :], ident[:, :]).then_inc(ext_turned, 1)
                    pe.wait_ge(diag_ready, 1)
                    pe.matmul(bank[1][:, 0:2 * HEADS], ones[0:2 * HEADS, :], diag[:, :], start=True,
                              stop=True).then_inc(amax_ready, 1)

                @block.scalar
                def _(act):
                    act.wait_ge(wexp_in, 1)
                    act.activation(wexp[:, :, :], wexp[:, :, :], ACT.Exp).then_inc(wexp_out, 1)

                @block.sync
                def _(sp):
                    tab = table.rearrange("(t p) c -> p t c", p=P)
                    sp.wait_ge(alpha_kept, 1)
                    for g in range(GROUPS):
                        sp.wait_ge(rows_ready, (g + 1) * (G - FOR_POOL))
                        sp.wait_ge(pool_rows, (g + 1) * FOR_POOL)
                        sp.dma_start(tab[:, g * G:(g + 1) * G, :], work[:, g * G:(g + 1) * G, 0:ROW]).then_inc(table_out, 16)
                    sp.wait_ge(table_out, 16 * GROUPS)

        COUNTED = 16 * ROUNDS
        got = big[:, 0:UNROLL * ROW].rearrange("p (s c) -> p s c", c=ROW)
        with ExitStack() as stage:
            def tmp(name, shape, dt=F32):
                return stage.enter_context(nc.sbuf_tensor(name, shape, dt))

            HALF = UNROLL // 2
            idx = tmp("idx", [P, UNROLL], I32)
            onehot = tmp("onehot", [P, 4, P])
            kv_x = tmp("kv_x", [P, C])
            squares = tmp("squares", [P, 2 * INNER])
            kv_var = tmp("kv_var", [P, 2 * MH])
            kv_r = tmp("kv_r", [P, 2 * MH])
            k_scale = tmp("k_scale", [P, MH])
            k_n = tmp("k_n", [P, INNER])
            v_n = tmp("v_n", [P, INNER])
            zeros = tmp("zeros", [P, 512])
            dotsS = tmp("dotsS", [P, 4, P])
            g1T = tmp("g1T", [P, 4, C])
            idx_ready = sem("idx_ready")
            row_got = [sem(f"row_got{s}") for s in range(UNROLL)]
            rows_used = sem("rows_used")
            onehot_ready = sem("onehot_ready")
            summed = sem("summed")
            kvx_in = sem("kvx_in")
            kv_done = sem("kv_done")
            squared, v_moved = sem("squared"), sem("v_moved")
            var_in, var_out = sem("var_in"), sem("var_out")
            k_ready = sem("k_ready")
            dots_done = sem("dots_done")
            eg_dve = sem("eg_dve")
            zeros_set = sem("zeros_set")
            dS_ready, g1_done, g1_moved, g_done, g_moved = (sem(n) for n in (
                "dS_ready", "g1_done", "g1_moved", "g_done", "g_moved"))
            KB, VB, DB = bank[4], bank[5], bank[6]
            with nc.Block() as block:
                @block.gpsimd
                def _(pool):
                    def gathers(r):
                        for s in range(UNROLL):
                            if s % HALF == 0:
                                pool.wait_ge(idx_ready, 2 * r + 1 + s // HALF)
                            pool.wait_ge(rows_used, r * UNROLL + s + 1)
                            pool.sem_inc(pool_on, 1)
                            pool.indirect_dma_start(got[:, s, :], None, table,
                                                    bass.IndirectOffsetOnAxis(ap=idx[:, s:s + 1], axis=0)
                                                    ).then_inc(row_got[s], 16)

                    with pool.Fori(0, ROUNDS) as r:
                        gathers(r)

                @block.scalar
                def _(act):
                    def indices(r):
                        for h in range(2):
                            act.wait_ge(rows_used, r * UNROLL + (h + 1) * HALF)
                            act.copy(idx[:, h * HALF:(h + 1) * HALF],
                                     src_cols[:, bass.ds(r * UNROLL + h * HALF, HALF)]).then_inc(idx_ready, 1)

                    def keys_values(r):
                        act.wait_ge(kv_done, r + 1)
                        act.activation(squares[:, 0:INNER], KB[:, :], ACT.Square)
                        act.activation(squares[:, INNER:2 * INNER], VB[:, :], ACT.Square).then_inc(squared, 1)
                        act.wait_ge(dots_done, r + 1)
                        act.copy(v_n[:, :], VB[:, :]).then_inc(v_moved, 1)
                        act.wait_ge(var_in, r + 1)
                        act.activation(kv_r[:, :], kv_var[:, :], ACT.Sqrt).then_inc(var_out, 1)

                    with act.Fori(0, TILES) as r:
                        indices(r)
                        keys_values(r)
                    with act.Fori(TILES, ROUNDS) as r:
                        indices(r)

                @block.sync
                def _(sp):
                    def load(r):
                        sp.dma_start(kv_x[:, :], xnT_d[bass.ds(r, 1), :, :].rearrange("a p c -> p (a c)")).then_inc(kvx_in, 16)

                    load(0)
                    with sp.Fori(1, TILES) as r:
                        sp.wait_ge(kv_done, r)
                        load(r)

                @block.tensor
                def _(pe):
                    pe.sem_inc(rows_used, UNROLL)
                    pe.sem_inc(summed, 4)
                    pe.sem_inc(k_ready, 1)
                    pe.wait_ge(zeros_set, 1)
                    pe.matmul(DB[:, :], zeros[:, 0:P], zeros[:, :], start=True, stop=False, skip_group_check=True).then_inc(dots_done, 1)

                    def sum_rows(r, s):
                        k = r * UNROLL + s
                        pe.wait_ge(onehot_ready, k + 1)
                        pe.wait_ge(row_got[s], r * 16 + 16)
                        pe.wait_ge(summed, k + 1)
                        pe.matmul(bank[s % 4][:, 0:ROW], onehot[:, s % 4, :], got[:, s, :], start=True,
                                  stop=True).then_inc(rows_used, 1)

                    def project_kv(r):
                        pe.wait_ge(kvx_in, r * 16 + 16)
                        pe.wait_ge(k_ready, r + 1)
                        for o, b in ((0, KB), (INNER, VB)):
                            for c in range(2):
                                m = pe.matmul(b[:, :], kv_x[:, c * P:(c + 1) * P], wkvT[:, c, o:o + INNER],
                                              start=c == 0, stop=c == 1)
                        m.then_inc(kv_done, 1)

                    def dots(r):
                        pe.wait_ge(k_ready, r + 2)
                        pe.wait_ge(v_moved, r + 1)
                        for q in range(4):
                            m = pe.matmul(DB[:, q * P:(q + 1) * P], k_n[:, q * P:(q + 1) * P], v_n[:, q * P:(q + 1) * P],
                                          start=False, stop=False, skip_group_check=True)
                        m.then_inc(dots_done, 1)

                    with pe.Fori(0, TILES) as r:
                        project_kv(r)
                        for s in range(UNROLL):
                            sum_rows(r, s)
                        dots(r)
                    pe.matmul(DB[:, :], zeros[:, 0:P], zeros[:, :], start=False, stop=True, skip_group_check=True).then_inc(dots_done, 1)
                    pe.wait_ge(dS_ready, 1)
                    for q in range(4):
                        m = pe.matmul([KB, VB][q // 2][:, (q % 2) * C:(q % 2 + 1) * C], dotsS[:, q, :], wq[:, q, :],
                                      start=True, stop=True)
                    m.then_inc(g1_done, 1)
                    pe.wait_ge(g1_moved, 1)
                    for c in range(2):
                        for q in range(4):
                            m = pe.matmul(bank[7][:, c * C:(c + 1) * C], g1T[:, q, c * P:(c + 1) * P], woutT[:, q, :],
                                          start=q == 0, stop=q == 3)
                    m.then_inc(g_done, 1)
                    with pe.Fori(TILES, ROUNDS) as r:
                        for s in range(UNROLL):
                            sum_rows(r, s)

                @block.vector
                def _(dve):
                    dve.memset(zeros[:, :], 0.0).then_inc(zeros_set, 1)
                    dve.memset(dotsS[:, :, :], 0.0).then_inc(zeros_set, 1)
                    regs = [dve.alloc_register(f"at{s}") for s in range(UNROLL)]

                    def targets(k, s):
                        dve.wait_ge(rows_used, k + UNROLL - 3)
                        dve.tensor_scalar(onehot[:, s % 4, :], iota[:, :], dst_cols[:, bass.ds(k, 1)], None,
                                          ALU.is_equal).then_inc(onehot_ready, 1)

                    def add(k, s):
                        at = dve.snap(regs[s], min_val=0, max_val=(TILES - 1) * EXT)
                        to = acc_f[:, bass.ds(at, ROW)]
                        dve.wait_ge(rows_used, k + UNROLL + 1)
                        dve.wait_ge(summed, k + 4)
                        dve.tensor_tensor(to, to, bank[s % 4][:, 0:ROW], ALU.add).then_inc(summed, 1)

                    steps = Steps(dve, eg_dve)

                    def kv_var_of(r):
                        dve.wait_ge(squared, r + 1)
                        steps.done(dve.tensor_reduce(kv_var[:, :], squares[:, :].rearrange("p (g d) -> p g d", d=MD), X, ALU.add))
                        dve.tensor_scalar(kv_var[:, :], kv_var[:, :], 1.0 / MD, EPS, ALU.mult, ALU.add).then_inc(var_in, 1)

                    def scale_k(r):
                        dve.wait_ge(var_out, r + 1)
                        steps.done(dve.reciprocal(kv_r[:, :], kv_r[:, :]))
                        steps.done(dve.tensor_tensor(k_scale[:, :], kv_r[:, 0:MH], kv_r[:, MH:2 * MH], ALU.mult))
                        dve.wait_ge(v_moved, r + 1)
                        dve.tensor_tensor(k_n[:, :].rearrange("p (g d) -> p g d", d=MD),
                                          KB[:, :].rearrange("p (g d) -> p g d", d=MD), spread(k_scale[:, :], MD),
                                          ALU.mult).then_inc(k_ready, 1)

                    targets(0, 0)
                    targets(1, 1)

                    def round_(r, with_kv):
                        dve.load(regs, pair_acc[0:1, bass.ds(r * UNROLL, UNROLL)])
                        for s in range(UNROLL):
                            targets(r * UNROLL + s + 2, s + 2)
                            add(r * UNROLL + s, s)
                            if with_kv and s == UNROLL // 2:
                                kv_var_of(r)
                            if with_kv and s == UNROLL // 2 + 4:
                                scale_k(r)

                    with dve.Fori(0, TILES) as r:
                        steps.at(r * 3)
                        round_(r, True)
                    dve.wait_ge(dots_done, TILES + 2)
                    dve.wait_ge(zeros_set, 2)
                    for q in range(4):
                        for h in range(2):
                            d = dve.tensor_scalar(dotsS[h * MD:(h + 1) * MD, q, h * MD:(h + 1) * MD],
                                                  DB[h * MD:(h + 1) * MD, q * P + h * MD:q * P + (h + 1) * MD],
                                                  1.0 / N, None, ALU.mult)
                    d.then_inc(dS_ready, 1)
                    dve.wait_ge(g1_done, 1)
                    for q, b in enumerate((KB, VB)):
                        d = dve.tensor_copy(g1T[:, 2 * q:2 * q + 2, :].rearrange("p a c -> p (a c)"), b[:, :])
                    d.then_inc(g1_moved, 1)
                    dve.wait_ge(g_done, 1)
                    dve.tensor_copy(mixG[:, :, :].rearrange("p a c -> p (a c)"), bank[7][:, :]).then_inc(g_moved, 1)
                    with dve.Fori(TILES, ROUNDS) as r:
                        round_(r, False)
                    dve.wait_ge(summed, PAIRS + 4)


        raw_d = dram("raw_d", (TILES * P, EXT))
        max_d = dram("max_d", (TILES * P, HEADS))
        sum_d = dram("sum_d", (TILES * P, ROW))
        with ExitStack() as stage:
            def tmp(name, shape, dt=F32):
                return stage.enter_context(nc.sbuf_tensor(name, shape, dt))

            src_i, dst_i = tmp("src_i", [P, 1], I32), tmp("dst_i", [P, 1], I32)
            goal_i = tmp("goal_i", [P, 1], I32)
            dst_1 = tmp("dst_1", [P, 1])
            not_first = tmp("not_first", [P, 1])
            above = tmp("above", [P, P])
            equal = tmp("equal", [P, P])
            other = tmp("other", [P, P])
            dst_diag = tmp("dst_diag", [P, P])
            of_src, of_dst = tmp("of_src", [P, EXT]), tmp("of_dst", [P, EXT])
            xT_any = tmp("xT_any", [P, C])
            top = tmp("top", [P, HEADS])
            logit = tmp("logit", [P, HEADS])
            best = tmp("best", [P, HEADS])
            logit_diag = big[:, 0:HEADS * P].rearrange("p (h j) -> p h j", h=HEADS)
            spread_out = big[:, HEADS * P:2 * HEADS * P].rearrange("p (h j) -> p h j", h=HEADS)
            sums, weighted = tmp("sums", [P, ROW]), tmp("weighted", [P, ROW])
            any_pool, any_dve, any_pe, any_act = (sem(n) for n in ("any_pool", "any_dve", "any_pe", "any_act"))
            any_dma = [sem("any_dma0"), sem("any_dma1")] + row_got[UNROLL - 5:UNROLL]
            PRESET, MAX_STEPS, SUM_STEPS = 3, 14, 12
            FAR = 1e30

            def taken(engine, name):
                reg = engine.alloc_register(f"general_{name}")
                engine.load(reg, general[0:1, 0:1])
                return engine.If(engine.snap(reg, min_val=0, max_val=1))

            with nc.Block() as block:
                @block.gpsimd
                def _(pool):
                    with taken(pool, "pool"):
                        used = [0] * len(any_dma)
                        base = [0] * 2 + [COUNTED] * 5
                        now = [0, 0]

                        def moved(dma):
                            i, now[1] = now[1], now[1] + 1
                            dma.then_inc(any_dma[i], 16)
                            pool.wait_ge(any_dma[i], 16 * now[0] + (16 * used[i] + 16 + base[i]))
                            pool.sem_inc(pool_on, 1)

                        def at(round_):
                            now[0], now[1] = round_, 0

                        def looped(rounds, dmas):
                            assert now[1] == dmas
                            for i in range(dmas):
                                used[i] += rounds

                        pool.wait_ge(any_dve, PRESET)
                        with pool.Fori(0, TILES) as t:
                            at(t)
                            moved(pool.dma_start(max_d[bass.ds(t * P, P), :], top[:, :]))
                            moved(pool.dma_start(sum_d[bass.ds(t * P, P), :], sums[:, :]))
                            moved(pool.dma_start(xT_any[:, :], xnT_d[bass.ds(t, 1), :, :].rearrange("a p c -> p (a c)")))
                            pool.sem_inc(any_pool, 1)
                            pool.wait_ge(any_dve, t + PRESET + 1)
                            pool.sem_inc(pool_on, 1)
                            moved(pool.dma_start(raw_d[bass.ds(t * P, P), :], of_src[:, :]))

                        def fetch(e):
                            with nc.allow_non_contiguous_dma(reason="128 numbers"):
                                moved(pool.dma_start(src_i[:, :], src_rows[bass.ds(e, 1), :].rearrange("a p -> p a")))
                                moved(pool.dma_start(dst_i[:, :], dst_rows[bass.ds(e, 1), :].rearrange("a p -> p a")))
                            gather(of_src, raw_d, src_i)
                            gather(of_dst, raw_d, dst_i)
                            gather(top, max_d, dst_i)

                        looped(TILES, 4)

                        def gather(to, rows, i):
                            moved(pool.indirect_dma_start(to[:, :], None, rows, bass.IndirectOffsetOnAxis(ap=i[:, 0:1], axis=0),
                                                          bounds_check=TILES * P - 1, oob_is_err=False))

                        def scatter(rows, from_):
                            pool.sem_inc(pool_on, 1)
                            moved(pool.indirect_dma_start(rows, bass.IndirectOffsetOnAxis(ap=goal_i[:, 0:1], axis=0), from_[:, :], None,
                                                          bounds_check=TILES * P - 1, oob_is_err=False))

                        with pool.Fori(0, ETILES) as e:
                            at(e)
                            fetch(e)
                            pool.sem_inc(any_pool, 1)
                            pool.wait_ge(any_dve, e * MAX_STEPS + (PRESET + TILES + MAX_STEPS))
                            scatter(max_d, top)
                        looped(ETILES, 6)
                        with pool.Fori(0, ETILES) as e:
                            at(e)
                            fetch(e)
                            gather(sums, sum_d, dst_i)
                            pool.sem_inc(any_pool, 1)
                            pool.wait_ge(any_dve, e * SUM_STEPS + (PRESET + TILES + ETILES * MAX_STEPS + SUM_STEPS))
                            scatter(sum_d, sums)
                        looped(ETILES, 7)
                        at(0)
                        moved(pool.dma_start(acc[:, :, 0:ROW], sum_d.rearrange("(t p) c -> p t c", p=P)))

                @block.tensor
                def _(pe):
                    with taken(pe, "pe"):
                        with pe.Fori(0, TILES) as t:
                            pe.wait_ge(any_pool, t + 1)
                            for c in range(2):
                                m = pe.matmul(bank[0][:, 0:EXT], xT_any[:, c * P:(c + 1) * P], wext[:, c, :], start=c == 0, stop=c == 1)
                            m.then_inc(any_pe, 1)
                        with pe.Fori(0, ETILES) as e:
                            pe.wait_ge(any_dve, e * MAX_STEPS + (PRESET + TILES + 4))
                            pe.matmul(bank[0][:, 0:P], ones[:, :], dst_diag[:, :], start=True, stop=True)
                            for q in range(2):
                                m = pe.matmul(bank[1 + q][:, :], ones[:, :], logit_diag[:, 4 * q:4 * q + 4, :].rearrange("p h j -> p (h j)"),
                                              start=True, stop=True)
                            m.then_inc(any_pe, 1)
                        with pe.Fori(0, ETILES) as e:
                            before = PRESET + TILES + ETILES * MAX_STEPS
                            pe.wait_ge(any_dve, e * SUM_STEPS + (before + 2))
                            pe.matmul(bank[0][:, 0:P], ones[:, :], dst_diag[:, :], start=True, stop=True).then_inc(any_pe, 1)
                            pe.wait_ge(any_dve, e * SUM_STEPS + (before + SUM_STEPS - 1))
                            pe.matmul(bank[1][:, 0:ROW], equal[:, :], weighted[:, :], start=True, stop=True).then_inc(any_pe, 1)

                @block.scalar
                def _(act):
                    with taken(act, "act"):
                        with act.Fori(0, ETILES) as e:
                            act.wait_ge(any_dve, e * SUM_STEPS + (PRESET + TILES + ETILES * MAX_STEPS + 5))
                            act.activation(weighted[:, C:ROW], logit[:, :], ACT.Exp).then_inc(any_act, 1)

                @block.vector
                def _(dve):
                    with taken(dve, "dve"):
                        steps = Steps(dve, any_dve)
                        steps.done(dve.tensor_tensor(above[:, :], ones[:, :], below[:, :], ALU.subtract))
                        steps.done(dve.memset(sums[:, :], 0.0))
                        steps.done(dve.memset(top[:, :], -FAR))
                        with dve.Fori(0, TILES) as t:
                            dve.wait_ge(any_pe, t + 1)
                            dve.tensor_copy(of_src[:, :], bank[0][:, 0:EXT]).then_inc(any_dve, 1)

                        def diagonal():
                            steps.done(dve.tensor_copy(dst_1[:, :], dst_i[:, :]))
                            steps.done(dve.tensor_scalar(dst_diag[:, :], ident[:, :], dst_1[:, 0:1], None, ALU.mult))

                        def logits_():
                            steps.done(dve.tensor_tensor(logit[:, :], of_src[:, C:C + HEADS], of_dst[:, C + HEADS:EXT], ALU.add))

                        def equals():
                            steps.done(dve.tensor_scalar(equal[:, :], bank[0][:, 0:P], dst_1[:, 0:1], None, ALU.is_equal))
                            steps.done(dve.tensor_tensor(other[:, :], equal[:, :], above[:, :], ALU.mult))
                            steps.done(dve.tensor_reduce(not_first[:, :], other[:, :], X, ALU.add))
                            steps.done(dve.tensor_scalar(not_first[:, :], not_first[:, :], 1.5, float(NO_NODE), ALU.is_gt, ALU.mult))
                            steps.done(dve.tensor_tensor(goal_i[:, :], not_first[:, :], dst_1[:, :], ALU.add))

                        with dve.Fori(0, ETILES) as e:
                            steps.at(e * MAX_STEPS + (PRESET + TILES))
                            dve.wait_ge(any_pool, e + (TILES + 1))
                            diagonal()
                            logits_()
                            steps.done(dve.tensor_tensor(logit_diag, over(ident[:, :], HEADS), spread(logit[:, :], P), ALU.mult))
                            dve.wait_ge(any_pe, e + (TILES + 1))
                            equals()
                            steps.done(dve.tensor_scalar(other[:, :], equal[:, :], -1.0, FAR, ALU.add, ALU.mult))
                            for q in range(2):
                                steps.done(dve.tensor_tensor(spread_out[:, 4 * q:4 * q + 4, :], bank[1 + q][:, :].rearrange("p (h j) -> p h j", h=4),
                                                             over(other[:, :], 4), ALU.add))
                            steps.done(dve.tensor_reduce(best[:, :], spread_out, X, ALU.max))
                            steps.done(dve.tensor_tensor(top[:, :], top[:, :], best[:, :], ALU.max))
                            assert steps.n == MAX_STEPS, steps.n
                        with dve.Fori(0, ETILES) as e:
                            steps.at(e * SUM_STEPS + (PRESET + TILES + ETILES * MAX_STEPS))
                            dve.wait_ge(any_pool, e + (TILES + ETILES + 1))
                            diagonal()
                            logits_()
                            steps.done(dve.tensor_tensor(logit[:, :], logit[:, :], top[:, :], ALU.subtract))
                            steps.done(dve.tensor_scalar(logit[:, :], logit[:, :], 0.0, None, ALU.min))
                            dve.wait_ge(any_pe, e * 2 + (TILES + ETILES + 1))
                            equals()
                            dve.wait_ge(any_act, e + 1)
                            steps.done(dve.tensor_tensor(weighted[:, 0:C].rearrange("p (h d) -> p h d", d=HD),
                                                         of_src[:, 0:C].rearrange("p (h d) -> p h d", d=HD),
                                                         spread(weighted[:, C:ROW], HD), ALU.mult))
                            dve.wait_ge(any_pe, e * 2 + (TILES + ETILES + 2))
                            steps.done(dve.tensor_tensor(sums[:, :], sums[:, :], bank[1][:, 0:ROW], ALU.add))
                            assert steps.n == SUM_STEPS, steps.n

        with ExitStack() as stage2:
            def keep_(name, shape, dt=F32):
                return stage2.enter_context(nc.sbuf_tensor(name, shape, dt))

            share = keep_("share", [P, 2, TILES])
            carry = keep_("carry", [P, EXPERTS])
            b1T = keep_("b1T", [P, EXPERTS * FC])
            plan = keep_("plan", [1, STILES, 4], I32)
            gamma_bc = keep_("gamma_bc", [P, C])
            beta_bc = keep_("beta_bc", [P, C])
            b2_bc = keep_("b2_bc", [P, EXPERTS * C])
            with ExitStack() as stage:
                def tmp(name, shape, dt=F32):
                    return stage.enter_context(nc.sbuf_tensor(name, shape, dt))

                cut = [0]

                def part_of_big(n, pattern, **kw):
                    a, cut[0] = cut[0], cut[0] + n
                    return big[:, a:cut[0]].rearrange(pattern, **kw)

                x_t = part_of_big(G * C, "p (i c) -> p i c", i=G)
                xnT_t = part_of_big(G * C, "p (i c) -> p i c", i=G)
                stage_x = part_of_big(G * 2 * XROW, "p (i q c) -> p i q c", i=G, q=2)
                gate = tmp("gate", [P, 2, EXPERTS])
                gate_b_bc = tmp("gate_b_bc", [P, EXPERTS])
                b1_raw = tmp("b1_raw", [EXPERTS * FC, P])
                rsum = tmp("rsum", [P, TILES, HEADS])
                gat = wq[:, 0:2, :]
                stat = tmp("stat", [P, G, 6])
                mv = tmp("mv", [P, G, 2])
                rs = tmp("rs", [P, G])
                row2 = wkvT[:, :, :].rearrange("p a f -> p (a f)")[:, 0:G * C].rearrange("p (i c) -> p i c", i=G)
                row2T = wq[:, 2:4, :]
                logits = tmp("logits", [P, G, EXPERTS])
                top8 = tmp("top8", [P, G, 8])
                top8i = tmp("top8i", [P, G, 8], U32)
                topf = tmp("topf", [P, 2, G])
                gap = tmp("gap", [P, G])
                duo = tmp("duo", [P, 2, G])
                one = tmp("one", [P, 2, G, EXPERTS])
                both = tmp("both", [P, G + 1, EXPERTS], BF16)
                below_h = tmp("below_h", [P, P], BF16)
                ones_h = tmp("ones_h", [P, P], BF16)
                place = tmp("place", [P, G, EXPERTS])
                hit = tmp("hit", [P, G, EXPERTS])
                slot_f = tmp("slot_f", [P, 2, G])
                slot = tmp("slot", [P, 2, G], I32)
                dest = tmp("dest", [P, G, 2])
                node = tmp("node", [P, 1])
                valid = tmp("valid", [P, 1])
                beyond = tmp("beyond", [P, 1])
                js_in = sem("js_in")
                x_got = [sem(f"x_got{i}") for i in range(G)]
                sent = row_got[0:G]
                jn_dve, ch_dve = sem("jn_dve"), sem("ch_dve")
                b1_turned, b1_kept = sem("b1_turned"), sem("b1_kept")
                preset = sem("preset")
                mixed = sem("mixed")
                x1_ready = sem("x1_ready")
                var2_ready, sqrt2 = sem("var2_ready"), sem("sqrt2")
                row2_ready, row2_turned, row2T_ready = sem("row2_ready"), sem("row2_turned"), sem("row2T_ready")
                gated, logits_read = sem("gated"), sem("logits_read")
                e_in, e_out = sem("e_in"), sem("e_out")
                both_ready, ranked = sem("both_ready"), sem("ranked")
                masked = sem("masked")
                meta_ready, staged = sem("meta_ready"), sem("staged")

                fill = tmp("fill", [P, XROW])
                fill_at = tmp("fill_at", [1, EXPERTS], I32)
                region0 = tmp("region0", [P, EXPERTS])
                count = tmp("count", [P, EXPERTS])
                etiles = tmp("etiles", [P, EXPERTS])
                etiles_i = tmp("etiles_i", [P, EXPERTS], I32)
                eend = tmp("eend", [P, EXPERTS])
                shift = tmp("shift", [P, EXPERTS])
                scol = tmp("scol", [P, 2])
                ecmp = tmp("ecmp", [P, 2, EXPERTS])
                eidx = tmp("eidx", [P, 2])
                real = tmp("real", [P, 1])
                expert = tmp("expert", [P, 2])
                plan_col = tmp("plan_col", [P, 3])
                plan_set, plan_turned = sem("plan_set"), sem("plan_turned")
                rt_set, rt_dve = sem("rt_set"), sem("rt_dve")
                fill_set, fill_at_set, filled = sem("fill_set"), sem("fill_at_set"), sem("filled")

                def before(i):
                    return 1 if i == 0 else 2

                with nc.Block() as block:
                    @block.sync
                    def _(sp):
                        sp.dma_start(gate[:, :, :], gate_w.rearrange("(c p) e -> p c e", p=P)).then_inc(js_in, 16)
                        sp.dma_start(gate_b_bc[:, :], gate_b.partition_broadcast(P)).then_inc(js_in, 16)
                        sp.dma_start(b1_raw[:, :], b1.rearrange("e (f p) -> (e f) p", p=P)).then_inc(js_in, 16)
                        sp.dma_start(gamma_bc[:, :], gamma.partition_broadcast(P)).then_inc(js_in, 16)
                        sp.dma_start(beta_bc[:, :], beta.partition_broadcast(P)).then_inc(js_in, 16)

                        def load(g):
                            for i in range(G):
                                t = g * G + i
                                if not starts(g):
                                    sp.wait_ge(x1_ready, t - G + 3)
                                sp.dma_start(x_t[:, i, :], xb_d[bass.ds(t * P, P), :]).then_inc(x_got[i], 16)
                                sp.dma_start(xnT_t[:, i, :], xnT_d[bass.ds(t, 1), :, :].rearrange("a p c -> p (a c)")).then_inc(x_got[i], 16)

                        load(0)
                        with sp.Fori(1, GROUPS - 1) as g:
                            load(g)
                        load(GROUPS - 1)
                        sp.dma_start(b2_bc[:, :], b2.rearrange("e c -> (e c)").partition_broadcast(P)).then_inc(js_in, 16)
                        sp.wait_ge(js_in, 96)
                        regs = [sp.alloc_register(f"fill{e}") for e in range(EXPERTS)]
                        sp.wait_ge(fill_set, 1)
                        sp.dma_start(slots_x[NULL_ROW:SLOTS, :], fill[:, :]).then_inc(filled, 16)
                        sp.wait_ge(fill_at_set, 1)
                        sp.load(regs, fill_at[0:1, :])
                        for e in range(EXPERTS):
                            at = sp.snap(regs[e], min_val=0, max_val=NULL_ROW - P)
                            sp.dma_start(slots_x[bass.ds(at, P), :], fill[:, :]).then_inc(filled, 16)
                        sp.wait_ge(filled, 16 * (EXPERTS + 1))

                    @block.tensor
                    def _(pe):
                        pe.sem_inc(x1_ready, 2)
                        pe.sem_inc(logits_read, 1)
                        pe.sem_inc(row2T_ready, 2)
                        pe.wait_ge(js_in, 80)
                        pe.transpose(bank[7][:, 0:EXPERTS * FC], b1_raw[:, :], ident[0:EXPERTS * FC, 0:EXPERTS * FC]).then_inc(b1_turned, 1)

                        def mix(g, i):
                            t, b = g * G + i, i % 2
                            pe.wait_ge(x_got[i], 32 * g + 32)
                            pe.wait_ge(x1_ready, t + 3 - before(i))
                            for c in range(2):
                                m = pe.matmul(bank[b][:, 0:C], xnT_t[:, i, c * P:(c + 1) * P], mixG[:, c, :], start=c == 0, stop=c == 1)
                            m.then_inc(mixed, 1)

                        def turn(g, i):
                            t, b = g * G + i, i % 2
                            pe.wait_ge(row2_ready, t + 1)
                            pe.wait_ge(row2T_ready, t + 3 - before(i))
                            for c in range(2):
                                m = pe.transpose(bank[2 + b][:, c * P:(c + 1) * P], row2[:, i, c * P:(c + 1) * P], ident[:, :])
                            m.then_inc(row2_turned, 1)

                        def gates(g, i):
                            t, b = g * G + i, i % 2
                            out_ = bank[4][:, i * EXPERTS:(i + 1) * EXPERTS]
                            if i == 0:
                                pe.wait_ge(logits_read, g + 1)
                            pe.wait_ge(row2T_ready, t + 3)
                            for c in range(2):
                                m = pe.matmul(out_, row2T[:, b, c * P:(c + 1) * P], gate[:, c, :], start=c == 0, stop=c == 1)
                            m.then_inc(gated, 1)

                        pe.wait_ge(preset, 1)

                        def rank(g):
                            pe.wait_ge(both_ready, g + 1)
                            pe.matmul(bank[6][:, 0:P], below_h[:, :], both[:, :, :].rearrange("p i e -> p (i e)"), start=True, stop=False)
                            for i in range(G):
                                m = pe.matmul(bank[6][:, (i + 1) * EXPERTS:P].rearrange("p (i e) -> p i e", e=EXPERTS), ones_h[:, :],
                                              over(both[:, i, :], G - i), start=False, stop=i == G - 1)
                            m.then_inc(ranked, 1)

                        def group(g, left):
                            for i in range(G):
                                turn(g, i)
                                if left > 0 and i + 2 < G:
                                    mix(g + 1, i + 2)
                                if i > 0:
                                    gates(g, i - 1)
                            gates(g, G - 1)
                            if left > 1:
                                mix(g + 2, 0)
                                mix(g + 2, 1)
                            rank(g)

                        for i in range(G):
                            mix(0, i)
                        mix(1, 0)
                        mix(1, 1)
                        with pe.Fori(0, GROUPS - 2) as g:
                            group(g, 2)
                        group(GROUPS - 2, 1)
                        group(GROUPS - 1, 0)
                        pe.wait_ge(plan_set, 1)
                        for q in range(3):
                            m = pe.transpose(bank[7][0:1, q * P:(q + 1) * P], plan_col[:, q:q + 1], ident[:, :])
                        m.then_inc(plan_turned, 1)

                    @block.scalar
                    def _(act):
                        act.wait_ge(b1_turned, 1)
                        act.copy(b1T[:, :], bank[7][:, 0:EXPERTS * FC]).then_inc(b1_kept, 1)

                        def root(g):
                            act.wait_ge(var2_ready, g + 1)
                            act.activation(rs[:, :], rs[:, :], ACT.Sqrt).then_inc(sqrt2, 1)

                        def stage_(g, places):
                            for i in places:
                                if not starts(g):
                                    act.wait_ge(sent[i], 32 * g + COUNTED)
                                for q in range(2):
                                    act.copy(stage_x[:, i, q, 0:C], row2[:, i, :])
                                act.copy(work_f[:, bass.ds((g * G + i) * EXT, C)], row2[:, i, :]).then_inc(staged, 1)

                        def group(g, more):
                            for i in range(G):
                                act.wait_ge(row2_turned, g * G + i + 1)
                                act.copy(row2T[:, i % 2, :], bank[2 + i % 2][:, 0:C]).then_inc(row2T_ready, 1)
                            if more:
                                root(g + 1)
                            stage_(g, range(G // 2 + 1))
                            act.wait_ge(e_in, g + 1)
                            act.activation(gap[:, :], gap[:, :], ACT.Exp).then_inc(e_out, 1)
                            stage_(g, range(G // 2 + 1, G))

                        root(0)
                        group(0, True)
                        with act.Fori(1, GROUPS - 1) as g:
                            group(g, True)
                        group(GROUPS - 1, False)

                    @block.gpsimd
                    def _(pool):
                        kw = dict(allow_small_or_imprecise_dtypes=True)
                        pool.iota(node[:, :], pattern=[[1, 1]], base=0, channel_multiplier=1, **kw)
                        pool.iota(carry[:, :], pattern=[[REGION, EXPERTS]], base=0, channel_multiplier=0, **kw)
                        pool.memset(fill[:, 0:C], 0.0)
                        pool.memset(fill[:, C:XROW], float(2 * TILES * P)).then_inc(fill_set, 1)
                        pool.iota(scol[:, :], pattern=[[-4, 2]], base=0, channel_multiplier=1, **kw)
                        pool.iota(region0[:, :], pattern=[[REGION, EXPERTS]], base=0, channel_multiplier=0, **kw).then_inc(rt_set, 1)
                        pool.memset(both[:, G, :], 0.0)
                        pool.memset(ones_h[:, :], 1.0)
                        pool.tensor_copy(below_h[:, :], below[:, :])
                        pool.iota(dest[:, :, :], pattern=[[2 * P, G], [1, 2]], base=0, channel_multiplier=2, **kw).then_inc(preset, 1)

                        def send(g):
                            pool.wait_ge(meta_ready, g + 1)
                            for i in range(G):
                                pool.wait_ge(staged, g * G + i + 1)
                                pool.sem_inc(pool_on, 1)
                                for q in range(2):
                                    pool.indirect_dma_start(slots_x, bass.IndirectOffsetOnAxis(ap=slot[:, q, i:i + 1], axis=0),
                                                            stage_x[:, i, q, :], None, bounds_check=SLOTS - 1,
                                                            oob_is_err=False).then_inc(sent[i], 16)

                        with pool.Fori(0, GROUPS) as g:
                            send(g)
                        for i in range(G):
                            pool.wait_ge(sent[i], 32 * GROUPS + COUNTED)

                    @block.vector
                    def _(dve):
                        steps = Steps(dve, jn_dve)
                        steps.done(dve.tensor_scalar(rsum[:, :, :], acc[:, :, C:C + HEADS], 1e-30, None, ALU.max))
                        steps.done(dve.reciprocal(rsum[:, :, :], rsum[:, :, :]))
                        dve.wait_ge(preset, 1)
                        steps.done(dve.tensor_scalar(valid[:, :], node[:, :], float(LAST), None, ALU.is_lt))
                        steps.done(dve.tensor_scalar(beyond[:, :], node[:, :], float(LAST), float(SLOTS), ALU.is_ge, ALU.mult))
                        rsum_f = rsum[:, :, :].rearrange("p t h -> p (t h)")
                        first = steps.n

                        def sweep(g, join):
                            if join is not None:
                                steps.at(first + join * 3 * G)
                            if g is not None and not starts(g):
                                dve.wait_ge(staged, g * G)
                            def normed(i):
                                if g is not None and i < G:
                                    dve.tensor_scalar(row2[:, i, :], acc_f[:, bass.ds((g * G + i) * EXT, C)], mv[:, i, 0:1],
                                                      rs[:, i:i + 1], ALU.subtract, ALU.mult).then_inc(row2_ready, 1)

                            normed(0)
                            normed(1)
                            for i in range(G):
                                if join is not None:
                                    t, b = join * G + i, i % 2
                                    rows = acc_f[:, bass.ds(t * EXT, C)]
                                    steps.go(dve.tensor_tensor(gat[:, b, :].rearrange("p (h d) -> p h d", d=HD),
                                                               rows.rearrange("p (h d) -> p h d", d=HD),
                                                               spread(rsum_f[:, bass.ds(t * HEADS, HEADS)], HD), ALU.mult))
                                normed(i + 2)
                                if join is not None:
                                    if i > 0:
                                        stats_of(join, i - 1)
                                    dve.wait_ge(jn_dve, steps.base + (3 * i + 1))
                                    dve.wait_ge(x_got[i], 32 * join + 32)
                                    steps.go(dve.tensor_tensor(gat[:, b, :], gat[:, b, :], x_t[:, i, :], ALU.add))
                                    dve.wait_ge(mixed, t + 1)
                                    dve.wait_ge(jn_dve, steps.base + (3 * i + 2))
                                    dve.tensor_tensor(rows, gat[:, b, :], bank[b][:, 0:C], ALU.add).then_inc(x1_ready, 1)
                            if join is not None:
                                stats_of(join, G - 1)

                        def stats_of(g, i):
                            t = g * G + i
                            dve.wait_ge(x1_ready, t + 3)
                            dve.sem_inc(dve_on, 1)
                            steps.go(dve.bn_stats(stat[:, i, :], acc_f[:, bass.ds(t * EXT, C)]))

                        chosen = Steps(dve, ch_dve)
                        NORMED, CHOICE = G + 1, 2 * G + 22

                        def spread_of(g):
                            if starts(g):
                                chosen.at(0)
                            else:
                                chosen.at(g * (NORMED + 1) + (g - 1) * CHOICE)
                            dve.wait_ge(jn_dve, first + (g + 1) * 3 * G)
                            dve.sem_inc(dve_on, 1)
                            for i in range(G):
                                chosen.go(dve.bn_aggr(mv[:, i, :], stat[:, i, :]))
                            dve.wait_ge(ch_dve, chosen.base + chosen.n)
                            chosen.done(dve.tensor_scalar(rs[:, :], mv[:, :, 1], EPS, None, ALU.add))
                            dve.sem_inc(var2_ready, 1)

                        def invert(g):
                            dve.wait_ge(sqrt2, g + 1)
                            dve.sem_inc(dve_on, 1)
                            chosen.done(dve.reciprocal(rs[:, :], rs[:, :]))

                        def choose(g):
                            last_group = is_group_last(g)
                            chosen.at((GROUPS if last_group else g + 2) * (NORMED + 1) + g * CHOICE - (0 if last_group else 1))
                            dve.wait_ge(gated, (g + 1) * G)
                            chosen.done(dve.tensor_tensor(logits[:, :, :], bank[4][:, 0:G * EXPERTS].rearrange("p (i e) -> p i e", e=EXPERTS),
                                                          over(gate_b_bc[:, :], G), ALU.add))
                            dve.sem_inc(logits_read, 1)
                            for i in range(G):
                                chosen.go(dve.max(top8[:, i, :], logits[:, i, :]))
                            dve.wait_ge(ch_dve, chosen.base + chosen.n)
                            dve.sem_inc(dve_on, 1)
                            for i in range(G):
                                chosen.go(dve.max_index(top8i[:, i, :], top8[:, i, :], logits[:, i, :]))
                            chosen.go(dve.tensor_copy(duo[:, :, :], top8[:, :, 0:2].rearrange("p i q -> p q i")))
                            dve.wait_ge(ch_dve, chosen.base + chosen.n)
                            chosen.go(dve.tensor_copy(topf[:, :, :], top8i[:, :, 0:2].rearrange("p i q -> p q i")))
                            chosen.done(dve.tensor_tensor(gap[:, :], duo[:, 1, :], duo[:, 0, :], ALU.subtract))
                            dve.sem_inc(e_in, 1)
                            for q in range(2):
                                chosen.go(dve.tensor_tensor(one[:, q, :, :], over(iota[:, 0:EXPERTS], G), spread(topf[:, q, :], EXPERTS), ALU.is_equal))
                            dve.wait_ge(ch_dve, chosen.base + chosen.n)
                            if last_group:
                                for q in range(2):
                                    dve.tensor_scalar(one[:, q, G - 1, :], one[:, q, G - 1, :], valid[:, 0:1], None, ALU.mult).then_inc(masked, 1)
                                dve.wait_ge(masked, 2)
                            chosen.done(dve.tensor_tensor(both[:, 0:G, :], one[:, 0, :, :], one[:, 1, :, :], ALU.add))
                            dve.sem_inc(both_ready, 1)
                            if not starts(g):
                                for i in range(G):
                                    dve.wait_ge(sent[i], 32 * g + COUNTED)
                            for q in range(2):
                                chosen.go(dve.tensor_copy(stage_x[:, :, q, C], dest[:, :, q]))
                            dve.wait_ge(ranked, g + 1)
                            chosen.done(dve.tensor_tensor(place[:, :, :], bank[6][:, 0:G * EXPERTS].rearrange("p (i e) -> p i e", e=EXPERTS),
                                                          over(carry[:, :], G), ALU.add))
                            chosen.done(dve.tensor_tensor(carry[:, :], carry[:, :], bank[6][:, G * EXPERTS:P], ALU.add))
                            for q in range(2):
                                chosen.done(dve.tensor_tensor(hit[:, :, :], place[:, :, :], one[:, q, :, :], ALU.mult))
                                chosen.done(dve.tensor_reduce(slot_f[:, q, :], hit[:, :, :], X, ALU.add))
                            if last_group:
                                for q in range(2):
                                    dve.tensor_tensor(slot_f[:, q, G - 1:G], slot_f[:, q, G - 1:G], beyond[:, :], ALU.add).then_inc(masked, 1)
                                dve.wait_ge(masked, 4)
                            chosen.done(dve.tensor_copy(slot[:, :, :], slot_f[:, :, :]))
                            chosen.done(dve.tensor_scalar(dest[:, :, :], dest[:, :, :], float(2 * P * G), None, ALU.add))
                            dve.sem_inc(meta_ready, 1)
                            dve.wait_ge(e_out, g + 1)
                            chosen.done(dve.tensor_scalar(duo[:, 0, :], gap[:, :], 1.0, None, ALU.add))
                            chosen.done(dve.reciprocal(duo[:, 0, :], duo[:, 0, :]))
                            chosen.done(dve.tensor_tensor(duo[:, 1, :], duo[:, 0, :], gap[:, :], ALU.mult))
                            for q in range(2):
                                chosen.go(dve.tensor_copy(share_f[:, bass.ds(g * G + q * TILES, G)], duo[:, q, :]))
                            assert chosen.n == CHOICE, chosen.n
                            chosen.at(chosen.base + CHOICE)

                        share_f = share[:, :, :].rearrange("p q t -> p (q t)")
                        sweep(None, 0)
                        spread_of(0)
                        invert(0)

                        def group(g):
                            sweep(g, g + 1)
                            spread_of(g + 1)
                            choose(g)
                            invert(g + 1)

                        group(0)
                        with dve.Fori(1, GROUPS - 1) as g:
                            group(g)
                        sweep(GROUPS - 1, None)
                        choose(GROUPS - 1)
                        dve.wait_ge(b1_kept, 1)

                        steps = Steps(dve, rt_dve)
                        steps.done(dve.tensor_copy(fill_at[:, :], carry[0:1, :]))
                        dve.sem_inc(fill_at_set, 1)
                        dve.wait_ge(rt_set, 1)
                        steps.done(dve.tensor_tensor(count[:, :], carry[:, :], region0[:, :], ALU.subtract))
                        steps.done(dve.tensor_scalar(etiles_i[:, :], count[:, :], float(P - 1), None, ALU.add))
                        steps.done(dve.tensor_scalar(etiles_i[:, :], etiles_i[:, :], 7, None, ALU.arith_shift_right))
                        steps.done(dve.tensor_copy(etiles[:, :], etiles_i[:, :]))
                        steps.done(dve.tensor_tensor_scan(eend[:, :], ones[:, 0:EXPERTS], etiles[:, :], 0.0, ALU.mult, ALU.add))
                        steps.done(dve.tensor_tensor(shift[:, :], etiles[:, :], eend[:, :], ALU.subtract))
                        steps.done(dve.scalar_tensor_tensor(shift[:, :], shift[:, :], float(P), region0[:, :], ALU.mult, ALU.add))
                        for q in range(2):
                            steps.go(dve.tensor_scalar(ecmp[:, q, :], eend[:, :], scol[:, q:q + 1], None, ALU.is_le))
                        dve.wait_ge(rt_dve, steps.n)
                        steps.done(dve.tensor_reduce(eidx[:, :], ecmp[:, :, :], X, ALU.add))
                        steps.done(dve.tensor_scalar(expert[:, :], eidx[:, :], float(EXPERTS - 1), None, ALU.min))
                        steps.go(dve.tensor_copy(plan_col[:, 1:2], expert[:, 0:1]))
                        steps.go(dve.tensor_tensor(plan_col[:, 2:3], expert[:, 0:1], expert[:, 1:2], ALU.not_equal))
                        steps.go(dve.tensor_scalar(real[:, :], eidx[:, 0:1], float(EXPERTS), None, ALU.is_lt))
                        steps.done(dve.tensor_scalar(ecmp[:, 0, :], iota[:, 0:EXPERTS], eidx[:, 0:1], None, ALU.is_equal))
                        steps.done(dve.tensor_tensor(ecmp[:, 0, :], ecmp[:, 0, :], shift[:, :], ALU.mult))
                        steps.done(dve.tensor_reduce(plan_col[:, 0:1], ecmp[:, 0, :], X, ALU.add))
                        steps.done(dve.scalar_tensor_tensor(plan_col[:, 0:1], scol[:, 0:1], float(P), plan_col[:, 0:1], ALU.mult, ALU.add))
                        steps.done(dve.tensor_scalar(plan_col[:, 0:1], plan_col[:, 0:1], -float(NULL_ROW), None, ALU.add))
                        steps.done(dve.tensor_tensor(plan_col[:, 0:1], plan_col[:, 0:1], real[:, :], ALU.mult))
                        steps.done(dve.tensor_scalar(plan_col[:, 0:1], plan_col[:, 0:1], float(NULL_ROW), None, ALU.add))
                        dve.sem_inc(plan_set, 1)
                        dve.wait_ge(plan_turned, 1)
                        steps.done(dve.tensor_copy(plan[:, :, 0:3], bank[7][0:1, 0:3 * P].rearrange("a (q s) -> a s q", q=3)[:, 0:STILES, :]))
                        steps.done(dve.memset(plan[:, 0:4, 2], 1))
                        steps.done(dve.memset(plan[:, :, 3], 0))

            with ExitStack() as stage:
                def tmp(name, shape, dt=F32):
                    return stage.enter_context(nc.sbuf_tensor(name, shape, dt))

                w1_s = [big[:, 1024 * m:1024 * (m + 1)] for m in range(2)] + [wkvT[:, m, :] for m in range(2)]
                w1_s = [w.rearrange("p (c f) -> p c f", c=2) for w in w1_s]
                w2_s = [big[:, 1024 * m:1024 * (m + 1)].rearrange("p (c f) -> p c f", c=4) for m in (2, 3)] + [wq, woutT]
                hid = big[:, 4096:5120].rearrange("p (b f s) -> p b f s", b=2, f=4)
                inT = big[:, 5120:5632].rearrange("p (b c) -> p b c", b=2)
                res = big[:, 5632:6656].rearrange("p (m c) -> p m c", m=4)
                in_s = big[:, 6656:6656 + 4 * XROW].rearrange("p (m c) -> p m c", m=4)
                goal = tmp("goal", [P, 8, 1], I32)
                w1_got, W1_BASE = x_got[0:4], 32 * GROUPS
                w2_got = [sem(f"w2_got{m}") for m in range(4)]
                in_got = [sem(f"in_got{m}") for m in range(4)]
                in_turned, inT_ready = sem("in_turned"), sem("inT_ready")
                h_done, h_ready = sem("h_done"), sem("h_ready")
                y_done, y_ready = sem("y_done"), sem("y_ready")
                y_out = row_got[G:G + 4]
                x1_shifted = sem("x1_shifted")
                with nc.Block() as block:
                    @block.sync
                    def _(sp):
                        r_reg = sp.alloc_register("row_sp")
                        regs = [sp.alloc_register(f"plan_sp{q}") for q in range(2)]

                        def rows(s, m):
                            sp.load(r_reg, plan[0:1, bass.ds(s, 1), 0:1].rearrange("p a q -> p (a q)"))
                            r = sp.snap(r_reg, min_val=0, max_val=NULL_ROW)
                            if not (isinstance(s, int) and s < 4):
                                sp.wait_ge(inT_ready, s - 1)
                            sp.dma_start(in_s[:, m, :], slots_x[bass.ds(r, P), :]).then_inc(in_got[m], 16)

                        def weights(s, m):
                            sp.load(regs, plan[0:1, bass.ds(s, 1), 1:3].rearrange("p a q -> p (a q)"))
                            e = sp.snap(regs[0], min_val=0, max_val=EXPERTS - 1)
                            other = sp.snap(regs[1], min_val=0, max_val=1)
                            first = isinstance(s, int) and s < 4
                            if not first:
                                sp.wait_ge(h_done, s - 1)
                            sp.dma_start(w1_s[m][:, :, :], w1[bass.ds(e, 1), :, :].rearrange("a (c p) f -> p (a c) f", p=P),
                                         cond=other).then_inc(w1_got[m], 16)
                            if not first:
                                sp.wait_ge(y_done, s - 1)
                            sp.dma_start(w2_s[m][:, :, :], w2[bass.ds(e, 1), :, :].rearrange("a (c p) f -> p (a c) f", p=P),
                                         cond=other).then_inc(w2_got[m], 16)

                        for s in range(4):
                            rows(s, s)
                        for s in range(3):
                            weights(s, s)

                        def step(s, i):
                            rows(s + i + 4, i)
                            weights(s + i + 3, (i + 3) % 4)

                        for i in range(4):
                            step(0, i)
                        with sp.Fori(1, STILES // 4 - 1) as h:
                            for i in range(4):
                                step(h * 4, i)
                        for s in range(STILES // 4 * 4 - 4, STILES - 3):
                            if s + 4 < STILES:
                                rows(s + 4, s % 4)
                            weights(s + 3, (s + 3) % 4)

                    @block.tensor
                    def _(pe):
                        pe.sem_inc(inT_ready, 2)
                        pe.sem_inc(h_done, 2)
                        pe.sem_inc(y_done, 2)
                        pe.sem_inc(y_ready, 2)

                        def turn(s, i):
                            pe.wait_ge(in_got[i % 4], 4 * (s - i) + 16 * (i // 4 + 1))
                            b = i % 2
                            for c in range(2):
                                m = pe.transpose(bank[b][:, c * P:(c + 1) * P], in_s[:, i % 4, c * P:(c + 1) * P], ident[:, :])
                            m.then_inc(in_turned, 1)

                        def hidden(s, i):
                            b = i % 2
                            pe.wait_ge(inT_ready, s + 3)
                            pe.wait_ge(w1_got[i], 4 * (s - i) + 16 + W1_BASE)
                            for f in range(FC):
                                for c in range(2):
                                    m = pe.matmul(bank[2 + b][:, f * P:(f + 1) * P], w1_s[i][:, c, f * P:(f + 1) * P],
                                                  inT[:, b, c * P:(c + 1) * P], start=c == 0, stop=c == 1)
                            m.then_inc(h_done, 1)

                        def down(s, i):
                            b = i % 2
                            pe.wait_ge(h_ready, s + 1)
                            pe.wait_ge(w2_got[i], 4 * (s - i) + 16)
                            pe.wait_ge(y_ready, s + 1)
                            for f in range(FC):
                                m = pe.matmul(bank[4 + b][:, 0:C], hid[:, b, f, :], w2_s[i][:, f, :], start=f == 0, stop=f == FC - 1)
                            m.then_inc(y_done, 1)

                        def step(s0, i):
                            s = s0 + i
                            hidden(s, i)
                            if not (isinstance(s, int) and s >= STILES - 2):
                                turn(s + 2, i + 2)
                            if not (isinstance(s, int) and s == 0):
                                down(s - 1, (i + 3) % 4)

                        turn(0, 0)
                        turn(1, 1)
                        for i in range(4):
                            step(0, i)
                        with pe.Fori(1, STILES // 4) as h:
                            for i in range(4):
                                step(h * 4, i)
                        for i in range(STILES % 4):
                            step(STILES - STILES % 4, i)
                        down(STILES - 1, (STILES - 1) % 4)

                    @block.scalar
                    def _(act):
                        e_reg = act.alloc_register("expert_act")

                        def relu(s0, b):
                            s = s0 + b
                            act.load(e_reg, plan[0:1, bass.ds(s, 1), 1:2].rearrange("p a q -> p (a q)"))
                            e = act.snap(e_reg, min_val=0, max_val=EXPERTS - 1)
                            act.wait_ge(h_done, s + 3)
                            act.wait_ge(y_done, s + 1)
                            for f in range(FC):
                                a = act.activation(hid[:, b, f, :], bank[2 + b][:, f * P:(f + 1) * P], ACT.Relu,
                                                   bias=b1T[:, bass.ds(e * FC + f, 1)])
                            a.then_inc(h_ready, 1)

                        with by_two(act, 0, STILES) as s0:
                            relu(s0, 0)
                            relu(s0, 1)

                    @block.vector
                    def _(dve):
                        e_reg = dve.alloc_register("expert_dve")

                        def move_in(s, b, m):
                            dve.wait_ge(in_turned, s + 1)
                            dve.wait_ge(h_done, s + 1)
                            dve.tensor_copy(goal[:, m, :], in_s[:, m % 4, C:XROW])
                            dve.tensor_copy(inT[:, b, :], bank[b][:, 0:C]).then_inc(inT_ready, 1)

                        def move_out(s, b, m):
                            dve.load(e_reg, plan[0:1, bass.ds(s, 1), 1:2].rearrange("p a q -> p (a q)"))
                            e = dve.snap(e_reg, min_val=0, max_val=EXPERTS - 1)
                            dve.wait_ge(y_done, s + 3)
                            if not (isinstance(s, int) and s < 4):
                                dve.wait_ge(y_out[m % 4], 4 * (s - m % 4) + COUNTED)
                            dve.tensor_tensor(res[:, m % 4, :], bank[4 + b][:, 0:C], b2_bc[:, bass.ds(e * C, C)], ALU.add).then_inc(y_ready, 1)

                        def eight(s):
                            for i in range(8):
                                move_in(s + i + 2, i % 2, (i + 2) % 8)
                                move_out(s + i, i % 2, i)

                        move_in(0, 0, 0)
                        move_in(1, 1, 1)
                        eight(0)
                        with dve.Fori(1, (STILES - 2) // 8) as h:
                            eight(h * 8)
                        move_out(STILES - 2, 0, 0)
                        move_out(STILES - 1, 1, 1)

                    @block.gpsimd
                    def _(pool):
                        def send(s, b, m):
                            pool.wait_ge(y_ready, s + 3)
                            pool.sem_inc(pool_on, 1)
                            pool.indirect_dma_start(moe_d, bass.IndirectOffsetOnAxis(ap=goal[:, m, :], axis=0), res[:, m % 4, :], None,
                                                    bounds_check=2 * TILES * P - 1, oob_is_err=False).then_inc(y_out[m % 4], 16)

                        def shift_x1(t):
                            rows = acc_f[:, bass.ds(t * EXT, C)]
                            pool.tensor_tensor(rows, rows, beta_bc[:, :], ALU.add).then_inc(x1_shifted, 1)

                        shift_x1(TILES - 1)
                        with pool.Fori(0, (TILES - 1) // 4) as h:
                            for i in range(8):
                                send(h * 8 + i, i % 2, i)
                                if i % 2 == 0:
                                    shift_x1(h * 4 + i // 2)
                        with pool.Fori((TILES - 1) // 4, (STILES - 2) // 8) as h:
                            for i in range(8):
                                send(h * 8 + i, i % 2, i)
                        send(STILES - 2, 0, 0)
                        send(STILES - 1, 1, 1)
                        pool.wait_ge(x1_shifted, TILES)
                        for m in range(4):
                            pool.wait_ge(y_out[m], 16 * ((STILES - 1 - m) // 4 + 1) + COUNTED)

            with ExitStack() as stage:
                y_got = big[:, 0:2 * G * 2 * C].rearrange("p (b i q c) -> p b i q c", b=2, i=G, q=2)
                y_in = [sem(f"y_in{b}") for b in range(2)]
                cb_dve, y_used = sem("cb_dve"), sem("y_used")
                var3_ready, sqrt3 = sem("var3_ready"), sem("sqrt3")
                scaled, stretched = sem("scaled"), sem("stretched")
                o_ready, o_out = sem("o_ready"), sem("o_out")
                moe_t = moe_d.rearrange("(t p q) c -> t p q c", p=P, q=2)

                with nc.Block() as block:
                    @block.sync
                    def _(sp):
                        def load(g):
                            full = G - 1 if g == GROUPS - 1 else G
                            sp.wait_ge(y_used, g + 1)
                            sp.dma_start(y_got[:, g % 2, 0:full, :, :].rearrange("p i q c -> p i (q c)"),
                                         moe_t[g * G:g * G + full, :, :, :].rearrange("t p q c -> p t (q c)")).then_inc(y_in[g % 2], 16)
                            if full < G:
                                sp.dma_start(y_got[0:LAST, g % 2, full, :, :], moe_t[TILES - 1, 0:LAST, :, :]).then_inc(y_in[g % 2], 16)

                        def store(g):
                            full = G - 1 if g == GROUPS - 1 else G
                            sp.wait_ge(o_ready, (g + 1) * G)
                            sp.dma_start(out[g * G * P:(g * G + full) * P, :].rearrange("(t p) c -> p t c", p=P),
                                         work[:, g * G:g * G + full, 0:C]).then_inc(o_out, 16)
                            if full < G:
                                sp.dma_start(out[(TILES - 1) * P:N, :], work[0:LAST, TILES - 1, 0:C]).then_inc(o_out, 16)

                        for g in range(GROUPS + 3):
                            if g < GROUPS:
                                load(g)
                            if g >= 3:
                                store(g - 3)
                        sp.wait_ge(o_out, 16 * (GROUPS + 1))

                    @block.scalar
                    def _(act):
                        with act.Fori(0, GROUPS) as g:
                            group_rstd = rstd[:, bass.ds(g * G, G)]
                            act.wait_ge(var3_ready, 2 * g + 1)
                            act.activation(group_rstd, group_rstd, ACT.Sqrt).then_inc(sqrt3, 1)
                            act.wait_ge(var3_ready, 2 * g + 2)
                            for i in range(G):
                                rows = work_f[:, bass.ds((g * G + i) * EXT, C)]
                                act.activation(rows, rows, ACT.Identity, bias=mean[:, bass.ds(g * G + i, 1)],
                                               scale=rstd[:, bass.ds(g * G + i, 1)]).then_inc(scaled, 1)

                    @block.gpsimd
                    def _(pool):
                        with pool.Fori(0, GROUPS) as g:
                            for i in range(G):
                                rows = work_f[:, bass.ds((g * G + i) * EXT, C)]
                                pool.wait_ge(scaled, g * G + i + 1)
                                pool.tensor_tensor(rows, rows, gamma_bc[:, :], ALU.mult).then_inc(stretched, 1)

                    @block.vector
                    def _(dve):
                        steps = Steps(dve, cb_dve)
                        share_f = share[:, :, :].rearrange("p q t -> p (q t)")
                        STEPS = 3 * G + 9
                        dve.sem_inc(y_used, 2)

                        def sums(g, b):
                            steps.at(g * STEPS)
                            dve.wait_ge(y_in[b], 8 * (g - b) + 16 + (16 if is_group_last(g) else 0))
                            for q in range(2):
                                for i in range(G):
                                    rows = work_f[:, bass.ds((g * G + i) * EXT, C)]
                                    steps.go(dve.scalar_tensor_tensor(rows, y_got[:, b, i, q, :], share_f[:, bass.ds(g * G + i + q * TILES, 1)],
                                                                      rows, ALU.mult, ALU.add))
                                dve.wait_ge(cb_dve, steps.base + steps.n)
                            dve.sem_inc(y_used, 1)
                            for i in range(G):
                                t = g * G + i
                                steps.go(dve.bn_stats(stats[:, bass.ds(t, 1), :].rearrange("p a c -> p (a c)"),
                                                      work_f[:, bass.ds(t * EXT, C)]))
                            dve.wait_ge(cb_dve, steps.base + steps.n)
                            layer_stats(dve, steps, bass.ds(g * G, G))
                            dve.sem_inc(var3_ready, 1)

                        def invert(g):
                            group_rstd, group_mean = rstd[:, bass.ds(g * G, G)], mean[:, bass.ds(g * G, G)]
                            dve.wait_ge(sqrt3, g + 1)
                            dve.sem_inc(dve_on, 1)
                            steps.done(dve.reciprocal(group_rstd, group_rstd))
                            steps.done(dve.scalar_tensor_tensor(group_mean, group_mean, -1.0, group_rstd, ALU.mult, ALU.mult))
                            dve.sem_inc(var3_ready, 1)
                            assert steps.n == STEPS, steps.n

                        def final(g):
                            for i in range(G):
                                t = g * G + i
                                rows = work_f[:, bass.ds(t * EXT, C)]
                                dve.wait_ge(stretched, t + 1)
                                dve.tensor_tensor(rows, rows, acc_f[:, bass.ds(t * EXT, C)], ALU.add).then_inc(o_ready, 1)

                        def group(g, b):
                            sums(g, b)
                            final(g - 1)
                            invert(g)

                        sums(0, 0)
                        invert(0)
                        with dve.Fori(0, GROUPS // 2 - 1) as h:
                            group(h * 2 + 1, 1)
                            group(h * 2 + 2, 0)
                        group(GROUPS - 2, 1)
                        group(GROUPS - 1, 0)
                        final(GROUPS - 1)


_INS = ['x', 'src', 'dst', 'L0_gnn_W', 'L0_gnn_a_src', 'L0_gnn_a_dst', 'L0_mix_Wqkv', 'L0_mix_Wout', 'L0_mix_bout',
        'L0_ffn_gate_w', 'L0_ffn_gate_b', 'L0_ffn_w1', 'L0_ffn_b1', 'L0_ffn_w2', 'L0_ffn_b2', 'L0_ffn_gamma',
        'L0_ffn_beta']


def kernel(**inputs):
    import concourse.bacc as _bacc
    from concourse.bass_utils import run_bass_kernel_spmd as _run

    nc = _bacc.Bacc("TRN2", target_bir_lowering=False, num_devices=1)
    arrays, args = {}, []
    for name in _INS:
        a = np.ascontiguousarray(inputs[name])
        arrays[f"in_{name}"] = a
        args.append(nc.dram_tensor(f"in_{name}", a.shape, mybir.dt.from_np(a.dtype), kind="ExternalInput").ap())
    args.append(nc.dram_tensor("out_0", (N, C), F32, kind="ExternalOutput").ap())
    build(nc, *args)
    r = _run(nc, [arrays], core_ids=[0])
    return r.results[0]["out_0"]
```
